# Optimizing a Trainium2 kernel written in Bass

```python
import numpy as np
import jax
import jax.numpy as jnp

def _softmax(x, axis=-1):
    return jax.nn.softmax(x, axis=axis)

def _gelu(x):
    return jax.nn.gelu(x, approximate=True)

def _silu(x):
    return jax.nn.silu(x)

def _sigmoid(x):
    return jax.nn.sigmoid(x)

def _layernorm(x, axis=-1, eps=1e-05):
    m = jnp.mean(x, axis=axis, keepdims=True)
    v = jnp.var(x, axis=axis, keepdims=True)
    return (x - m) / jnp.sqrt(v + eps)

def _scatter_add(tgt, idx, src, axis=0):
    return tgt.at[idx].add(src)

def _segment_sum(src, seg, n):
    return jax.ops.segment_sum(src, seg, n)
kernel_name = 'mk_pixart_seq_d4_seqx_r4_7d0ddf'

def setup_inputs(seed: int=0):
    np.random.seed(seed)
    _w = jnp.asarray

    def _rec_inputs():
        import jax
        import jax.numpy as jnp
        _rk = jax.random.key(seed)
        x = -0.0002928 + 1 * jax.random.normal(jax.random.fold_in(_rk, 1), (4, 512, 256), jnp.float32)
        _lenS = 512 - jax.random.randint(jax.random.fold_in(_rk, 7), (4,), 0, max(1, 512 // 4) + 1, jnp.int32)
        _lenS2 = 64 - jax.random.randint(jax.random.fold_in(_rk, 8), (4,), 0, max(1, 64 // 4) + 1, jnp.int32)
        _ctx_768P = jax.random.normal(jax.random.fold_in(_rk, 11), (4, 16, 192), jnp.float32)
        _ctx_768c = jax.random.dirichlet(jax.random.fold_in(_rk, 511), 0.3 * jnp.ones((16,), jnp.float32), (4, 64))
        _ctx_768t = jnp.einsum('bsk,bkd->bsd', _ctx_768c, _ctx_768P)
        _ctx_768t = _ctx_768t * jax.lax.rsqrt(jnp.mean(jnp.square(_ctx_768t)) + 1e-12) * 0.953939
        ctx_768 = 0.00095986 + 0.999812 * (_ctx_768t + 0.3 * jax.random.normal(jax.random.fold_in(_rk, 611), (4, 64, 192), jnp.float32))
        cond_1024 = 0.0132156 + 1.00766 * jax.random.normal(jax.random.fold_in(_rk, 12), (4, 256), jnp.float32)
        return (x, ctx_768, cond_1024)
    x, ctx_768, cond_1024 = _rec_inputs()

    def _L0_xcond_setup():
        import jax, jax.numpy as jnp
        import numpy as np
        D = 256
        CD = 192
        H = 16
        HD = D // H
        EPS = 1e-05

        def _ln(x, w, b):
            m = jnp.mean(x, axis=-1, keepdims=True)
            v = jnp.var(x, axis=-1, keepdims=True)
            return (x - m) * jax.lax.rsqrt(v + EPS) * w + b

        def _attn(q, k, v):
            q = q.reshape(q.shape[0], q.shape[1], H, HD).transpose(0, 2, 1, 3)
            k = k.reshape(k.shape[0], k.shape[1], H, HD).transpose(0, 2, 1, 3)
            v = v.reshape(v.shape[0], v.shape[1], H, HD).transpose(0, 2, 1, 3)
            scores = jnp.einsum('bhnd,bhmd->bhnm', q, k) * HD ** (-0.5)
            p = jax.nn.softmax(scores, axis=-1)
            o = jnp.einsum('bhnm,bhmd->bhnd', p, v)
            return o.transpose(0, 2, 1, 3).reshape(o.shape[0], o.shape[2], D)
        key = jax.random.key(seed)
        ks = iter(jax.random.split(key, 32))
        s = 0.02
        inp = {'x': jax.random.normal(next(ks), (4, 256, D), jnp.float32), 'context': jax.random.normal(next(ks), (4, 64, CD), jnp.float32), 'time_emb': jax.random.normal(next(ks), (4, D), jnp.float32), 'ln1_w': jnp.ones((D,)), 'ln1_b': jnp.zeros((D,)), 'ln2_w': jnp.ones((D,)), 'ln2_b': jnp.zeros((D,)), 'ln3_w': jnp.ones((D,)), 'ln3_b': jnp.zeros((D,)), 'Wqkv': jax.random.normal(next(ks), (D, 3 * D)) * s, 'bqkv': jnp.zeros((3 * D,)), 'Wos': jax.random.normal(next(ks), (D, D)) * s, 'bos': jnp.zeros((D,)), 'Wq': jax.random.normal(next(ks), (D, D)) * s, 'bq': jnp.zeros((D,)), 'Wk': jax.random.normal(next(ks), (CD, D)) * s, 'bk': jnp.zeros((D,)), 'Wv': jax.random.normal(next(ks), (CD, D)) * s, 'bv': jnp.zeros((D,)), 'Woc': jax.random.normal(next(ks), (D, D)) * s, 'boc': jnp.zeros((D,)), 'W1': jax.random.normal(next(ks), (D, 4 * D)) * s, 'b1': jnp.zeros((4 * D,)), 'W2': jax.random.normal(next(ks), (4 * D, D)) * s, 'b2': jnp.zeros((D,)), 'Wmod': jax.random.normal(next(ks), (D, 6 * D)) * s, 'bmod': jnp.zeros((6 * D,))}
        return inp
    _L0_xcond_all = _L0_xcond_setup()
    _L0_xcond_in = {k: v for k, v in _L0_xcond_all.items() if k in ('ln1_w', 'ln1_b', 'ln2_w', 'ln2_b', 'ln3_w', 'ln3_b', 'Wqkv', 'bqkv', 'Wos', 'bos', 'Wq', 'bq', 'Wk', 'bk', 'Wv', 'bv', 'Woc', 'boc', 'W1', 'b1', 'W2', 'b2', 'Wmod', 'bmod')}
    del _L0_xcond_all

    def _L1_xcond_setup():
        import jax, jax.numpy as jnp
        import numpy as np
        B, N, M = (2, 256, 128)
        D, H, DH = (256, 16, 64)
        MID = H * DH
        DC = 192
        MULT = 4
        EPS = 1e-05

        def _ln(x, w, b):
            mu = jnp.mean(x, -1, keepdims=True)
            var = jnp.mean((x - mu) ** 2, -1, keepdims=True)
            return (x - mu) * jax.lax.rsqrt(var + EPS) * w + b

        def _sincos(n, d):
            inv = 1.0 / 10000.0 ** (jnp.arange(0, d, 2, dtype=jnp.float32) / d)
            ang = jnp.arange(n, dtype=jnp.float32)[:, None] * inv[None, :]
            return (jnp.sin(ang), jnp.cos(ang))

        def _rope(x, sin, cos):
            s = sin[None, None]
            c = cos[None, None]
            xe = x[..., ::2]
            xo = x[..., 1::2]
            re = xe * c - xo * s
            ro = xe * s + xo * c
            return jnp.stack((re, ro), axis=-1).reshape(x.shape)

        def _heads(t):
            b, n, _ = t.shape
            return t.reshape(b, n, H, DH).transpose(0, 2, 1, 3)

        def _attn(xq, ctx, wq, wkv, wo, bo):
            q = _heads(xq @ wq)
            k, v = jnp.split(ctx @ wkv, 2, axis=-1)
            k = _heads(k)
            v = _heads(v)
            sq, cq = _sincos(q.shape[2], DH)
            sk, ck = _sincos(k.shape[2], DH)
            q = _rope(q, sq, cq)
            k = _rope(k, sk, ck)
            sim = jnp.einsum('bhnd,bhmd->bhnm', q, k) * DH ** (-0.5)
            a = jax.nn.softmax(sim, axis=-1)
            o = jnp.einsum('bhnm,bhmd->bhnd', a, v)
            o = o.transpose(0, 2, 1, 3).reshape(xq.shape[0], xq.shape[1], MID)
            return o @ wo + bo

        def _adaln(x, c, lw, lb, gw, gb, bw, bb):
            g = (c @ gw + gb)[:, None, :]
            bt = (c @ bw + bb)[:, None, :]
            return _ln(x, lw, lb) * (1.0 + g) + bt
        ks = jax.random.split(jax.random.key(seed), 24)
        s = 0.02
        inp = {'x': jax.random.normal(ks[0], (B, N, D), jnp.float32), 'cond': jax.random.normal(ks[1], (B, D), jnp.float32), 'context': jax.random.normal(ks[2], (B, M, DC), jnp.float32), 'ln1_w': jnp.ones((D,), jnp.float32), 'ln1_b': jnp.zeros((D,), jnp.float32), 'g1_w': jax.random.normal(ks[3], (D, D), jnp.float32) * s, 'g1_b': jnp.zeros((D,), jnp.float32), 'b1_w': jax.random.normal(ks[4], (D, D), jnp.float32) * s, 'b1_b': jnp.zeros((D,), jnp.float32), 'ln2_w': jnp.ones((D,), jnp.float32), 'ln2_b': jnp.zeros((D,), jnp.float32), 'g2_w': jax.random.normal(ks[5], (D, D), jnp.float32) * s, 'g2_b': jnp.zeros((D,), jnp.float32), 'b2_w': jax.random.normal(ks[6], (D, D), jnp.float32) * s, 'b2_b': jnp.zeros((D,), jnp.float32), 'sa_wq': jax.random.normal(ks[7], (D, MID), jnp.float32) * s, 'sa_wkv': jax.random.normal(ks[8], (D, 2 * MID), jnp.float32) * s, 'sa_wo': jax.random.normal(ks[9], (MID, D), jnp.float32) * s, 'sa_bo': jnp.zeros((D,), jnp.float32), 'ca_lnc_w': jnp.ones((DC,), jnp.float32), 'ca_lnc_b': jnp.zeros((DC,), jnp.float32), 'ca_wq': jax.random.normal(ks[10], (D, MID), jnp.float32) * s, 'ca_wkv': jax.random.normal(ks[11], (DC, 2 * MID), jnp.float32) * s, 'ca_wo': jax.random.normal(ks[12], (MID, D), jnp.float32) * s, 'ca_bo': jnp.zeros((D,), jnp.float32), 'ff_w1': jax.random.normal(ks[13], (D, MULT * D), jnp.float32) * s, 'ff_b1': jnp.zeros((MULT * D,), jnp.float32), 'ff_w2': jax.random.normal(ks[14], (MULT * D, D), jnp.float32) * s, 'ff_b2': jnp.zeros((D,), jnp.float32)}
        return inp
    _L1_xcond_all = _L1_xcond_setup()
    _L1_xcond_in = {k: v for k, v in _L1_xcond_all.items() if k in ('ln1_w', 'ln1_b', 'g1_w', 'g1_b', 'b1_w', 'b1_b', 'ln2_w', 'ln2_b', 'g2_w', 'g2_b', 'b2_w', 'b2_b', 'sa_wq', 'sa_wkv', 'sa_wo', 'sa_bo', 'ca_lnc_w', 'ca_lnc_b', 'ca_wq', 'ca_wkv', 'ca_wo', 'ca_bo', 'ff_w1', 'ff_b1', 'ff_w2', 'ff_b2')}
    del _L1_xcond_all

    def _L2_xcond_setup():
        import jax, jax.numpy as jnp
        import numpy as np
        B, N, D, H, TD, TL = (4, 256, 256, 16, 192, 77)
        HD = D // H
        EPS = 1e-06

        def _ln(x):
            mu = jnp.mean(x, axis=-1, keepdims=True)
            var = jnp.var(x, axis=-1, keepdims=True)
            return (x - mu) * jax.lax.rsqrt(var + EPS)

        def _modulate(x, shift, scale):
            return x * (1.0 + scale[:, None, :]) + shift[:, None, :]

        def _heads(t):
            return t.reshape(t.shape[0], t.shape[1], H, HD).transpose(0, 2, 1, 3)

        def _attend(q, k, v):
            sim = jnp.einsum('bhid,bhjd->bhij', q, k) * HD ** (-0.5)
            attn = jax.nn.softmax(sim, axis=-1)
            out = jnp.einsum('bhij,bhjd->bhid', attn, v)
            return out.transpose(0, 2, 1, 3).reshape(out.shape[0], -1, D)
        key = jax.random.key(seed)
        ks = jax.random.split(key, 16)
        s = 0.02
        return {'x': jax.random.normal(ks[0], (B, N, D), jnp.float32), 'c': jax.random.normal(ks[1], (B, D), jnp.float32), 'text_embed': jax.random.normal(ks[2], (B, TL, TD), jnp.float32), 'W_ada': jax.random.normal(ks[3], (D, 6 * D), jnp.float32) * s, 'b_ada': jnp.zeros((6 * D,), jnp.float32), 'W_qkv': jax.random.normal(ks[4], (D, 3 * D), jnp.float32) * s, 'b_qkv': jnp.zeros((3 * D,), jnp.float32), 'W_proj': jax.random.normal(ks[5], (D, D), jnp.float32) * s, 'b_proj': jnp.zeros((D,), jnp.float32), 'W_ctx': jax.random.normal(ks[6], (TD, D), jnp.float32) * s, 'b_ctx': jnp.zeros((D,), jnp.float32), 'W_q': jax.random.normal(ks[7], (D, D), jnp.float32) * s, 'W_k': jax.random.normal(ks[8], (D, D), jnp.float32) * s, 'W_v': jax.random.normal(ks[9], (D, D), jnp.float32) * s, 'W_out': jax.random.normal(ks[10], (D, D), jnp.float32) * s, 'b_out': jnp.zeros((D,), jnp.float32), 'W_fc1': jax.random.normal(ks[11], (D, 4 * D), jnp.float32) * s, 'b_fc1': jnp.zeros((4 * D,), jnp.float32), 'W_fc2': jax.random.normal(ks[12], (4 * D, D), jnp.float32) * s, 'b_fc2': jnp.zeros((D,), jnp.float32)}
    _L2_xcond_all = _L2_xcond_setup()
    _L2_xcond_in = {k: v for k, v in _L2_xcond_all.items() if k in ('W_ada', 'b_ada', 'W_qkv', 'b_qkv', 'W_proj', 'b_proj', 'W_ctx', 'b_ctx', 'W_q', 'W_k', 'W_v', 'W_out', 'b_out', 'W_fc1', 'b_fc1', 'W_fc2', 'b_fc2')}
    del _L2_xcond_all

    def _L3_xcond_setup():
        import jax, jax.numpy as jnp
        import numpy as np
        EPS = 1e-06

        def ln(x, eps=EPS):
            m = jnp.mean(x, axis=-1, keepdims=True)
            v = jnp.mean(jnp.square(x - m), axis=-1, keepdims=True)
            return (x - m) * jax.lax.rsqrt(v + eps)

        def modulate(x, shift, scale):
            return x * (1.0 + scale[:, None, :]) + shift[:, None, :]

        def _heads(t, H):
            B, N, D = t.shape
            return t.reshape(B, N, H, D // H).transpose(0, 2, 1, 3)

        def _unheads(t):
            B, H, N, hd = t.shape
            return t.transpose(0, 2, 1, 3).reshape(B, N, H * hd)
        key = jax.random.key(seed)
        B, N, D, H, T, CD = (4, 256, 256, 16, 64, 192)
        FF = 4 * D
        ks = jax.random.split(key, 20)
        s = 0.02
        return {'x': jax.random.normal(ks[0], (B, N, D), jnp.float32), 'c': jax.random.normal(ks[1], (B, D), jnp.float32), 'brain_tokens': jax.random.normal(ks[2], (B, T, CD), jnp.float32), 'adaln_w': jax.random.normal(ks[3], (9 * D, D), jnp.float32) * s, 'adaln_b': jax.random.normal(ks[4], (9 * D,), jnp.float32) * s, 'qn_w': jnp.ones((D // H,), jnp.float32), 'qn_b': jnp.zeros((D // H,), jnp.float32), 'kn_w': jnp.ones((D // H,), jnp.float32), 'kn_b': jnp.zeros((D // H,), jnp.float32), 'ca_in_w': jax.random.normal(ks[5], (3 * D, D), jnp.float32) * s, 'ca_in_b': jax.random.normal(ks[6], (3 * D,), jnp.float32) * s, 'ca_out_w': jax.random.normal(ks[7], (D, D), jnp.float32) * s, 'ca_out_b': jax.random.normal(ks[8], (D,), jnp.float32) * s, 'cond_w': jax.random.normal(ks[9], (D, CD), jnp.float32) * s, 'cond_b': jax.random.normal(ks[10], (D,), jnp.float32) * s, 'w1': jax.random.normal(ks[11], (FF, D), jnp.float32) * s, 'w3': jax.random.normal(ks[12], (FF, D), jnp.float32) * s, 'w2': jax.random.normal(ks[13], (D, FF), jnp.float32) * s}
    _L3_xcond_all = _L3_xcond_setup()
    _L3_xcond_in = {k: v for k, v in _L3_xcond_all.items() if k in ('adaln_w', 'adaln_b', 'qn_w', 'qn_b', 'kn_w', 'kn_b', 'ca_in_w', 'ca_in_b', 'ca_out_w', 'ca_out_b', 'cond_w', 'cond_b', 'w1', 'w3', 'w2')}
    del _L3_xcond_all
    return {'x': x, 'ctx_768': ctx_768, 'cond_1024': cond_1024, 'L0_xcond_ln1_w': _L0_xcond_in['ln1_w'], 'L0_xcond_ln1_b': _L0_xcond_in['ln1_b'], 'L0_xcond_ln2_w': _L0_xcond_in['ln2_w'], 'L0_xcond_ln2_b': _L0_xcond_in['ln2_b'], 'L0_xcond_ln3_w': _L0_xcond_in['ln3_w'], 'L0_xcond_ln3_b': _L0_xcond_in['ln3_b'], 'L0_xcond_Wqkv': _L0_xcond_in['Wqkv'], 'L0_xcond_bqkv': _L0_xcond_in['bqkv'], 'L0_xcond_Wos': _L0_xcond_in['Wos'], 'L0_xcond_bos': _L0_xcond_in['bos'], 'L0_xcond_Wq': _L0_xcond_in['Wq'], 'L0_xcond_bq': _L0_xcond_in['bq'], 'L0_xcond_Wk': _L0_xcond_in['Wk'], 'L0_xcond_bk': _L0_xcond_in['bk'], 'L0_xcond_Wv': _L0_xcond_in['Wv'], 'L0_xcond_bv': _L0_xcond_in['bv'], 'L0_xcond_Woc': _L0_xcond_in['Woc'], 'L0_xcond_boc': _L0_xcond_in['boc'], 'L0_xcond_W1': _L0_xcond_in['W1'], 'L0_xcond_b1': _L0_xcond_in['b1'], 'L0_xcond_W2': _L0_xcond_in['W2'], 'L0_xcond_b2': _L0_xcond_in['b2'], 'L0_xcond_Wmod': _L0_xcond_in['Wmod'], 'L0_xcond_bmod': _L0_xcond_in['bmod'], 'L1_xcond_ln1_w': _L1_xcond_in['ln1_w'], 'L1_xcond_ln1_b': _L1_xcond_in['ln1_b'], 'L1_xcond_g1_w': _L1_xcond_in['g1_w'], 'L1_xcond_g1_b': _L1_xcond_in['g1_b'], 'L1_xcond_b1_w': _L1_xcond_in['b1_w'], 'L1_xcond_b1_b': _L1_xcond_in['b1_b'], 'L1_xcond_ln2_w': _L1_xcond_in['ln2_w'], 'L1_xcond_ln2_b': _L1_xcond_in['ln2_b'], 'L1_xcond_g2_w': _L1_xcond_in['g2_w'], 'L1_xcond_g2_b': _L1_xcond_in['g2_b'], 'L1_xcond_b2_w': _L1_xcond_in['b2_w'], 'L1_xcond_b2_b': _L1_xcond_in['b2_b'], 'L1_xcond_sa_wq': _L1_xcond_in['sa_wq'], 'L1_xcond_sa_wkv': _L1_xcond_in['sa_wkv'], 'L1_xcond_sa_wo': _L1_xcond_in['sa_wo'], 'L1_xcond_sa_bo': _L1_xcond_in['sa_bo'], 'L1_xcond_ca_lnc_w': _L1_xcond_in['ca_lnc_w'], 'L1_xcond_ca_lnc_b': _L1_xcond_in['ca_lnc_b'], 'L1_xcond_ca_wq': _L1_xcond_in['ca_wq'], 'L1_xcond_ca_wkv': _L1_xcond_in['ca_wkv'], 'L1_xcond_ca_wo': _L1_xcond_in['ca_wo'], 'L1_xcond_ca_bo': _L1_xcond_in['ca_bo'], 'L1_xcond_ff_w1': _L1_xcond_in['ff_w1'], 'L1_xcond_ff_b1': _L1_xcond_in['ff_b1'], 'L1_xcond_ff_w2': _L1_xcond_in['ff_w2'], 'L1_xcond_ff_b2': _L1_xcond_in['ff_b2'], 'L2_xcond_W_ada': _L2_xcond_in['W_ada'], 'L2_xcond_b_ada': _L2_xcond_in['b_ada'], 'L2_xcond_W_qkv': _L2_xcond_in['W_qkv'], 'L2_xcond_b_qkv': _L2_xcond_in['b_qkv'], 'L2_xcond_W_proj': _L2_xcond_in['W_proj'], 'L2_xcond_b_proj': _L2_xcond_in['b_proj'], 'L2_xcond_W_ctx': _L2_xcond_in['W_ctx'], 'L2_xcond_b_ctx': _L2_xcond_in['b_ctx'], 'L2_xcond_W_q': _L2_xcond_in['W_q'], 'L2_xcond_W_k': _L2_xcond_in['W_k'], 'L2_xcond_W_v': _L2_xcond_in['W_v'], 'L2_xcond_W_out': _L2_xcond_in['W_out'], 'L2_xcond_b_out': _L2_xcond_in['b_out'], 'L2_xcond_W_fc1': _L2_xcond_in['W_fc1'], 'L2_xcond_b_fc1': _L2_xcond_in['b_fc1'], 'L2_xcond_W_fc2': _L2_xcond_in['W_fc2'], 'L2_xcond_b_fc2': _L2_xcond_in['b_fc2'], 'L3_xcond_adaln_w': _L3_xcond_in['adaln_w'], 'L3_xcond_adaln_b': _L3_xcond_in['adaln_b'], 'L3_xcond_qn_w': _L3_xcond_in['qn_w'], 'L3_xcond_qn_b': _L3_xcond_in['qn_b'], 'L3_xcond_kn_w': _L3_xcond_in['kn_w'], 'L3_xcond_kn_b': _L3_xcond_in['kn_b'], 'L3_xcond_ca_in_w': _L3_xcond_in['ca_in_w'], 'L3_xcond_ca_in_b': _L3_xcond_in['ca_in_b'], 'L3_xcond_ca_out_w': _L3_xcond_in['ca_out_w'], 'L3_xcond_ca_out_b': _L3_xcond_in['ca_out_b'], 'L3_xcond_cond_w': _L3_xcond_in['cond_w'], 'L3_xcond_cond_b': _L3_xcond_in['cond_b'], 'L3_xcond_w1': _L3_xcond_in['w1'], 'L3_xcond_w3': _L3_xcond_in['w3'], 'L3_xcond_w2': _L3_xcond_in['w2']}

def reference(x, ctx_768, cond_1024, L0_xcond_ln1_w, L0_xcond_ln1_b, L0_xcond_ln2_w, L0_xcond_ln2_b, L0_xcond_ln3_w, L0_xcond_ln3_b, L0_xcond_Wqkv, L0_xcond_bqkv, L0_xcond_Wos, L0_xcond_bos, L0_xcond_Wq, L0_xcond_bq, L0_xcond_Wk, L0_xcond_bk, L0_xcond_Wv, L0_xcond_bv, L0_xcond_Woc, L0_xcond_boc, L0_xcond_W1, L0_xcond_b1, L0_xcond_W2, L0_xcond_b2, L0_xcond_Wmod, L0_xcond_bmod, L1_xcond_ln1_w, L1_xcond_ln1_b, L1_xcond_g1_w, L1_xcond_g1_b, L1_xcond_b1_w, L1_xcond_b1_b, L1_xcond_ln2_w, L1_xcond_ln2_b, L1_xcond_g2_w, L1_xcond_g2_b, L1_xcond_b2_w, L1_xcond_b2_b, L1_xcond_sa_wq, L1_xcond_sa_wkv, L1_xcond_sa_wo, L1_xcond_sa_bo, L1_xcond_ca_lnc_w, L1_xcond_ca_lnc_b, L1_xcond_ca_wq, L1_xcond_ca_wkv, L1_xcond_ca_wo, L1_xcond_ca_bo, L1_xcond_ff_w1, L1_xcond_ff_b1, L1_xcond_ff_w2, L1_xcond_ff_b2, L2_xcond_W_ada, L2_xcond_b_ada, L2_xcond_W_qkv, L2_xcond_b_qkv, L2_xcond_W_proj, L2_xcond_b_proj, L2_xcond_W_ctx, L2_xcond_b_ctx, L2_xcond_W_q, L2_xcond_W_k, L2_xcond_W_v, L2_xcond_W_out, L2_xcond_b_out, L2_xcond_W_fc1, L2_xcond_b_fc1, L2_xcond_W_fc2, L2_xcond_b_fc2, L3_xcond_adaln_w, L3_xcond_adaln_b, L3_xcond_qn_w, L3_xcond_qn_b, L3_xcond_kn_w, L3_xcond_kn_b, L3_xcond_ca_in_w, L3_xcond_ca_in_b, L3_xcond_ca_out_w, L3_xcond_ca_out_b, L3_xcond_cond_w, L3_xcond_cond_b, L3_xcond_w1, L3_xcond_w3, L3_xcond_w2):
    import jax
    import jax.numpy as jnp

    def _L0_xcond_ref(x, context, time_emb, ln1_w, ln1_b, ln2_w, ln2_b, ln3_w, ln3_b, Wqkv, bqkv, Wos, bos, Wq, bq, Wk, bk, Wv, bv, Woc, boc, W1, b1, W2, b2, Wmod, bmod):
        import jax, jax.numpy as jnp
        import numpy as np
        D = 256
        CD = 192
        H = 16
        HD = D // H
        EPS = 1e-05

        def _ln(x, w, b):
            m = jnp.mean(x, axis=-1, keepdims=True)
            v = jnp.var(x, axis=-1, keepdims=True)
            return (x - m) * jax.lax.rsqrt(v + EPS) * w + b

        def _attn(q, k, v):
            q = q.reshape(q.shape[0], q.shape[1], H, HD).transpose(0, 2, 1, 3)
            k = k.reshape(k.shape[0], k.shape[1], H, HD).transpose(0, 2, 1, 3)
            v = v.reshape(v.shape[0], v.shape[1], H, HD).transpose(0, 2, 1, 3)
            scores = jnp.einsum('bhnd,bhmd->bhnm', q, k) * HD ** (-0.5)
            p = jax.nn.softmax(scores, axis=-1)
            o = jnp.einsum('bhnm,bhmd->bhnd', p, v)
            return o.transpose(0, 2, 1, 3).reshape(o.shape[0], o.shape[2], D)
        mod = jax.nn.silu(time_emb) @ Wmod + bmod
        sh1, sc1, sh2, sc2, sh3, sc3 = jnp.split(mod, 6, axis=-1)
        h = _ln(x, ln1_w, ln1_b) * (1 + sc1[:, None, :]) + sh1[:, None, :]
        qkv = h @ Wqkv + bqkv
        q, k, v = jnp.split(qkv, 3, axis=-1)
        x = x + _attn(q, k, v) @ Wos + bos
        h = _ln(x, ln2_w, ln2_b) * (1 + sc2[:, None, :]) + sh2[:, None, :]
        x = x + _attn(h @ Wq + bq, context @ Wk + bk, context @ Wv + bv) @ Woc + boc
        h = _ln(x, ln3_w, ln3_b) * (1 + sc3[:, None, :]) + sh3[:, None, :]
        x = x + jax.nn.gelu(h @ W1 + b1, approximate=False) @ W2 + b2
        return x

    def _L1_xcond_ref(x, cond, context, ln1_w, ln1_b, g1_w, g1_b, b1_w, b1_b, ln2_w, ln2_b, g2_w, g2_b, b2_w, b2_b, sa_wq, sa_wkv, sa_wo, sa_bo, ca_lnc_w, ca_lnc_b, ca_wq, ca_wkv, ca_wo, ca_bo, ff_w1, ff_b1, ff_w2, ff_b2):
        import jax, jax.numpy as jnp
        import numpy as np
        B, N, M = (2, 256, 128)
        D, H, DH = (256, 16, 64)
        MID = H * DH
        DC = 192
        MULT = 4
        EPS = 1e-05

        def _ln(x, w, b):
            mu = jnp.mean(x, -1, keepdims=True)
            var = jnp.mean((x - mu) ** 2, -1, keepdims=True)
            return (x - mu) * jax.lax.rsqrt(var + EPS) * w + b

        def _sincos(n, d):
            inv = 1.0 / 10000.0 ** (jnp.arange(0, d, 2, dtype=jnp.float32) / d)
            ang = jnp.arange(n, dtype=jnp.float32)[:, None] * inv[None, :]
            return (jnp.sin(ang), jnp.cos(ang))

        def _rope(x, sin, cos):
            s = sin[None, None]
            c = cos[None, None]
            xe = x[..., ::2]
            xo = x[..., 1::2]
            re = xe * c - xo * s
            ro = xe * s + xo * c
            return jnp.stack((re, ro), axis=-1).reshape(x.shape)

        def _heads(t):
            b, n, _ = t.shape
            return t.reshape(b, n, H, DH).transpose(0, 2, 1, 3)

        def _attn(xq, ctx, wq, wkv, wo, bo):
            q = _heads(xq @ wq)
            k, v = jnp.split(ctx @ wkv, 2, axis=-1)
            k = _heads(k)
            v = _heads(v)
            sq, cq = _sincos(q.shape[2], DH)
            sk, ck = _sincos(k.shape[2], DH)
            q = _rope(q, sq, cq)
            k = _rope(k, sk, ck)
            sim = jnp.einsum('bhnd,bhmd->bhnm', q, k) * DH ** (-0.5)
            a = jax.nn.softmax(sim, axis=-1)
            o = jnp.einsum('bhnm,bhmd->bhnd', a, v)
            o = o.transpose(0, 2, 1, 3).reshape(xq.shape[0], xq.shape[1], MID)
            return o @ wo + bo

        def _adaln(x, c, lw, lb, gw, gb, bw, bb):
            g = (c @ gw + gb)[:, None, :]
            bt = (c @ bw + bb)[:, None, :]
            return _ln(x, lw, lb) * (1.0 + g) + bt
        attn_in = _adaln(x, cond, ln1_w, ln1_b, g1_w, g1_b, b1_w, b1_b)
        x = _attn(attn_in, attn_in, sa_wq, sa_wkv, sa_wo, sa_bo) + x
        cross_in = _adaln(x, cond, ln1_w, ln1_b, g1_w, g1_b, b1_w, b1_b)
        ctx_n = _ln(context, ca_lnc_w, ca_lnc_b)
        x = _attn(cross_in, ctx_n, ca_wq, ca_wkv, ca_wo, ca_bo) + x
        ffn_in = _adaln(x, cond, ln2_w, ln2_b, g2_w, g2_b, b2_w, b2_b)
        h = jax.nn.gelu(ffn_in @ ff_w1 + ff_b1, approximate=False)
        x = h @ ff_w2 + ff_b2 + x
        return x

    def _L2_xcond_ref(x, c, text_embed, W_ada, b_ada, W_qkv, b_qkv, W_proj, b_proj, W_ctx, b_ctx, W_q, W_k, W_v, W_out, b_out, W_fc1, b_fc1, W_fc2, b_fc2):
        import jax, jax.numpy as jnp
        import numpy as np
        B, N, D, H, TD, TL = (4, 256, 256, 16, 192, 77)
        HD = D // H
        EPS = 1e-06

        def _ln(x):
            mu = jnp.mean(x, axis=-1, keepdims=True)
            var = jnp.var(x, axis=-1, keepdims=True)
            return (x - mu) * jax.lax.rsqrt(var + EPS)

        def _modulate(x, shift, scale):
            return x * (1.0 + scale[:, None, :]) + shift[:, None, :]

        def _heads(t):
            return t.reshape(t.shape[0], t.shape[1], H, HD).transpose(0, 2, 1, 3)

        def _attend(q, k, v):
            sim = jnp.einsum('bhid,bhjd->bhij', q, k) * HD ** (-0.5)
            attn = jax.nn.softmax(sim, axis=-1)
            out = jnp.einsum('bhij,bhjd->bhid', attn, v)
            return out.transpose(0, 2, 1, 3).reshape(out.shape[0], -1, D)
        mod = jax.nn.silu(c) @ W_ada + b_ada
        sh_msa, sc_msa, sh_x, sc_x, sh_mlp, sc_mlp = jnp.split(mod, 6, axis=-1)
        h1 = _modulate(_ln(x), sh_msa, sc_msa)
        qkv = h1 @ W_qkv + b_qkv
        q, k, v = jnp.split(qkv, 3, axis=-1)
        out = _attend(_heads(q), _heads(k), _heads(v))
        x = x + (out @ W_proj + b_proj)
        h2 = _modulate(_ln(x), sh_x, sc_x)
        ctx = text_embed @ W_ctx + b_ctx
        q = _heads(h2 @ W_q)
        k = _heads(ctx @ W_k)
        v = _heads(ctx @ W_v)
        out = _attend(q, k, v)
        x = x + (out @ W_out + b_out)
        h3 = _modulate(_ln(x), sh_mlp, sc_mlp)
        hidden = jax.nn.gelu(h3 @ W_fc1 + b_fc1, approximate=True)
        x = x + (hidden @ W_fc2 + b_fc2)
        return x

    def _L3_xcond_ref(x, c, brain_tokens, adaln_w, adaln_b, qn_w, qn_b, kn_w, kn_b, ca_in_w, ca_in_b, ca_out_w, ca_out_b, cond_w, cond_b, w1, w3, w2):
        import jax, jax.numpy as jnp
        import numpy as np
        EPS = 1e-06

        def ln(x, eps=EPS):
            m = jnp.mean(x, axis=-1, keepdims=True)
            v = jnp.mean(jnp.square(x - m), axis=-1, keepdims=True)
            return (x - m) * jax.lax.rsqrt(v + eps)

        def modulate(x, shift, scale):
            return x * (1.0 + scale[:, None, :]) + shift[:, None, :]

        def _heads(t, H):
            B, N, D = t.shape
            return t.reshape(B, N, H, D // H).transpose(0, 2, 1, 3)

        def _unheads(t):
            B, H, N, hd = t.shape
            return t.transpose(0, 2, 1, 3).reshape(B, N, H * hd)
        B, N, D = x.shape
        H = 16
        hd = D // H
        scale = hd ** (-0.5)
        mod = jax.nn.silu(c) @ adaln_w.T + adaln_b
        shift_sa, scale_sa, gate_sa, shift_ca, scale_ca, gate_ca, shift_ff, scale_ff, gate_ff = jnp.split(mod, 9, axis=-1)
        h = modulate(ln(x), shift_sa, scale_sa)
        q = ln(_heads(h, H)) * qn_w + qn_b
        k = ln(_heads(h, H)) * kn_w + kn_b
        v = _heads(h, H)
        attn = jax.nn.softmax(jnp.einsum('bhqd,bhkd->bhqk', q, k) * scale, axis=-1)
        h = _unheads(jnp.einsum('bhqk,bhkd->bhqd', attn, v))
        x = x + gate_sa[:, None, :] * h
        h = modulate(ln(x), shift_ca, scale_ca)
        kv = brain_tokens @ cond_w.T + cond_b
        wq, wk, wv = jnp.split(ca_in_w, 3, axis=0)
        bq, bk, bv = jnp.split(ca_in_b, 3, axis=0)
        q = _heads(h @ wq.T + bq, H)
        k = _heads(kv @ wk.T + bk, H)
        v = _heads(kv @ wv.T + bv, H)
        attn = jax.nn.softmax(jnp.einsum('bhqd,bhkd->bhqk', q, k) * scale, axis=-1)
        h = _unheads(jnp.einsum('bhqk,bhkd->bhqd', attn, v)) @ ca_out_w.T + ca_out_b
        x = x + gate_ca[:, None, :] * h
        h = modulate(ln(x), shift_ff, scale_ff)
        h = jax.nn.silu(h @ w1.T) * (h @ w3.T) @ w2.T
        x = x + gate_ff[:, None, :] * h
        return x
    x = _L0_xcond_ref(x, ctx_768, cond_1024, L0_xcond_ln1_w, L0_xcond_ln1_b, L0_xcond_ln2_w, L0_xcond_ln2_b, L0_xcond_ln3_w, L0_xcond_ln3_b, L0_xcond_Wqkv, L0_xcond_bqkv, L0_xcond_Wos, L0_xcond_bos, L0_xcond_Wq, L0_xcond_bq, L0_xcond_Wk, L0_xcond_bk, L0_xcond_Wv, L0_xcond_bv, L0_xcond_Woc, L0_xcond_boc, L0_xcond_W1, L0_xcond_b1, L0_xcond_W2, L0_xcond_b2, L0_xcond_Wmod, L0_xcond_bmod)
    x = _L1_xcond_ref(x, cond_1024, ctx_768, L1_xcond_ln1_w, L1_xcond_ln1_b, L1_xcond_g1_w, L1_xcond_g1_b, L1_xcond_b1_w, L1_xcond_b1_b, L1_xcond_ln2_w, L1_xcond_ln2_b, L1_xcond_g2_w, L1_xcond_g2_b, L1_xcond_b2_w, L1_xcond_b2_b, L1_xcond_sa_wq, L1_xcond_sa_wkv, L1_xcond_sa_wo, L1_xcond_sa_bo, L1_xcond_ca_lnc_w, L1_xcond_ca_lnc_b, L1_xcond_ca_wq, L1_xcond_ca_wkv, L1_xcond_ca_wo, L1_xcond_ca_bo, L1_xcond_ff_w1, L1_xcond_ff_b1, L1_xcond_ff_w2, L1_xcond_ff_b2)
    x = _L2_xcond_ref(x, cond_1024, ctx_768, L2_xcond_W_ada, L2_xcond_b_ada, L2_xcond_W_qkv, L2_xcond_b_qkv, L2_xcond_W_proj, L2_xcond_b_proj, L2_xcond_W_ctx, L2_xcond_b_ctx, L2_xcond_W_q, L2_xcond_W_k, L2_xcond_W_v, L2_xcond_W_out, L2_xcond_b_out, L2_xcond_W_fc1, L2_xcond_b_fc1, L2_xcond_W_fc2, L2_xcond_b_fc2)
    x = _L3_xcond_ref(x, cond_1024, ctx_768, L3_xcond_adaln_w, L3_xcond_adaln_b, L3_xcond_qn_w, L3_xcond_qn_b, L3_xcond_kn_w, L3_xcond_kn_b, L3_xcond_ca_in_w, L3_xcond_ca_in_b, L3_xcond_ca_out_w, L3_xcond_ca_out_b, L3_xcond_cond_w, L3_xcond_cond_b, L3_xcond_w1, L3_xcond_w3, L3_xcond_w2)
    return x

_drawn_inputs = setup_inputs


def setup_inputs(seed=0):
    import zlib

    import numpy as np

    out = dict(_drawn_inputs(seed))
    spreads = {'L0_xcond_ln1_w': (1.0, 0.6),
     'L0_xcond_ln1_b': (0.0, 0.786),
     'L0_xcond_ln2_w': (1.0, 0.6),
     'L0_xcond_ln2_b': (0.0, 0.8),
     'L0_xcond_ln3_w': (1.0, 0.6),
     'L0_xcond_ln3_b': (0.0, 0.669),
     'L0_xcond_bqkv': (0.0, 0.1),
     'L0_xcond_bos': (0.0, 0.1),
     'L0_xcond_bq': (0.0, 0.8),
     'L0_xcond_bk': (0.0, 2.0),
     'L0_xcond_bv': (0.0, 0.1),
     'L0_xcond_boc': (0.0, 0.1),
     'L0_xcond_b1': (0.0, 0.1),
     'L0_xcond_b2': (0.0, 0.1),
     'L0_xcond_bmod': (0.0, 0.415),
     'L1_xcond_ln1_w': (1.0, 0.6),
     'L1_xcond_ln1_b': (0.0, 0.385),
     'L1_xcond_g1_b': (0.0, 0.8),
     'L1_xcond_b1_b': (0.0, 0.426),
     'L1_xcond_ln2_w': (1.0, 0.6),
     'L1_xcond_ln2_b': (0.0, 0.742),
     'L1_xcond_g2_b': (0.0, 0.8),
     'L1_xcond_b2_b': (0.0, 0.743),
     'L1_xcond_sa_bo': (0.0, 0.1),
     'L1_xcond_ca_lnc_w': (1.0, 0.6),
     'L1_xcond_ca_lnc_b': (0.0, 0.48),
     'L1_xcond_ca_bo': (0.0, 0.1),
     'L1_xcond_ff_b1': (0.0, 0.1),
     'L1_xcond_ff_b2': (0.0, 0.1),
     'L2_xcond_b_ada': (0.0, 0.477),
     'L2_xcond_b_qkv': (0.0, 0.1),
     'L2_xcond_b_proj': (0.0, 0.1),
     'L2_xcond_b_ctx': (0.0, 0.8),
     'L2_xcond_b_out': (0.0, 0.1),
     'L2_xcond_b_fc1': (0.0, 0.1),
     'L2_xcond_b_fc2': (0.0, 0.1),
     'L3_xcond_qn_w': (1.0, 0.6),
     'L3_xcond_qn_b': (0.0, 0.8),
     'L3_xcond_kn_w': (1.0, 0.6),
     'L3_xcond_kn_b': (0.0, 2.0)}
    factors = {'L0_xcond_Wq': 8.0,
     'L0_xcond_Wk': 8.0,
     'L1_xcond_g1_w': 3.834,
     'L1_xcond_sa_wq': 8.0,
     'L1_xcond_ca_wq': 8.0,
     'L2_xcond_W_ctx': 3.868,
     'L2_xcond_W_q': 8.0,
     'L2_xcond_W_k': 8.0,
     'L2_xcond_W_v': 3.335,
     'L2_xcond_W_out': 3.415,
     'L3_xcond_adaln_b': 4.798,
     'L3_xcond_ca_in_w': 8.0,
     'L3_xcond_ca_in_b': 8.0,
     'L3_xcond_ca_out_w': 8.0,
     'L3_xcond_ca_out_b': 39.718,
     'L3_xcond_cond_w': 8.0,
     'L3_xcond_cond_b': 8.0,
     'L3_xcond_w1': 8.0,
     'L3_xcond_w3': 8.0,
     'L3_xcond_w2': 8.0}
    for name, (base, spread) in spreads.items():
        noise = np.random.default_rng([zlib.crc32(name.encode()), seed]).standard_normal(out[name].shape)
        drawn = base * np.exp(spread * noise) if base else spread * noise
        out[name] = jnp.asarray(drawn.astype(out[name].dtype))
    for name, factor in factors.items():
        out[name] = (out[name] * factor).astype(out[name].dtype)
    return out
```

```python
from contextlib import ExitStack

import concourse.bass as bass
from concourse import mybir
import numpy as np

F32 = mybir.dt.float32
BF16 = mybir.dt.bfloat16
ACT = mybir.ActivationFunctionType
ALU = mybir.AluOpType
AX = mybir.AxisListType

B, N, D, H = 4, 512, 256, 16
M, DC = 64, 192
T = B * N
P = 128
TILES = T // P
TB = N // P
C = D // P
FF = 4 * D
FC = FF // P
HEADS = B * H
MID = 1024
WIDE = MID // H
NARROW = D // H

VECTORS = (
    [("L0_bmod", 12), ("L1_g1_b", 2), ("L1_b1_b", 2), ("L1_g2_b", 2), ("L1_b2_b", 2), ("L2_b_ada", 12), ("L3_adaln_b", 18)]
    + [(f"L0_ln{i}_{v}", 2) for i in (1, 2, 3) for v in "wb"]
    + [(f"L1_ln{i}_{v}", 2) for i in (1, 2) for v in "wb"]
    + [("L0_bqkv", 6), ("L0_bos", 2), ("L0_bq", 2), ("L0_bk", 2), ("L0_bv", 2), ("L0_boc", 2), ("L0_b1", 8), ("L0_b2", 2)]
    + [("L1_sa_bo", 2), ("L1_ca_lnc_w", 2), ("L1_ca_lnc_b", 2), ("L1_ca_bo", 2), ("L1_ff_b1", 8), ("L1_ff_b2", 2)]
    + [("L2_b_qkv", 6), ("L2_b_proj", 2), ("L2_b_ctx", 2), ("L2_b_out", 2), ("L2_b_fc1", 8), ("L2_b_fc2", 2)]
    + [("L3_qn_w", 1), ("L3_qn_b", 1), ("L3_kn_w", 1), ("L3_kn_b", 1), ("L3_ca_in_b", 6), ("L3_ca_out_b", 2), ("L3_cond_b", 2)]
)
OFFSET = {}
for _name, _n in VECTORS:
    OFFSET[_name] = sum(n for k, n in VECTORS if k in OFFSET)
NVEC = sum(n for _, n in VECTORS)

MODS = [("L0_Wmod", 1536), ("L1_g1_w", 256), ("L1_b1_w", 256), ("L1_g2_w", 256), ("L1_b2_w", 256), ("L2_W_ada", 1536), ("L3_adaln_w", 2304)]
MOD_AT = {"L0": 0, "L1": 12, "L2": 20, "L3": 32}
NMOD = sum(n for _, n in MODS) // P

WEIGHTS = {
    "L0_Wqkv": (D, 3 * D), "L0_Wos": (D, D), "L0_Wq": (D, D), "L0_Wk": (DC, D), "L0_Wv": (DC, D), "L0_Woc": (D, D),
    "L0_W1": (D, FF), "L0_W2": (FF, D),
    "L1_sa_wq": (D, MID), "L1_sa_wk": (D, MID), "L1_sa_wv": (D, MID), "L1_sa_wo": (MID, D),
    "L1_ca_wq": (D, MID), "L1_ca_wk": (DC, MID), "L1_ca_wv": (DC, MID), "L1_ca_wo": (MID, D),
    "L1_ff_w1": (D, FF), "L1_ff_w2": (FF, D),
    "L2_W_qkv": (D, 3 * D), "L2_W_proj": (D, D), "L2_W_ctx": (DC, D), "L2_W_q": (D, D), "L2_W_k": (D, D), "L2_W_v": (D, D),
    "L2_W_out": (D, D), "L2_W_fc1": (D, FF), "L2_W_fc2": (FF, D),
    "L3_cond_w": (DC, D), "L3_ca_q": (D, D), "L3_ca_k": (D, D), "L3_ca_v": (D, D), "L3_ca_out_w": (D, D),
    "L3_w1": (D, FF), "L3_w3": (D, FF), "L3_w2": (FF, D),
}


class Counted:

    def __init__(self, sem):
        self.sem, self.base = sem, 0

    def at(self, n):
        return self.sem, self.base + n

    def passed(self, n):
        self.base += n


class Chip:

    def __init__(self, nc, ctx, ins, out):
        self.nc, self.ins, self.out = nc, ins, out
        self._ctx, self._named = ctx, {}

        def sb(name, shape, dt=F32):
            return ctx.enter_context(nc.sbuf_tensor(name, shape, dt))

        self.x = sb("x", [P, TILES, D])
        self.hT = sb("hT", [P, C, T])
        self.w = [sb(f"w{i}", [P, 2048]) for i in range(4)]
        self.big1 = sb("big1", [P, 16384])
        self.big2 = sb("big2", [P, 16384])
        self.ident = sb("ident", [P, P])
        self.identb = sb("identb", [P, P], BF16)
        self.vec = sb("vec", [P, NVEC])
        self.mod = sb("mod", [P, NMOD, B])
        self.scale = sb("scale", [P, C, B])
        self.shift = sb("shift", [P, C, B])
        self.ctxT = sb("ctxT", [P, 2, B * M])
        self.ctx2T = sb("ctx2T", [P, 2, B * M])
        self.rows = sb("rows", [P, 4, D])
        self.small = sb("small", [P, 512])
        self.eps = sb("eps", [P, 2])
        self.ps = ctx.enter_context(nc.psum_tensor("ps", [P, 8, 512], F32))

        def dram(name, shape, dt):
            return nc.dram_tensor(name, shape, dt, kind="Internal").ap()

        self.q_parts = dram("q_parts", [HEADS // 4, 3, 4 * NARROW, N], BF16)
        self.k_parts = dram("k_parts", [HEADS // 4, 3, 4 * NARROW, N], BF16)
        self.kx_parts = dram("kx_parts", [HEADS // 4, 3, 4 * NARROW, M], BF16)
        self.q_wide = dram("q_wide", [HEADS, WIDE, N], F32)
        self.k_wide = dram("k_wide", [HEADS, WIDE, N], F32)
        self.kx_wide = dram("kx_wide", [HEADS, WIDE, M], F32)
        self.o_sums = dram("o_sums", [HEADS, 2 * NARROW, N], F32)
        self.o_wide = dram("o_wide", [HEADS, WIDE, N], F32)
        self.w_turn = 0
        self.where = {}
        self.weights_in = [self.semaphore("weights_in_even"), self.semaphore("weights_in_odd")]
        self.stage, self.due, self.coming = 0, 0, 0

    def semaphore(self, name):
        if name not in self._named:
            self._named[name] = Counted(self._ctx.enter_context(self.nc.semaphore(name)))
        return self._named[name]

    def v(self, name, c=0, n=1):
        return self.vec[:, OFFSET[name] + c:OFFSET[name] + c + n]

    def load_weights(self, sp, names):
        sig = self.weights_in[(self.stage + 1) % 2]
        n = 0
        for name in names:
            rows, cols = WEIGHTS[name]
            slot = self.w[self.w_turn % 4]
            self.w_turn += 1
            src = self.ins[name]
            chunks = -(-rows // P)
            view = slot[:, 0:chunks * cols].rearrange("p (c n) -> p c n", c=chunks)
            self.where[name] = view
            whole = rows // P
            sp.dma_start(view[:, 0:whole, :], src[0:whole * P, :].rearrange("(c p) n -> p c n", p=P)).then_inc(sig.sem, 16)
            n += 16
            if rows % P:
                sp.dma_start(view[0:rows % P, whole, :], src[whole * P:rows, :]).then_inc(sig.sem, 16)
                n += 16
        self.coming = n

    def weights_due(self):
        return self.weights_in[self.stage % 2].at(self.due)

    def end_stage(self):
        self.weights_in[self.stage % 2].passed(self.due)
        self.stage += 1
        self.due, self.coming = self.coming, 0


def setup(k, next_weights):
    nc = k.nc
    ins = k.ins
    loaded, mods_loaded = k.semaphore("inputs_loaded"), k.semaphore("mod_weights_loaded")
    made, masked, cond_ready = k.semaphore("constants_made"), k.semaphore("identity_ready"), k.semaphore("cond_ready")
    modded, done, trans = k.semaphore("mod_products"), k.semaphore("mod_done"), k.semaphore("ctx_transposed")
    wmod = k.big1[:, 0:C * NMOD * P].rearrange("p (c n) -> p c n", c=C)
    ctx_tok = k.big2[:, 0:2 * DC].rearrange("p (t d) -> p t d", t=2)
    condT = k.big2[:, 400:400 + C * B].rearrange("p (c b) -> p c b", c=C)
    siluT = k.big2[:, 416:416 + C * B].rearrange("p (c b) -> p c b", c=C)
    with nc.Block() as block:
        @block.sync
        def _(sp):
            sp.dma_start(k.vec[:, :], ins["vectors"]).then_inc(loaded.sem, 16)
            sp.dma_start(condT, ins["condT"].rearrange("(c p) b -> p c b", p=P)).then_inc(loaded.sem, 16)
            sp.dma_start(ctx_tok, ins["ctx"].rearrange("(t p) d -> p t d", p=P)).then_inc(loaded.sem, 16)
            for c in range(C):
                sp.dma_start(wmod[:, c, :], ins["mods"][c * P:(c + 1) * P, :]).then_inc(mods_loaded.sem, 16)
            sp.dma_start(k.x[:, :, :], ins["x"].rearrange("(t p) d -> p t d", p=P)).then_inc(loaded.sem, 16)
            k.load_weights(sp, next_weights)

        @block.gpsimd
        def _(pool):
            nc.gpsimd.memset(k.ident[:, :], 0.0).then_inc(made.sem, 1)
            nc.gpsimd.memset(k.identb[:, :], 0.0).then_inc(made.sem, 1)
            nc.gpsimd.memset(k.eps[:, 0:1], 1e-5).then_inc(made.sem, 1)
            nc.gpsimd.memset(k.eps[:, 1:2], 1e-6).then_inc(made.sem, 1)
            pool.wait_ge(*made.at(4))
            for m in (k.ident, k.identb):
                nc.gpsimd.affine_select(out=m[:, :], in_=m[:, :], compare_op=ALU.not_equal, fill=1.0, base=0,
                                        pattern=[[-1, P]], channel_multiplier=1).then_inc(masked.sem, 1)

        @block.scalar
        def _(act):
            act.wait_ge(*loaded.at(64))
            nc.scalar.activation(siluT, condT, ACT.Silu).then_inc(cond_ready.sem, 1)

        @block.tensor
        def _(pe):
            pe.wait_ge(*masked.at(2))
            pe.wait_ge(*loaded.at(64))
            for t in range(2):
                nc.tensor.transpose(k.ps[:, 1, t * P:(t + 1) * P], ctx_tok[:, t, 0:P], k.ident[:, :])
                last = nc.tensor.transpose(k.ps[0:DC - P, 2, t * P:(t + 1) * P], ctx_tok[:, t, P:DC], k.ident[:, :])
            last.then_inc(trans.sem, 1)
            pe.wait_ge(*cond_ready.at(1))
            pe.wait_ge(*mods_loaded.at(32))
            for m in range(NMOD):
                src = condT if MOD_AT["L1"] <= m < MOD_AT["L2"] else siluT
                for c in range(C):
                    last = nc.tensor.matmul(k.ps[:, 0, m * B:(m + 1) * B], wmod[:, c, m * P:(m + 1) * P], src[:, c, :],
                                            start=c == 0, stop=c == C - 1)
            last.then_inc(modded.sem, 1)

        @block.vector
        def _(dve):
            dve.wait_ge(*trans.at(1))
            nc.vector.tensor_copy(k.ctxT[:, 0, :], k.ps[:, 1, 0:B * M])
            nc.vector.tensor_copy(k.ctxT[0:DC - P, 1, :], k.ps[0:DC - P, 2, 0:B * M])
            dve.wait_ge(*modded.at(1))
            nc.vector.tensor_tensor(k.mod[:, :, :], k.ps[:, 0, 0:NMOD * B].rearrange("p (m b) -> p m b", b=B),
                                    k.vec[:, 0:NMOD].unsqueeze(2).broadcast_to([P, NMOD, B]), ALU.add).then_inc(done.sem, 1)
    for s, n in ((loaded, 64), (mods_loaded, 32), (made, 4), (masked, 2), (cond_ready, 1), (modded, 1), (done, 1), (trans, 1)):
        s.passed(n)
    k.end_stage()


def normalise(k, next_weights, shift_at, scale_at, w, b, eps):
    nc = k.nc
    coef, stats, var = k.semaphore("coefficients"), k.semaphore("stats"), k.semaphore("variances")
    root, rstd, rows = k.semaphore("roots"), k.semaphore("rstd"), k.semaphore("normed_rows")
    turned, out = k.semaphore("transposed"), k.semaphore("modulated")
    st = k.small[:, 0:96].rearrange("p (t s) -> p t s", s=6)
    mv = k.small[:, 96:128].rearrange("p (t s) -> p t s", s=2)
    sd, rs = k.small[:, 128:144], k.small[:, 144:160]
    xn = k.big1[:, 0:2 * TB * D].rearrange("p (s t d) -> p s t d", s=2, t=TB)
    with nc.Block() as block:
        @block.sync
        def _(sp):
            k.load_weights(sp, next_weights)

        @block.vector
        def _(dve):
            g = k.mod[:, scale_at:scale_at + C, :]
            s = k.mod[:, shift_at:shift_at + C, :]
            if w is None:
                nc.vector.tensor_scalar(k.scale[:, :, :], g, 1.0, None, ALU.add).then_inc(coef.sem, 1)
                nc.vector.tensor_copy(k.shift[:, :, :], s).then_inc(coef.sem, 1)
            else:
                wv = k.v(w, 0, C).unsqueeze(2).broadcast_to([P, C, B])
                bv = k.v(b, 0, C).unsqueeze(2).broadcast_to([P, C, B])
                nc.vector.scalar_tensor_tensor(k.scale[:, :, :], g, 1.0, wv, ALU.add, ALU.mult).then_inc(coef.sem, 1)
                nc.vector.scalar_tensor_tensor(k.shift[:, :, :], g, 1.0, bv, ALU.add, ALU.mult).then_inc(coef.sem, 1)
                dve.wait_ge(*coef.at(2))
                nc.vector.tensor_tensor(k.shift[:, :, :], k.shift[:, :, :], s, ALU.add).then_inc(coef.sem, 1)
            for t in range(TILES):
                nc.vector.bn_stats(st[:, t, :], k.x[:, t, :]).then_inc(stats.sem, 1)
            for t in range(TILES):
                dve.wait_ge(*stats.at(t + 1))
                nc.vector.bn_aggr(mv[:, t, :], st[:, t, :]).then_inc(var.sem, 1)
            dve.wait_ge(*root.at(1))
            nc.vector.reciprocal(rs, sd).then_inc(rstd.sem, 1)
            dve.wait_ge(*rstd.at(1))
            for bb in range(B):
                if bb >= 2:
                    dve.wait_ge(*turned.at(bb - 1))
                for i in range(TB):
                    t = bb * TB + i
                    nc.vector.tensor_scalar(xn[:, bb % 2, i, :], k.x[:, t, :], mv[:, t, 0:1], rs[:, t:t + 1],
                                            ALU.subtract, ALU.mult).then_inc(rows.sem, 1)

        @block.scalar
        def _(act):
            act.wait_ge(*var.at(TILES))
            nc.scalar.activation(sd, mv[:, :, 1], ACT.Sqrt, bias=k.eps[:, eps:eps + 1]).then_inc(root.sem, 1)
            act.wait_ge(*coef.at(2 if w is None else 3))
            for bb in range(B):
                act.wait_ge(*turned.at(bb + 1))
                for c in range(C):
                    nc.scalar.activation(k.hT[:, c, bb * N:(bb + 1) * N], k.ps[:, 2 * (bb % 2) + c, :], ACT.Identity,
                                         bias=k.shift[:, c, bb:bb + 1], scale=k.scale[:, c, bb:bb + 1]).then_inc(out.sem, 1)

        @block.tensor
        def _(pe):
            for bb in range(B):
                pe.wait_ge(*rows.at((bb + 1) * TB))
                if bb >= 2:
                    pe.wait_ge(*out.at(C * (bb - 1)))
                for c in range(C):
                    for i in range(TB):
                        last = nc.tensor.transpose(k.ps[:, 2 * (bb % 2) + c, i * P:(i + 1) * P],
                                                   xn[:, bb % 2, i, c * P:(c + 1) * P], k.ident[:, :])
                last.then_inc(turned.sem, 1)
    for s, n in ((coef, 2 if w is None else 3), (stats, TILES), (var, TILES), (root, 1), (rstd, 1), (rows, TILES),
                 (turned, B), (out, B * C)):
        s.passed(n)
    k.end_stage()


def row_of(k, pe, out, columns):
    for c in range(C):
        last = k.nc.tensor.matmul(out[:, c * P:(c + 1) * P], columns[c].broadcast_to([P, P]), k.ident[:, :],
                                  start=True, stop=True)
    return last



def set_row(k, bank, columns):
    for c in range(C):
        last = k.nc.tensor.matmul(bank[:, c * P:(c + 1) * P], columns[c].broadcast_to([P, P]), k.ident[:, :],
                                  start=True, stop=True)
    return last


class Split:

    SLOTS = 3

    def __init__(self, k):
        n = self.SLOTS
        self.k = k
        self.whole_ready, self.first_ready = k.semaphore("whole_ready"), k.semaphore("part_1_ready")
        self.left_ready, self.second_ready = k.semaphore("remainder_ready"), k.semaphore("part_2_ready")
        self.third_ready = k.semaphore("part_3_ready")
        self.stored = [k.semaphore(f"parts_stored_{i}") for i in range(n)]
        self.stores = [0] * n
        self.before = []
        self.whole = k.big1[:, 0:n * 512].rearrange("p (s n) -> p s n", s=n)
        self.left = k.big1[:, n * 512:2 * n * 512].rearrange("p (s n) -> p s n", s=n)
        self.parts = k.big1[:, 2 * n * 512:2 * n * 512 + n * 768].bitcast(BF16).rearrange("p (s c n) -> p s c n", s=n, c=3)

    def plan(self, stores):
        for u, n in enumerate(stores):
            self.before.append(self.stores[u % self.SLOTS])
            self.stores[u % self.SLOTS] += 16 * n

    def act_whole(self, act, u, source, bias, width, scale=1.0):
        if u >= self.SLOTS:
            act.wait_ge(*self.third_ready.at(u - self.SLOTS + 1))
        self.k.nc.scalar.activation(self.whole[:, u % self.SLOTS, 0:width], source, ACT.Identity, bias=bias,
                                    scale=scale).then_inc(self.whole_ready.sem, 1)

    def act_first(self, act, u, width):
        act.wait_ge(*self.whole_ready.at(u + 1))
        if u >= self.SLOTS:
            act.wait_ge(*self.stored[u % self.SLOTS].at(self.before[u]))
        self.k.nc.scalar.activation(self.parts[:, u % self.SLOTS, 0, 0:width], self.whole[:, u % self.SLOTS, 0:width],
                                    ACT.Copy).then_inc(self.first_ready.sem, 1)

    def dve_rest(self, dve, u, width):
        vector = self.k.nc.vector
        s, w = u % self.SLOTS, slice(0, width)
        dve.wait_ge(*self.first_ready.at(u + 1))
        vector.tensor_tensor(self.left[:, s, w], self.whole[:, s, w], self.parts[:, s, 0, w],
                             ALU.subtract).then_inc(self.left_ready.sem, 1)
        dve.wait_ge(*self.left_ready.at(u + 1))
        vector.tensor_copy(self.parts[:, s, 1, w], self.left[:, s, w]).then_inc(self.second_ready.sem, 1)
        dve.wait_ge(*self.second_ready.at(u + 1))
        vector.tensor_tensor(self.parts[:, s, 2, w], self.left[:, s, w], self.parts[:, s, 1, w],
                             ALU.subtract).then_inc(self.third_ready.sem, 1)

    def store(self, sp, u, dst, g):
        sp.wait_ge(*self.third_ready.at(u + 1))
        for half in range(2):
            sp.dma_start(dst[g + half].rearrange("c r t -> r c t"),
                         self.parts[64 * half:64 * half + 64, u % self.SLOTS, :, :]).then_inc(self.stored[u % self.SLOTS].sem, 16)

    def store_context(self, sp, u, m):
        sp.wait_ge(*self.third_ready.at(u + 1))
        by_batch = self.k.kx_parts.rearrange("(b g) c r t -> b g c r t", b=B)
        for half in range(2):
            for c in range(3):
                src = self.parts[64 * half:64 * half + 64, u % self.SLOTS, c, 0:B * M].rearrange("r (b t) -> r b t", b=B)
                sp.dma_start(by_batch[:, m * 2 + half, c, :, :].rearrange("b r t -> r b t"),
                             src).then_inc(self.stored[u % self.SLOTS].sem, 16)

    def all_stored(self, sp):
        for s in range(self.SLOTS):
            sp.wait_ge(*self.stored[s].at(self.stores[s]))

    def passed(self):
        units = len(self.before)
        for s in (self.whole_ready, self.first_ready, self.left_ready, self.second_ready, self.third_ready):
            s.passed(units)
        for s in range(self.SLOTS):
            self.stored[s].passed(self.stores[s])


def v_narrow(k):
    return k.big2[:, 0:TILES * D].rearrange("p (b g i d) -> p b g i d", b=B, g=4, i=TB)


def vx_narrow(k):
    return k.big2[0:M, 0:B * D].rearrange("p (b g d) -> p b g d", b=B, g=4)


def project_qkv(k, next_weights, w, bias):
    nc = k.nc
    split = Split(k)
    product, v_product, v_read = k.semaphore("product"), k.semaphore("v_product"), k.semaphore("v_read")
    row_made, row_in = k.semaphore("row_made"), k.semaphore("row_in")
    units = [(m, b) for m in range(4) for b in range(B)]
    split.plan([2] * len(units))
    v = v_narrow(k)
    with nc.Block() as block:
        @block.sync
        def _(sp):
            k.load_weights(sp, next_weights)
            for u, (m, b) in enumerate(units):
                split.store(sp, u, (k.q_parts, k.k_parts)[m // 2], b * 4 + (m % 2) * 2)
            split.all_stored(sp)

        @block.tensor
        def _(pe):
            wt = k.where[w]
            pe.wait_ge(*k.weights_due())
            set_row(k, k.ps[:, 7, :], [k.v(bias, 4 + c) for c in range(C)]).then_inc(row_made.sem, 1)
            for u, (m, b) in enumerate(units):
                if u >= 4:
                    pe.wait_ge(*split.whole_ready.at(u - 3))
                for c in range(C):
                    last = nc.tensor.matmul(k.ps[:, u % 4, :], wt[:, c, m * P:(m + 1) * P], k.hT[:, c, b * N:(b + 1) * N],
                                            start=c == 0, stop=c == C - 1)
                last.then_inc(product.sem, 1)
            for t in range(TILES):
                if t >= 3:
                    pe.wait_ge(*v_read.at(t - 2))
                for c in range(C):
                    last = nc.tensor.matmul(k.ps[:, 4 + t % 3, 0:D], k.hT[:, c, t * P:(t + 1) * P], wt[:, c, 2 * D:3 * D],
                                            start=c == 0, stop=c == C - 1)
                last.then_inc(v_product.sem, 1)

        @block.scalar
        def _(act):
            for u, (m, b) in enumerate(units):
                act.wait_ge(*product.at(u + 1))
                split.act_whole(act, u, k.ps[:, u % 4, :], k.v(bias, m), N)
                split.act_first(act, u, N)

        @block.vector
        def _(dve):
            dve.wait_ge(*row_made.at(1))
            nc.vector.tensor_copy(k.rows[:, 0, :], k.ps[:, 7, 0:D]).then_inc(row_in.sem, 1)
            for u in range(len(units)):
                split.dve_rest(dve, u, N)
            dve.wait_ge(*row_in.at(1))
            for t in range(TILES):
                dve.wait_ge(*v_product.at(t + 1))
                nc.vector.tensor_tensor(v[:, t // TB, :, t % TB, :], k.ps[:, 4 + t % 3, 0:D].rearrange("p (g d) -> p g d", g=4),
                                        k.rows[:, 0, :].rearrange("p (g d) -> p g d", g=4), ALU.add).then_inc(v_read.sem, 1)
    for s, n in ((product, len(units)), (v_product, TILES), (v_read, TILES), (row_made, 1), (row_in, 1)):
        s.passed(n)
    split.passed()
    k.end_stage()


def due(n):
    return not isinstance(n, int) or n > 0


def attend(k, next_weights, context):
    nc = k.nc
    keys = M if context else N
    blocks, width = (1, M) if context else (TB, P)
    score_units, exp_units = (1, 1) if context else (TB, 2)
    groups = HEADS // 4
    rows, stack = 6 * NARROW, 6 * NARROW + 2
    k_dram = k.kx_parts if context else k.k_parts
    v = vx_narrow(k).rearrange("p b g d -> p (b g) d").unsqueeze(2) if context else \
        v_narrow(k).rearrange("p b g i d -> p (b g) i d")

    q_st = k.big1[0:stack, 0:2048].bitcast(BF16).rearrange("p (u h t) -> p u h t", u=2, h=4)
    k_st = k.big1[0:stack, 2048:2048 + 4 * keys].bitcast(BF16).rearrange("p (u h t) -> p u h t", u=2, h=4)
    probs = [z[:, 4096:4096 + 4 * blocks * N].rearrange("p (h i t) -> p h i t", h=4, i=blocks) for z in (k.big1, k.big2)]
    spare = k.hT[:, :, :].rearrange("p c t -> p (c t)")
    v_st = spare[:, 0:2 * blocks * P].rearrange("p (u i h d) -> p u i h d", u=2, i=blocks, h=4)
    o_sb = spare[:, 1024:2048].rearrange("p (u t) -> p u t", u=2)
    neg_max = k.small[:, 0:8].rearrange("p (s a) -> p s a", s=2)
    max_parts = k.small[:, 8:16].bitcast(BF16).rearrange("p (s a c) -> p s a c", s=2, c=2)

    q_in, k_in = [k.semaphore(f"q_in_{u}") for u in range(2)], [k.semaphore(f"k_in_{u}") for u in range(2)]
    out_stored = [k.semaphore(f"out_stored_{u}") for u in range(2)]
    ones, v_in = k.semaphore("ones_made"), k.semaphore("v_staged")
    scores, maxed, max_split = k.semaphore("scores"), k.semaphore("maxed"), k.semaphore("max_split")
    max_turned, max_rows = k.semaphore("max_turned"), k.semaphore("max_rows")
    scores_t, exped, summed, o_out = k.semaphore("scores_t"), k.semaphore("exped"), k.semaphore("summed"), k.semaphore("o_out")

    with nc.Block() as block:
        @block.sync
        def _(sp):
            k.load_weights(sp, next_weights)

            def load(it, u):
                g = 2 * it + u
                if due(g - 1):
                    sp.wait_ge(*scores_t.at((g - 1) * 4 * exp_units))
                for p0, parts in ((0, 3), (3, 2), (5, 1)):
                    sp.dma_start(q_st[p0 * NARROW:(p0 + parts) * NARROW, u, :, :],
                                 k.q_parts[bass.ds(g, 1), 0:parts].rearrange("g c (d h) t -> (g c d) h t", h=4)).then_inc(q_in[u].sem, 16)
                for p0, part in ((0, 0), (1, 0), (2, 0), (3, 1), (4, 1), (5, 2)):
                    sp.dma_start(k_st[p0 * NARROW:(p0 + 1) * NARROW, u, :, :],
                                 k_dram[bass.ds(g, 1), part].rearrange("g (d h) t -> (g d) h t", h=4)).then_inc(k_in[u].sem, 16)

            def store(g, u):
                sp.wait_ge(*o_out.at(g + 1))
                sp.dma_start(k.o_sums[bass.ds(g * 4, 4)].rearrange("h r t -> (h r) t"), o_sb[:, u, :]).then_inc(out_stored[u].sem, 16)

            def groups_of(it):
                for u in range(2):
                    load(it, u)
                    if due(2 * it + u - 2):
                        store(2 * it + u - 3, 1 - u)

            groups_of(0)
            groups_of(1)
            with sp.Fori(2, groups // 2) as it:
                groups_of(it)
            for g in range(groups - 3, groups):
                store(g, g % 2)
            for u in range(2):
                sp.wait_ge(*out_stored[u].at(16 * (groups // 2)))

        @block.gpsimd
        def _(pool):
            nc.gpsimd.memset(k_st[rows:stack, :, :, :], 1.0).then_inc(ones.sem, 1)
            pool.wait_ge(*ones.at(1))
            nc.gpsimd.memset(v_st[:, :, :, :, NARROW:2 * NARROW], 1.0).then_inc(ones.sem, 1)

            def stage(it, u):
                g = 2 * it + u
                if due(g - 1):
                    pool.wait_ge(*summed.at(g - 1))
                src = v[0:width, bass.ds(g, 1), :, :].rearrange("p g i (h d) -> p (g i) h d", h=4)
                nc.gpsimd.tensor_copy(v_st[0:width, u, :, :, 0:NARROW], src).then_inc(v_in.sem, 1)

            for it in range(2):
                stage(it, 0)
                stage(it, 1)
            with pool.Fori(2, groups // 2) as it:
                stage(it, 0)
                stage(it, 1)

        @block.tensor
        def _(pe):
            def score(it, j):
                n, u, h = 8 * it + j, j // 4, j % 4
                if h == 0:
                    pe.wait_ge(*q_in[u].at(48 * it + 48))
                    pe.wait_ge(*k_in[u].at(96 * it + 96))
                for i in range(score_units):
                    m = n * score_units + i
                    if due(m - 1):
                        pe.wait_ge(*maxed.at(m - 1))
                    if context:
                        for a in range(TB):
                            last = nc.tensor.matmul(k.ps[:, j % 2, a * M:(a + 1) * M], q_st[0:rows, u, h, a * P:(a + 1) * P],
                                                    k_st[0:rows, u, h, :], start=True, stop=True)
                        last.then_inc(scores.sem, 1)
                    else:
                        nc.tensor.matmul(k.ps[:, i % 2, :], q_st[0:rows, u, h, i * P:(i + 1) * P], k_st[0:rows, u, h, :],
                                         start=True, stop=True).then_inc(scores.sem, 1)

            def score_t(it, j):
                n = 8 * it + j - 1
                u, h = (j - 1) // 4 % 2, (j - 1) % 4
                pe.wait_ge(*max_split.at(2 * n + 2))
                if due(n):
                    pe.wait_ge(*max_rows.at(n))
                for a in range(TB):
                    last = nc.tensor.matmul(k.ps[rows:stack, 7, a * P:(a + 1) * P], max_parts[:, (j - 1) % 2, a, :],
                                            k.identb[:, :], start=True, stop=True)
                last.then_inc(max_turned.sem, 1)
                pe.wait_ge(*max_rows.at(n + 1))
                for e in range(exp_units):
                    m = n * exp_units + e
                    if due(m - 1):
                        pe.wait_ge(*exped.at(m - 1))
                    if context:
                        last = nc.tensor.matmul(k.ps[0:M, 2 + (j - 1) % 2, :], k_st[:, u, h, :], q_st[:, u, h, :],
                                                start=True, stop=True)
                    else:
                        for i in (2 * e, 2 * e + 1):
                            last = nc.tensor.matmul(k.ps[:, 2 + i, :], k_st[:, u, h, i * P:(i + 1) * P], q_st[:, u, h, :],
                                                    start=True, stop=True)
                    last.then_inc(scores_t.sem, 1)

            def sum_ready(it, u):
                g = 2 * it + u - 1
                pe.wait_ge(*exped.at((g + 1) * 4 * exp_units))
                pe.wait_ge(*v_in.at(g + 1))
                if due(g):
                    pe.wait_ge(*o_out.at(g))

            def sum_up(u, i):
                for h in range(4):
                    last = nc.tensor.matmul(k.ps[32 * h:32 * h + 32, 6, :], v_st[0:width, 1 - u, i, h, :],
                                            probs[1 - u][0:width, h, i, :], start=i == 0, stop=i == blocks - 1)
                if i == blocks - 1:
                    last.then_inc(summed.sem, 1)

            def step(it, j):
                score(it, j)
                u, h = j // 4, j % 4
                with_sums = due(2 * it + u)
                if context and h == 2 and with_sums:
                    sum_ready(it, u)
                if due(8 * it + j):
                    score_t(it, j)
                if not with_sums:
                    return
                if context:
                    if h == 2:
                        sum_up(u, 0)
                elif h == 1:
                    sum_ready(it, u)
                    sum_up(u, 0)
                elif h == 2:
                    sum_up(u, 1)
                    sum_up(u, 2)
                elif h == 3:
                    sum_up(u, 3)

            pe.wait_ge(*ones.at(2))
            for it in range(2):
                for j in range(8):
                    step(it, j)
            with pe.Fori(2, groups // 2) as it:
                for j in range(8):
                    step(it, j)
            score_t(groups // 2, 0)
            sum_ready(groups // 2, 0)
            for i in range(blocks):
                sum_up(0, i)

        @block.vector
        def _(dve):
            def step(it, j):
                n, s = 8 * it + j, j % 2
                if due(n - 1):
                    dve.wait_ge(*max_split.at(2 * n - 2))
                    dve.wait_ge(*max_turned.at(n - 1))
                for i in range(score_units):
                    dve.wait_ge(*scores.at(n * score_units + i + 1))
                    if context:
                        nc.vector.tensor_reduce(neg_max[:, s, :], k.ps[:, s, 0:TB * M].rearrange("p (a m) -> p a m", a=TB),
                                                axis=AX.X, op=ALU.max, negate=True).then_inc(maxed.sem, 1)
                    else:
                        nc.vector.tensor_reduce(neg_max[:, s, i:i + 1], k.ps[:, i % 2, :], axis=AX.X, op=ALU.max,
                                                negate=True).then_inc(maxed.sem, 1)
                dve.wait_ge(*maxed.at((n + 1) * score_units))
                nc.vector.tensor_copy(max_parts[:, s, :, 0], neg_max[:, s, :]).then_inc(max_split.sem, 1)
                dve.wait_ge(*max_split.at(2 * n + 1))
                nc.vector.tensor_tensor(max_parts[:, s, :, 1], neg_max[:, s, :], max_parts[:, s, :, 0],
                                        ALU.subtract).then_inc(max_split.sem, 1)

            for it in range(2):
                for j in range(8):
                    step(it, j)
            with dve.Fori(2, groups // 2) as it:
                for j in range(8):
                    step(it, j)

        @block.scalar
        def _(act):
            def exps(it, j):
                n, g = 8 * it + j - 1, 2 * it + (j - 1) // 4
                u, h = (j - 1) // 4 % 2, (j - 1) % 4
                act.wait_ge(*max_turned.at(n + 1))
                nc.scalar.activation(q_st[rows:stack, u, h, :], k.ps[rows:stack, 7, :], ACT.Copy).then_inc(max_rows.sem, 1)
                if h == 0 and due(g - 1):
                    act.wait_ge(*summed.at(g - 1))
                for e in range(exp_units):
                    act.wait_ge(*scores_t.at(n * exp_units + e + 1))
                    if context:
                        nc.scalar.activation(probs[u][0:M, h, 0, :], k.ps[0:M, 2 + (j - 1) % 2, :], ACT.Exp,
                                             scale=NARROW ** -0.5).then_inc(exped.sem, 1)
                    else:
                        nc.scalar.activation(probs[u][:, h, 2 * e:2 * e + 2, :], k.ps[:, 2 + 2 * e:4 + 2 * e, :], ACT.Exp,
                                             scale=NARROW ** -0.5).then_inc(exped.sem, 1)

            def out(it, u):
                g = 2 * it + u
                act.wait_ge(*summed.at(g - 1))
                if due(it - 1):
                    act.wait_ge(*out_stored[u].at(16 * it - 16))
                nc.scalar.activation(o_sb[:, u, :], k.ps[:, 6, :], ACT.Copy).then_inc(o_out.sem, 1)

            def step(it, j):
                if due(8 * it + j):
                    exps(it, j)
                if j % 4 == 0 and due(it):
                    out(it, j // 4)

            for it in range(2):
                for j in range(8):
                    step(it, j)
            with act.Fori(2, groups // 2) as it:
                for j in range(8):
                    step(it, j)
            exps(groups // 2, 0)
            out(groups // 2, 0)
            out(groups // 2, 1)
    for s, n in ((q_in[0], 24 * groups), (q_in[1], 24 * groups), (k_in[0], 48 * groups), (k_in[1], 48 * groups),
                 (out_stored[0], 8 * groups), (out_stored[1], 8 * groups), (ones, 2), (v_in, groups),
                 (scores, HEADS * score_units), (maxed, HEADS * score_units), (max_split, 2 * HEADS), (max_turned, HEADS),
                 (max_rows, HEADS), (scores_t, HEADS * exp_units), (exped, HEADS * exp_units), (summed, groups), (o_out, groups)):
        s.passed(n)
    k.end_stage()


def rows_at(k, n):
    return k.big2[:, 12288:12288 + n * D].rearrange("p (n d) -> p n d", n=n)


def project_out(k, next_weights, w, bias, gate, wide):
    nc = k.nc
    chunks = MID // P if wide else C
    loaded = [k.semaphore(f"out_loaded_{b}") for b in range(B)]
    inverse, divided = k.semaphore("inverse"), k.semaphore("divided")
    row_made, row_in, row_scaled, biased = k.semaphore("row_made"), k.semaphore("row_in"), k.semaphore("row_scaled"), k.semaphore("biased")
    product, scaled, added = k.semaphore("product"), k.semaphore("scaled"), k.semaphore("added")
    o = k.big1[:, 0:chunks * T].rearrange("p (c t) -> p c t", c=chunks)
    sums = k.big1[:, C * T:2 * C * T].rearrange("p (c t) -> p c t", c=C)
    gates, gated_bias = rows_at(k, 2 * B)[:, 0:B, :], rows_at(k, 2 * B)[:, B:2 * B, :]
    tmp = k.big2[:, 0:2 * D].rearrange("p (s d) -> p s d", s=2)
    bias_row = k.rows[:, 0, :]
    n_rows = (bias is not None) + (B if gate is not None else 0)
    with nc.Block() as block:
        @block.sync
        def _(sp):
            for b in range(B):
                cols = slice(b * N, (b + 1) * N)
                if wide:
                    src = k.o_wide[b * H:(b + 1) * H].rearrange("h d t -> (h d) t").rearrange("(c p) t -> p c t", p=P)
                    sp.dma_start(o[:, :, cols], src).then_inc(loaded[b].sem, 16)
                    continue
                for c in range(C):
                    h = b * H + c * 8
                    sp.dma_start(o[:, c, cols], k.o_sums[h:h + 8, 0:NARROW, :]).then_inc(loaded[b].sem, 16)
                    sp.dma_start(sums[:, c, cols], k.o_sums[h:h + 8, NARROW:2 * NARROW, :]).then_inc(loaded[b].sem, 16)
            k.load_weights(sp, next_weights)

        @block.tensor
        def _(pe):
            pe.wait_ge(*k.weights_due()) if k.due else None
            n = 0
            if bias is not None:
                set_row(k, k.ps[:, 7, :], [k.v(bias, c) for c in range(C)]).then_inc(row_made.sem, 1)
                n += 1
            if gate is not None:
                for b in range(B):
                    if n:
                        pe.wait_ge(*row_in.at(n))
                    set_row(k, k.ps[:, 7, :], [k.mod[:, gate + c, b:b + 1] for c in range(C)]).then_inc(row_made.sem, 1)
                    n += 1
            wt = k.where[w] if w else None
            for t in range(TILES):
                if t % TB == 0:
                    if wide:
                        pe.wait_ge(*loaded[t // TB].at(16))
                    else:
                        pe.wait_ge(*divided.at(C * (t // TB + 1)))
                if t >= 4:
                    pe.wait_ge(*added.at(t - 3))
                for c in range(chunks):
                    if w:
                        last = nc.tensor.matmul(k.ps[:, t % 4, 0:D], o[:, c, t * P:(t + 1) * P], wt[:, c, :],
                                                start=c == 0, stop=c == chunks - 1)
                    else:
                        last = nc.tensor.transpose(k.ps[:, t % 4, c * P:(c + 1) * P], o[:, c, t * P:(t + 1) * P], k.ident[:, :])
                last.then_inc(product.sem, 1)

        @block.gpsimd
        def _(pool):
            if bias is None:
                return
            pool.wait_ge(*row_in.at(n_rows))
            for b in range(B):
                row = bias_row
                if gate is not None:
                    nc.gpsimd.tensor_tensor(gated_bias[:, b, :], gates[:, b, :], bias_row, ALU.mult).then_inc(row_scaled.sem, 1)
                    pool.wait_ge(*row_scaled.at(b + 1))
                    row = gated_bias[:, b, :]
                xb = k.x[:, b * TB:(b + 1) * TB, :]
                nc.gpsimd.tensor_tensor(xb, xb, row.unsqueeze(1).broadcast_to([P, TB, D]), ALU.add).then_inc(biased.sem, 1)

        @block.scalar
        def _(act):
            for r in range(n_rows):
                act.wait_ge(*row_made.at(r + 1))
                dst = bias_row if bias is not None and r == 0 else gates[:, r - (bias is not None), :]
                nc.scalar.activation(dst, k.ps[:, 7, 0:D], ACT.Copy).then_inc(row_in.sem, 1)

        @block.vector
        def _(dve):
            for b in range(0 if wide else B):
                cols = slice(b * N, (b + 1) * N)
                dve.wait_ge(*loaded[b].at(64))
                for c in range(C):
                    nc.vector.reciprocal(sums[:, c, cols], sums[:, c, cols]).then_inc(inverse.sem, 1)
                    dve.wait_ge(*inverse.at(b * C + c + 1))
                    nc.vector.tensor_tensor(o[:, c, cols], o[:, c, cols], sums[:, c, cols], ALU.mult).then_inc(divided.sem, 1)
            if gate is not None:
                dve.wait_ge(*row_in.at(n_rows))
            for t in range(TILES):
                if bias is not None and t % TB == 0:
                    dve.wait_ge(*biased.at(t // TB + 1))
                dve.wait_ge(*product.at(t + 1))
                src = k.ps[:, t % 4, 0:D]
                if gate is not None:
                    if t >= 2:
                        dve.wait_ge(*added.at(t - 1))
                    nc.vector.tensor_tensor(tmp[:, t % 2, :], src, gates[:, t // TB, :], ALU.mult).then_inc(scaled.sem, 1)
                    dve.wait_ge(*scaled.at(t + 1))
                    src = tmp[:, t % 2, :]
                nc.vector.tensor_tensor(k.x[:, t, :], src, k.x[:, t, :], ALU.add).then_inc(added.sem, 1)
    for b in range(B):
        loaded[b].passed(16 if wide else 64)
    for s, n in ((inverse, 0 if wide else B * C), (divided, 0 if wide else B * C), (row_made, n_rows), (row_in, n_rows),
                 (row_scaled, B if bias is not None and gate is not None else 0), (biased, B if bias is not None else 0),
                 (product, TILES), (scaled, TILES if gate is not None else 0), (added, TILES)):
        s.passed(n)
    k.end_stage()


def project_cross(k, next_weights, pre, wq, wk, wv, bq, bk, bv):
    nc = k.nc
    split = Split(k)
    product, v_product, v_read = k.semaphore("product"), k.semaphore("v_product"), k.semaphore("v_read")
    row_made, row_in, pre_made, pre_in = k.semaphore("row_made"), k.semaphore("row_in"), k.semaphore("pre_made"), k.semaphore("pre_in")
    units = [("k", m, 0) for m in range(C)] + [("q", m, b) for m in range(C) for b in range(B)]
    split.plan([6 if kind == "k" else 2 for kind, _, _ in units])
    source = k.ctx2T if pre else k.ctxT
    depth = [P, P] if pre else [P, DC - P]
    v = vx_narrow(k)

    def width(kind):
        return B * M if kind == "k" else N

    with nc.Block() as block:
        @block.sync
        def _(sp):
            k.load_weights(sp, next_weights)
            for u, (kind, m, b) in enumerate(units):
                if kind == "k":
                    split.store_context(sp, u, m)
                else:
                    split.store(sp, u, k.q_parts, b * 4 + m * 2)
            split.all_stored(sp)

        @block.tensor
        def _(pe):
            pe.wait_ge(*k.weights_due())
            if bv:
                set_row(k, k.ps[:, 7, :], [k.v(bv[0], bv[1] + c) for c in range(C)]).then_inc(row_made.sem, 1)
            if pre:
                wt = k.where[pre[0]]
                for m in range(C):
                    for c, r in enumerate((P, DC - P)):
                        last = nc.tensor.matmul(k.ps[:, 6, m * B * M:(m + 1) * B * M], wt[0:r, c, m * P:(m + 1) * P],
                                                k.ctxT[0:r, c, :], start=c == 0, stop=c == 1)
                last.then_inc(pre_made.sem, 1)
                pe.wait_ge(*pre_in.at(C))
            for u, (kind, m, b) in enumerate(units):
                if u >= 4:
                    pe.wait_ge(*split.whole_ready.at(u - 3))
                for c in range(C):
                    if kind == "k":
                        r = depth[c]
                        last = nc.tensor.matmul(k.ps[:, u % 4, 0:B * M], k.where[wk][0:r, c, m * P:(m + 1) * P], source[0:r, c, :],
                                                start=c == 0, stop=c == C - 1)
                    else:
                        last = nc.tensor.matmul(k.ps[:, u % 4, :], k.where[wq][:, c, m * P:(m + 1) * P],
                                                k.hT[:, c, b * N:(b + 1) * N], start=c == 0, stop=c == C - 1)
                last.then_inc(product.sem, 1)
            for b in range(B):
                if b >= 2:
                    pe.wait_ge(*v_read.at(b - 1))
                for c in range(C):
                    r = depth[c]
                    last = nc.tensor.matmul(k.ps[0:M, 4 + b % 2, 0:D], source[0:r, c, b * M:(b + 1) * M], k.where[wv][0:r, c, :],
                                            start=c == 0, stop=c == C - 1)
                last.then_inc(v_product.sem, 1)

        @block.scalar
        def _(act):
            if pre:
                act.wait_ge(*pre_made.at(1))
                for m in range(C):
                    nc.scalar.activation(k.ctx2T[:, m, :], k.ps[:, 6, m * B * M:(m + 1) * B * M], ACT.Identity,
                                         bias=k.v(pre[1], m)).then_inc(pre_in.sem, 1)
            for u, (kind, m, b) in enumerate(units):
                bias = bk if kind == "k" else bq
                act.wait_ge(*product.at(u + 1))
                split.act_whole(act, u, k.ps[:, u % 4, 0:width(kind)], k.v(bias[0], bias[1] + m) if bias else 0.0, width(kind))
                split.act_first(act, u, width(kind))

        @block.vector
        def _(dve):
            if bv:
                dve.wait_ge(*row_made.at(1))
                nc.vector.tensor_copy(k.rows[:, 0, :], k.ps[:, 7, 0:D]).then_inc(row_in.sem, 1)
            for u, (kind, _, _) in enumerate(units):
                split.dve_rest(dve, u, width(kind))
            if bv:
                dve.wait_ge(*row_in.at(1))
            for b in range(B):
                dve.wait_ge(*v_product.at(b + 1))
                src = k.ps[0:M, 4 + b % 2, 0:D].rearrange("p (g d) -> p g d", g=4)
                if bv:
                    nc.vector.tensor_tensor(v[:, b, :, :], src, k.rows[0:M, 0, :].rearrange("p (g d) -> p g d", g=4),
                                            ALU.add).then_inc(v_read.sem, 1)
                else:
                    nc.vector.tensor_copy(v[:, b, :, :], src).then_inc(v_read.sem, 1)
    for s, n in ((product, len(units)), (v_product, B), (v_read, B), (row_made, 1 if bv else 0), (row_in, 1 if bv else 0),
                 (pre_made, 1 if pre else 0), (pre_in, C if pre else 0)):
        s.passed(n)
    split.passed()
    k.end_stage()


def feed_forward(k, next_weights, up, gate_up, down, b_up, b_down, func, gate):
    nc = k.nc
    product, halved, hidden_ready = k.semaphore("product"), k.semaphore("activated"), k.semaphore("hidden")
    row_made, row_in, biased = k.semaphore("row_made"), k.semaphore("row_in"), k.semaphore("biased")
    down_product, scaled, added, final = k.semaphore("down_product"), k.semaphore("scaled"), k.semaphore("added"), k.semaphore("final_stored")
    hidden = k.big1[:, 0:2 * FC * N].rearrange("p (s m t) -> p s m t", s=2, m=FC)
    half = k.big1[:, 8192:8192 + 2 * N].rearrange("p (s t) -> p s t", s=2)
    gates = rows_at(k, B)
    tmp = k.big2[:, 0:2 * D].rearrange("p (s d) -> p s d", s=2)
    n_rows = (b_down is not None) + (B if gate is not None else 0)
    last_stage = next_weights is None
    with nc.Block() as block:
        @block.sync
        def _(sp):
            if not last_stage:
                k.load_weights(sp, next_weights)
                return
            out = k.out.rearrange("b (t p) d -> p (b t) d", p=P)
            for t in range(0, TILES, 2):
                sp.wait_ge(*added.at(t + 2))
                sp.dma_start(out[:, t:t + 2, :], k.x[:, t:t + 2, :]).then_inc(final.sem, 16)
            sp.wait_ge(*final.at(16 * TILES // 2))

        @block.tensor
        def _(pe):
            pe.wait_ge(*k.weights_due())
            n = 0
            if b_down is not None:
                set_row(k, k.ps[:, 7, :], [k.v(b_down, c) for c in range(C)]).then_inc(row_made.sem, 1)
                n += 1
            if gate is not None:
                for b in range(B):
                    if n:
                        pe.wait_ge(*row_in.at(n))
                    set_row(k, k.ps[:, 7, :], [k.mod[:, gate + c, b:b + 1] for c in range(C)]).then_inc(row_made.sem, 1)
                    n += 1

            def ups(b):
                for m in range(FC):
                    u = b * FC + m
                    if gate_up:
                        if u >= 2:
                            pe.wait_ge(*hidden_ready.at(u - 1))
                    elif u >= 4:
                        pe.wait_ge(*hidden_ready.at(u - 3))
                    for i, name in enumerate((up, gate_up) if gate_up else (up,)):
                        bank = 2 * (u % 2) + i if gate_up else u % 4
                        for c in range(C):
                            last = nc.tensor.matmul(k.ps[:, bank, :], k.where[name][:, c, m * P:(m + 1) * P],
                                                    k.hT[:, c, b * N:(b + 1) * N], start=c == 0, stop=c == C - 1)
                    last.then_inc(product.sem, 1)

            def downs(b):
                pe.wait_ge(*hidden_ready.at((b + 1) * FC))
                for i in range(TB):
                    t = b * TB + i
                    if t >= 2:
                        pe.wait_ge(*added.at(t - 1))
                    for m in range(FC):
                        last = nc.tensor.matmul(k.ps[:, 4 + t % 2, 0:D], hidden[:, b % 2, m, i * P:(i + 1) * P], k.where[down][:, m, :],
                                                start=m == 0, stop=m == FC - 1)
                    last.then_inc(down_product.sem, 1)

            for b in range(B):
                ups(b)
                if b:
                    downs(b - 1)
            downs(B - 1)

        @block.gpsimd
        def _(pool):
            if b_down is None:
                return
            pool.wait_ge(*row_in.at(1))
            for b in range(B):
                xb = k.x[:, b * TB:(b + 1) * TB, :]
                nc.gpsimd.tensor_tensor(xb, xb, k.rows[:, 0:1, :].broadcast_to([P, TB, D]), ALU.add).then_inc(biased.sem, 1)

        @block.scalar
        def _(act):
            for r in range(n_rows):
                act.wait_ge(*row_made.at(r + 1))
                dst = k.rows[:, 0, :] if b_down is not None and r == 0 else gates[:, r - (b_down is not None), :]
                nc.scalar.activation(dst, k.ps[:, 7, 0:D], ACT.Copy).then_inc(row_in.sem, 1)
            for b in range(B):
                if b >= 2:
                    act.wait_ge(*down_product.at((b - 1) * TB))
                for m in range(FC):
                    u = b * FC + m
                    act.wait_ge(*product.at(u + 1))
                    if gate_up:
                        if u >= 2:
                            act.wait_ge(*hidden_ready.at(u - 1))
                        nc.scalar.activation(half[:, u % 2, :], k.ps[:, 2 * (u % 2), :], func).then_inc(halved.sem, 1)
                    else:
                        nc.scalar.activation(hidden[:, b % 2, m, :], k.ps[:, u % 4, :], func,
                                             bias=k.v(b_up, m)).then_inc(hidden_ready.sem, 1)

        @block.vector
        def _(dve):
            def mix(b):
                for m in range(FC):
                    u = b * FC + m
                    dve.wait_ge(*halved.at(u + 1))
                    nc.vector.tensor_tensor(hidden[:, b % 2, m, :], k.ps[:, 2 * (u % 2) + 1, :], half[:, u % 2, :],
                                            ALU.mult).then_inc(hidden_ready.sem, 1)

            def add(b):
                for i in range(TB):
                    t = b * TB + i
                    if b_down is not None and i == 0:
                        dve.wait_ge(*biased.at(b + 1))
                    dve.wait_ge(*down_product.at(t + 1))
                    src = k.ps[:, 4 + t % 2, 0:D]
                    if gate is not None:
                        if t >= 2:
                            dve.wait_ge(*added.at(t - 1))
                        nc.vector.tensor_tensor(tmp[:, t % 2, :], src, gates[:, b, :], ALU.mult).then_inc(scaled.sem, 1)
                        dve.wait_ge(*scaled.at(t + 1))
                        src = tmp[:, t % 2, :]
                    nc.vector.tensor_tensor(k.x[:, t, :], src, k.x[:, t, :], ALU.add).then_inc(added.sem, 1)

            if gate is not None:
                dve.wait_ge(*row_in.at(n_rows))
            for b in range(B):
                if gate_up:
                    mix(b)
                if b:
                    add(b - 1)
            add(B - 1)
    for s, n in ((product, B * FC), (halved, B * FC if gate_up else 0), (hidden_ready, B * FC), (row_made, n_rows), (row_in, n_rows),
                 (biased, B if b_down is not None else 0), (down_product, TILES), (scaled, TILES if gate is not None else 0),
                 (added, TILES), (final, 8 * TILES if last_stage else 0)):
        s.passed(n)
    k.end_stage()


def normalise_heads(k, next_weights, shift_at, scale_at, eps):
    nc = k.nc
    split = Split(k)
    row_made, row_in = k.semaphore("row_made"), k.semaphore("row_in")
    stats, var, root, rstd, normed = k.semaphore("stats"), k.semaphore("variances"), k.semaphore("roots"), k.semaphore("rstd"), k.semaphore("normed_rows")
    h_scaled, h_ready, v_copied = k.semaphore("h_scaled"), k.semaphore("h_ready"), k.semaphore("v_copied")
    h_sum, h_mean, h_centred, h_squared = k.semaphore("h_sum"), k.semaphore("h_mean"), k.semaphore("h_centred"), k.semaphore("h_squared")
    h_var, h_root, h_rstd, h_normed, turned = k.semaphore("h_var"), k.semaphore("h_root"), k.semaphore("h_rstd"), k.semaphore("h_normed"), k.semaphore("transposed")
    st = k.small[:, 0:96].rearrange("p (t s) -> p t s", s=6)
    mv = k.small[:, 96:128].rearrange("p (t s) -> p t s", s=2)
    sd, rs = k.small[:, 128:144], k.small[:, 144:160]
    hs, hm, hv, hsd, hr = (k.small[:, 160 + 64 * i:224 + 64 * i] for i in range(5))
    xn = k.big1[:, 6144:7168].rearrange("p (i d) -> p i d", i=TB)
    h1 = k.big1[:, 7168:8192].rearrange("p (i d) -> p i d", i=TB)
    h = k.big1[:, 8192:10240].rearrange("p (s i d) -> p s i d", s=2, i=TB)
    hc = k.big1[:, 10240:11264]
    sq = k.big1[:, 11264:12288]
    hn = k.big1[:, 12288:14336].rearrange("p (s j) -> p s j", s=2)
    rows = rows_at(k, 2 * B)
    v = v_narrow(k)
    units = [(b, c, kind) for b in range(B) for c in range(C) for kind in range(2)]
    split.plan([2] * len(units))

    def per_head(flat):
        return flat.unsqueeze(2).broadcast_to([P, TB * H, NARROW])

    with nc.Block() as block:
        @block.sync
        def _(sp):
            k.load_weights(sp, next_weights)
            for u, (b, c, kind) in enumerate(units):
                split.store(sp, u, (k.q_parts, k.k_parts)[kind], b * 4 + c * 2)
            split.all_stored(sp)

        @block.tensor
        def _(pe):
            for r in range(2 * B):
                b, at = r // 2, (scale_at, shift_at)[r % 2]
                if r >= 2:
                    pe.wait_ge(*row_in.at(r - 1))
                set_row(k, k.ps[:, 6 + r % 2, :], [k.mod[:, at + c, b:b + 1] for c in range(C)]).then_inc(row_made.sem, 1)
            for b in range(B):
                pe.wait_ge(*h_normed.at(b + 1))
                if b >= 2:
                    pe.wait_ge(*split.whole_ready.at(4 * (b - 1)))
                for c in range(C):
                    for i in range(TB):
                        src = hn[:, b % 2, i * D + c * P:i * D + (c + 1) * P]
                        last = nc.tensor.transpose(k.ps[:, 2 * (b % 2) + c, i * P:(i + 1) * P], src, k.ident[:, :])
                last.then_inc(turned.sem, 1)

        @block.gpsimd
        def _(pool):
            for b in range(B):
                pool.wait_ge(*h_ready.at(b + 1))
                nc.gpsimd.tensor_copy(v[:, b].rearrange("p g i d -> p i g d"),
                                      h[:, b % 2].rearrange("p i (g d) -> p i g d", g=4)).then_inc(v_copied.sem, 1)

        @block.scalar
        def _(act):
            for r in range(2 * B):
                act.wait_ge(*row_made.at(r + 1))
                nc.scalar.activation(rows[:, r, :], k.ps[:, 6 + r % 2, 0:D], ACT.Identity, bias=1.0 if r % 2 == 0 else 0.0).then_inc(row_in.sem, 1)
            act.wait_ge(*var.at(TILES))
            nc.scalar.activation(sd, mv[:, :, 1], ACT.Sqrt, bias=k.eps[:, eps:eps + 1]).then_inc(root.sem, 1)

            def parts(b):
                act.wait_ge(*turned.at(b + 1))
                for u in range(4 * b, 4 * b + 4):
                    _, c, kind = units[u]
                    w, bias = (("L3_qn_w", "L3_qn_b"), ("L3_kn_w", "L3_kn_b"))[kind]
                    split.act_whole(act, u, k.ps[:, 2 * (b % 2) + c, :], k.v(bias), N, scale=k.v(w))
                    split.act_first(act, u, N)

            for b in range(B):
                act.wait_ge(*h_centred.at(b + 1))
                nc.scalar.activation(sq, hc, ACT.Square).then_inc(h_squared.sem, 1)
                act.wait_ge(*h_var.at(b + 1))
                nc.scalar.activation(hsd, hv, ACT.Sqrt, bias=k.eps[:, eps:eps + 1], scale=1.0 / NARROW).then_inc(h_root.sem, 1)
                if b:
                    parts(b - 1)
            parts(B - 1)

        @block.vector
        def _(dve):
            for t in range(TILES):
                nc.vector.bn_stats(st[:, t, :], k.x[:, t, :]).then_inc(stats.sem, 1)
            for t in range(TILES):
                dve.wait_ge(*stats.at(t + 1))
                nc.vector.bn_aggr(mv[:, t, :], st[:, t, :]).then_inc(var.sem, 1)
            dve.wait_ge(*root.at(1))
            nc.vector.reciprocal(rs, sd).then_inc(rstd.sem, 1)
            dve.wait_ge(*rstd.at(1))
            dve.wait_ge(*row_in.at(2 * B))
            for b in range(B):
                if b:
                    dve.wait_ge(*h_scaled.at(b))
                for i in range(TB):
                    t = b * TB + i
                    nc.vector.tensor_scalar(xn[:, i, :], k.x[:, t, :], mv[:, t, 0:1], rs[:, t:t + 1],
                                            ALU.subtract, ALU.mult).then_inc(normed.sem, 1)
                dve.wait_ge(*normed.at((b + 1) * TB))
                if b:
                    dve.wait_ge(*h_ready.at(b))
                nc.vector.tensor_tensor(h1, xn, rows[:, 2 * b:2 * b + 1, :].broadcast_to([P, TB, D]), ALU.mult).then_inc(h_scaled.sem, 1)
                dve.wait_ge(*h_scaled.at(b + 1))
                if b >= 2:
                    dve.wait_ge(*v_copied.at(b - 1))
                nc.vector.tensor_tensor(h[:, b % 2], h1, rows[:, 2 * b + 1:2 * b + 2, :].broadcast_to([P, TB, D]), ALU.add).then_inc(h_ready.sem, 1)
                dve.wait_ge(*h_ready.at(b + 1))
                heads = h[:, b % 2].rearrange("p i (h d) -> p (i h) d", d=NARROW)
                if b:
                    dve.wait_ge(*h_mean.at(b))
                nc.vector.tensor_reduce(hs, heads, axis=AX.X, op=ALU.add).then_inc(h_sum.sem, 1)
                dve.wait_ge(*h_sum.at(b + 1))
                if b:
                    dve.wait_ge(*h_centred.at(b))
                nc.vector.tensor_scalar(hm, hs, 1.0 / NARROW, None, ALU.mult).then_inc(h_mean.sem, 1)
                dve.wait_ge(*h_mean.at(b + 1))
                if b:
                    dve.wait_ge(*h_normed.at(b))
                nc.vector.tensor_tensor(hc.rearrange("p (j d) -> p j d", d=NARROW), heads, per_head(hm),
                                        ALU.subtract).then_inc(h_centred.sem, 1)
                dve.wait_ge(*h_squared.at(b + 1))
                if b:
                    dve.wait_ge(*h_root.at(b))
                nc.vector.tensor_reduce(hv, sq.rearrange("p (j d) -> p j d", d=NARROW), axis=AX.X, op=ALU.add).then_inc(h_var.sem, 1)
                dve.wait_ge(*h_root.at(b + 1))
                nc.vector.reciprocal(hr, hsd).then_inc(h_rstd.sem, 1)
                dve.wait_ge(*h_rstd.at(b + 1))
                if b >= 2:
                    dve.wait_ge(*turned.at(b - 1))
                nc.vector.tensor_tensor(hn[:, b % 2].rearrange("p (j d h) -> p j h d", h=4, d=NARROW),
                                        hc.rearrange("p (j h d) -> p j h d", h=4, d=NARROW),
                                        hr.rearrange("p (j h) -> p j h", h=4).unsqueeze(3).broadcast_to([P, TB * 4, 4, NARROW]),
                                        ALU.mult).then_inc(h_normed.sem, 1)
                if b:
                    for u in range(4 * b - 4, 4 * b):
                        split.dve_rest(dve, u, N)
            for u in range(4 * B - 4, 4 * B):
                split.dve_rest(dve, u, N)
    for s, n in ((row_made, 2 * B), (row_in, 2 * B), (stats, TILES), (var, TILES), (root, 1), (rstd, 1), (normed, TILES),
                 (h_scaled, B), (h_ready, B), (v_copied, B), (h_sum, B), (h_mean, B), (h_centred, B), (h_squared, B), (h_var, B),
                 (h_root, B), (h_rstd, B), (h_normed, B), (turned, B)):
        s.passed(n)
    split.passed()
    k.end_stage()


def normalise_context(k, next_weights, w, b):
    nc = k.nc
    loaded, stats, var, root, rstd = k.semaphore("context_loaded"), k.semaphore("stats"), k.semaphore("variances"), k.semaphore("roots"), k.semaphore("rstd")
    rows, turned, out = k.semaphore("normed_rows"), k.semaphore("transposed"), k.semaphore("modulated")
    tok = k.big2[:, 0:2 * DC].rearrange("p (t d) -> p t d", t=2)
    xn = k.big2[:, 512:512 + 2 * DC].rearrange("p (t d) -> p t d", t=2)
    st, mv = k.small[:, 0:12].rearrange("p (t s) -> p t s", s=6), k.small[:, 12:16].rearrange("p (t s) -> p t s", s=2)
    sd, rs = k.small[:, 16:18], k.small[:, 18:20]
    depth = (P, DC - P)
    with nc.Block() as block:
        @block.sync
        def _(sp):
            sp.dma_start(tok, k.ins["ctx"].rearrange("(t p) d -> p t d", p=P)).then_inc(loaded.sem, 16)
            k.load_weights(sp, next_weights)

        @block.vector
        def _(dve):
            dve.wait_ge(*loaded.at(16))
            for t in range(2):
                nc.vector.bn_stats(st[:, t, :], tok[:, t, :]).then_inc(stats.sem, 1)
            dve.wait_ge(*stats.at(2))
            for t in range(2):
                nc.vector.bn_aggr(mv[:, t, :], st[:, t, :]).then_inc(var.sem, 1)
            dve.wait_ge(*root.at(1))
            nc.vector.reciprocal(rs, sd).then_inc(rstd.sem, 1)
            dve.wait_ge(*rstd.at(1))
            for t in range(2):
                nc.vector.tensor_scalar(xn[:, t, :], tok[:, t, :], mv[:, t, 0:1], rs[:, t:t + 1],
                                        ALU.subtract, ALU.mult).then_inc(rows.sem, 1)

        @block.scalar
        def _(act):
            act.wait_ge(*var.at(2))
            nc.scalar.activation(sd, mv[:, :, 1], ACT.Sqrt, bias=k.eps[:, 0:1]).then_inc(root.sem, 1)
            act.wait_ge(*turned.at(1))
            for c, r in enumerate(depth):
                nc.scalar.activation(k.ctx2T[0:r, c, :], k.ps[0:r, c, 0:B * M], ACT.Identity, bias=k.v(b, c)[0:r],
                                     scale=k.v(w, c)[0:r]).then_inc(out.sem, 1)

        @block.tensor
        def _(pe):
            pe.wait_ge(*rows.at(2))
            for c, r in enumerate(depth):
                for t in range(2):
                    last = nc.tensor.transpose(k.ps[0:r, c, t * P:(t + 1) * P], xn[:, t, c * P:c * P + r], k.ident[:, :])
            last.then_inc(turned.sem, 1)
    for s, n in ((loaded, 16), (stats, 2), (var, 2), (root, 1), (rstd, 1), (rows, 2), (turned, 1), (out, 2)):
        s.passed(n)
    k.end_stage()


def project_wide(k, next_weights, wq, wk, wv, context):
    nc = k.nc
    product, turned, joined = k.semaphore("product"), k.semaphore("rotated"), k.semaphore("joined")
    tables = k.semaphore("tables_in")
    stored = [k.semaphore(f"parts_stored_{i}") for i in range(2)]
    v_product, v_read = k.semaphore("v_product"), k.semaphore("v_read")
    table = k.big1[:, 0:2 * N].rearrange("p (a t) -> p a t", a=2)
    terms = k.big1[:, 1024:1024 + 8 * N].rearrange("p (s a t) -> p s a t", s=2, a=4)
    both = k.big1[:, 5120:5120 + 4 * N].rearrange("p (s a t) -> p s a t", s=2, a=2)
    units = ([("k", p, 0) for p in range(4)] if context else [("k", p, b) for p in range(4) for b in range(B)]) \
        + [("q", p, b) for p in range(4) for b in range(B)]
    dmas = [8 if context and kind == "k" else 2 for kind, _, _ in units]
    before = [16 * sum(dmas[i] for i in range(u % 2, u, 2)) for u in range(len(units))]
    depth = (P, DC - P) if context else (P, P)
    if context:
        v = k.big2[0:M, 0:B * MID].rearrange("p (b h d) -> p b h d", b=B, d=WIDE)
        v_units = [(b, half) for b in range(B) for half in range(2)]
    else:
        v = k.big2[:, :].rearrange("p (b h i d) -> p b h i d", b=B, h=H, i=TB)
        v_units = [(t, half) for t in range(TILES) for half in range(2)]

    def width(kind):
        return B * M if context and kind == "k" else N

    def angles(a, kind):
        return table[:, a, 0:M].unsqueeze(1).broadcast_to([P, B, M]) if width(kind) < N else table[:, a, :]

    def cut(ap, kind):
        return ap[:, 0:B * M].rearrange("p (b t) -> p b t", b=B) if width(kind) < N else ap

    with nc.Block() as block:
        @block.sync
        def _(sp):
            for a in range(2):
                sp.dma_start(table[:, a, :], k.ins["rotary"][a]).then_inc(tables.sem, 16)
            k.load_weights(sp, next_weights)
            for u, (kind, p, b) in enumerate(units):
                sp.wait_ge(*joined.at(2 * u + 2))
                for a in range(2):
                    rows = slice(a * WIDE // 2, (a + 1) * WIDE // 2)
                    if width(kind) == N:
                        h = b * H + 4 * p
                        dst = (k.q_wide if kind == "q" else k.k_wide)[h:h + 4, rows, :]
                        sp.dma_start(dst, both[:, u % 2, a, :]).then_inc(stored[u % 2].sem, 16)
                        continue
                    for bb in range(B):
                        h = bb * H + 4 * p
                        sp.dma_start(k.kx_wide[h:h + 4, rows, :], both[:, u % 2, a, bb * M:(bb + 1) * M]).then_inc(stored[u % 2].sem, 16)
            for s in range(2):
                sp.wait_ge(*stored[s].at(16 * sum(dmas[s::2])))

        @block.tensor
        def _(pe):
            pe.wait_ge(*k.weights_due())
            for u, (kind, p, b) in enumerate(units):
                if u >= 3:
                    pe.wait_ge(*turned.at(4 * (u - 2)))
                wt = k.where[wq if kind == "q" else wk]
                for a in range(2):
                    for c in range(C):
                        cols = slice((2 * p + a) * P, (2 * p + a + 1) * P)
                        if context and kind == "k":
                            r = depth[c]
                            lhs, rhs = wt[0:r, c, cols], k.ctx2T[0:r, c, :]
                        else:
                            lhs, rhs = wt[:, c, cols], k.hT[:, c, b * N:(b + 1) * N]
                        last = nc.tensor.matmul(k.ps[:, 2 * (u % 3) + a, 0:width(kind)], lhs, rhs, start=c == 0, stop=c == C - 1)
                last.then_inc(product.sem, 1)
            for u, (t, half) in enumerate(v_units):
                if u >= 2:
                    pe.wait_ge(*v_read.at(u - 1))
                for c in range(C):
                    r = depth[c]
                    lhs = k.ctx2T[0:r, c, t * M:(t + 1) * M] if context else k.hT[:, c, t * P:(t + 1) * P]
                    last = nc.tensor.matmul(k.ps[0:M if context else P, 6 + u % 2, :], lhs,
                                            k.where[wv][0:r, c, half * 512:(half + 1) * 512], start=c == 0, stop=c == C - 1)
                last.then_inc(v_product.sem, 1)

        @block.vector
        def _(dve):
            dve.wait_ge(*tables.at(32))
            for u, (kind, p, b) in enumerate(units):
                dve.wait_ge(*product.at(u + 1))
                if u >= 2:
                    dve.wait_ge(*joined.at(2 * (u - 1)))
                for i, (a, f) in enumerate(((0, 0), (1, 1), (0, 1), (1, 0))):
                    nc.vector.tensor_tensor(cut(terms[:, u % 2, i, :], kind), cut(k.ps[:, 2 * (u % 3) + a, :], kind),
                                            angles(f, kind), ALU.mult).then_inc(turned.sem, 1)

        @block.gpsimd
        def _(pool):
            for u, (kind, p, b) in enumerate(units):
                w = slice(0, width(kind))
                pool.wait_ge(*turned.at(4 * u + 4))
                if u >= 2:
                    pool.wait_ge(*stored[u % 2].at(before[u]))
                nc.gpsimd.tensor_tensor(both[:, u % 2, 0, w], terms[:, u % 2, 0, w], terms[:, u % 2, 1, w],
                                        ALU.subtract).then_inc(joined.sem, 1)
                nc.gpsimd.tensor_tensor(both[:, u % 2, 1, w], terms[:, u % 2, 2, w], terms[:, u % 2, 3, w],
                                        ALU.add).then_inc(joined.sem, 1)

        @block.scalar
        def _(act):
            for u, (t, half) in enumerate(v_units):
                act.wait_ge(*v_product.at(u + 1))
                src = k.ps[0:M if context else P, 6 + u % 2, :].rearrange("p (h d) -> p h d", d=WIDE)
                hs = slice(half * 8, half * 8 + 8)
                dst = v[:, t, hs, :] if context else v[:, t // TB, hs, t % TB, :]
                nc.scalar.activation(dst, src, ACT.Copy).then_inc(v_read.sem, 1)
    for s in range(2):
        stored[s].passed(16 * sum(dmas[s::2]))
    for s, n in ((product, len(units)), (turned, 4 * len(units)), (joined, 2 * len(units)), (tables, 32),
                 (v_product, len(v_units)), (v_read, len(v_units))):
        s.passed(n)
    k.end_stage()


def attend_wide(k, next_weights, context):
    nc = k.nc
    keys = M if context else N
    blocks, width = (1, M) if context else (TB, P)
    score_units, exp_units = (1, 1) if context else (TB, 2)
    k_dram = k.kx_wide if context else k.k_wide
    groups, slots = HEADS // 4, 4
    if context:
        v = k.big2[0:M, 0:B * MID].rearrange("p (n i d) -> p n i d", n=HEADS, i=1)
    else:
        v = k.big2[:, :].rearrange("p (n i d) -> p n i d", n=HEADS, i=TB)
    q_st = k.big1[0:WIDE + 1, 0:4096].rearrange("p (u h t) -> p u h t", u=2, h=4)
    k_st = k.big1[0:WIDE + 1, 4096:4096 + 8 * keys].rearrange("p (u h t) -> p u h t", u=2, h=4)
    probs = k.big1[:, 8192:8192 + slots * blocks * N].rearrange("p (s i t) -> p s i t", s=slots, i=blocks)
    spare = k.hT[:, :, :].rearrange("p c t -> p (c t)")
    v_st = spare[:, 0:slots * blocks * P].rearrange("p (s i d) -> p s i d", s=slots, i=blocks)
    o_sb = spare[0:WIDE, 2048:3072].rearrange("p (s t) -> p s t", s=2)
    inv = spare[0:WIDE, 3072:4096].rearrange("p (s t) -> p s t", s=2)
    neg_max = k.small[:, 0:8].rearrange("p (s a) -> p s a", s=2)
    max_parts = k.small[:, 8:16].bitcast(BF16).rearrange("p (s a c) -> p s a c", s=2, c=2)

    q_in, k_in = [k.semaphore(f"q_in_{u}") for u in range(2)], [k.semaphore(f"k_in_{u}") for u in range(2)]
    out_stored = [k.semaphore(f"out_stored_{u}") for u in range(2)]
    ones, v_in = k.semaphore("ones_made"), k.semaphore("v_staged")
    scores, maxed, max_split = k.semaphore("scores"), k.semaphore("maxed"), k.semaphore("max_split")
    max_turned, max_rows = k.semaphore("max_turned"), k.semaphore("max_rows")
    scores_t, exped, summed, inverted, o_out = k.semaphore("scores_t"), k.semaphore("exped"), k.semaphore("summed"), k.semaphore("inverse"), k.semaphore("o_out")

    with nc.Block() as block:
        @block.sync
        def _(sp):
            k.load_weights(sp, next_weights)

            def load(it, u):
                g = 2 * it + u
                if due(g - 1):
                    sp.wait_ge(*scores_t.at((g - 1) * 4 * exp_units))
                sp.dma_start(q_st[0:WIDE, u, :, :], k.q_wide[bass.ds(g * 4, 4)].rearrange("h d t -> d h t")).then_inc(q_in[u].sem, 16)
                sp.dma_start(k_st[0:WIDE, u, :, :], k_dram[bass.ds(g * 4, 4)].rearrange("h d t -> d h t")).then_inc(k_in[u].sem, 16)

            def store(it, j):
                n = 8 * it + j
                sp.wait_ge(*o_out.at(n + 1))
                sp.dma_start(k.o_wide[bass.ds(n, 1)].rearrange("h d t -> (h d) t"), o_sb[:, j % 2, :]).then_inc(out_stored[j % 2].sem, 16)

            def groups_of(it):
                for u in range(2):
                    load(it, u)
                    for j in range(4):
                        if due(8 * it + 4 * u + j - 7):
                            store(it - 1, 4 * u + j)

            load(0, 0)
            load(0, 1)
            groups_of(1)
            with sp.Fori(2, groups // 2) as it:
                groups_of(it)
            for j in range(8):
                store(groups // 2 - 1, j)
            for u in range(2):
                sp.wait_ge(*out_stored[u].at(16 * HEADS // 2))

        @block.gpsimd
        def _(pool):
            nc.gpsimd.memset(k_st[WIDE:WIDE + 1, :, :, :], 1.0).then_inc(ones.sem, 1)
            pool.wait_ge(*ones.at(1))
            nc.gpsimd.memset(v_st[:, :, :, WIDE:P], 1.0).then_inc(ones.sem, 1)

            def stage(it, j):
                n = 8 * it + j
                if due(n - slots + 1):
                    pool.wait_ge(*summed.at(n - slots + 1))
                nc.gpsimd.tensor_copy(v_st[0:width, j % slots, :, 0:WIDE],
                                      v[0:width, bass.ds(n, 1), :, :].rearrange("p n i d -> p (n i) d")).then_inc(v_in.sem, 1)

            for j in range(8):
                stage(0, j)
            with pool.Fori(1, groups // 2) as it:
                for j in range(8):
                    stage(it, j)

        @block.tensor
        def _(pe):
            def score(it, j):
                n, u, h = 8 * it + j, j // 4, j % 4
                if h == 0:
                    pe.wait_ge(*q_in[u].at(16 * it + 16))
                    pe.wait_ge(*k_in[u].at(16 * it + 16))
                for i in range(score_units):
                    m = n * score_units + i
                    if due(m - 1):
                        pe.wait_ge(*maxed.at(m - 1))
                    if context:
                        for a in range(TB):
                            last = nc.tensor.matmul(k.ps[:, j % 2, a * M:(a + 1) * M], q_st[0:WIDE, u, h, a * P:(a + 1) * P],
                                                    k_st[0:WIDE, u, h, :], start=True, stop=True)
                        last.then_inc(scores.sem, 1)
                    else:
                        nc.tensor.matmul(k.ps[:, i % 2, :], q_st[0:WIDE, u, h, i * P:(i + 1) * P], k_st[0:WIDE, u, h, :],
                                         start=True, stop=True).then_inc(scores.sem, 1)

            def score_t(it, j):
                n = 8 * it + j - 1
                u, h = (j - 1) // 4 % 2, (j - 1) % 4
                pe.wait_ge(*max_split.at(2 * n + 2))
                if due(n):
                    pe.wait_ge(*max_rows.at(n))
                for a in range(TB):
                    for c in range(2):
                        last = nc.tensor.matmul(k.ps[WIDE:WIDE + 1, 7, a * P:(a + 1) * P], max_parts[:, (j - 1) % 2, a, c:c + 1],
                                                k.identb[:, :], start=c == 0, stop=c == 1)
                last.then_inc(max_turned.sem, 1)
                pe.wait_ge(*max_rows.at(n + 1))
                for e in range(exp_units):
                    m = n * exp_units + e
                    if due(m - 1):
                        pe.wait_ge(*exped.at(m - 1))
                    if context:
                        last = nc.tensor.matmul(k.ps[0:M, 2 + (j - 1) % 2, :], k_st[:, u, h, :], q_st[:, u, h, :],
                                                start=True, stop=True)
                    else:
                        for i in (2 * e, 2 * e + 1):
                            last = nc.tensor.matmul(k.ps[:, 2 + i, :], k_st[:, u, h, i * P:(i + 1) * P], q_st[:, u, h, :],
                                                    start=True, stop=True)
                    last.then_inc(scores_t.sem, 1)

            def sum_up(it, j):
                n = 8 * it + j - 2
                s = (j - 2) % slots
                pe.wait_ge(*exped.at((n + 1) * exp_units))
                pe.wait_ge(*v_in.at(n + 1))
                if due(n):
                    pe.wait_ge(*o_out.at(n))
                for i in range(blocks):
                    last = nc.tensor.matmul(k.ps[:, 6, :], v_st[0:width, s, i, :], probs[0:width, s, i, :],
                                            start=i == 0, stop=i == blocks - 1)
                last.then_inc(summed.sem, 1)

            def step(it, j):
                score(it, j)
                if due(8 * it + j):
                    score_t(it, j)
                if due(8 * it + j - 1):
                    sum_up(it, j)

            pe.wait_ge(*ones.at(2))
            for j in range(8):
                step(0, j)
            with pe.Fori(1, groups // 2) as it:
                for j in range(8):
                    step(it, j)
            score_t(groups // 2, 0)
            sum_up(groups // 2, 0)
            sum_up(groups // 2, 1)

        @block.vector
        def _(dve):
            def maxima(it, j):
                n, s = 8 * it + j, j % 2
                if due(n - 1):
                    dve.wait_ge(*max_split.at(2 * n - 2))
                    dve.wait_ge(*max_turned.at(n - 1))
                for i in range(score_units):
                    dve.wait_ge(*scores.at(n * score_units + i + 1))
                    if context:
                        nc.vector.tensor_reduce(neg_max[:, s, :], k.ps[:, s, 0:TB * M].rearrange("p (a m) -> p a m", a=TB),
                                                axis=AX.X, op=ALU.max, negate=True).then_inc(maxed.sem, 1)
                    else:
                        nc.vector.tensor_reduce(neg_max[:, s, i:i + 1], k.ps[:, i % 2, :], axis=AX.X, op=ALU.max,
                                                negate=True).then_inc(maxed.sem, 1)
                dve.wait_ge(*maxed.at((n + 1) * score_units))
                nc.vector.tensor_copy(max_parts[:, s, :, 0], neg_max[:, s, :]).then_inc(max_split.sem, 1)
                dve.wait_ge(*max_split.at(2 * n + 1))
                nc.vector.tensor_tensor(max_parts[:, s, :, 1], neg_max[:, s, :], max_parts[:, s, :, 0],
                                        ALU.subtract).then_inc(max_split.sem, 1)

            def divide(it, j):
                n, s = 8 * it + j - 3, (j - 3) % 2
                dve.wait_ge(*summed.at(n + 1))
                if due(n - 1):
                    dve.wait_ge(*o_out.at(n - 1))
                nc.vector.reciprocal(inv[:, s, :], k.ps[WIDE:P, 6, :]).then_inc(inverted.sem, 1)
                dve.wait_ge(*inverted.at(n + 1))
                if due(n - 1):
                    dve.wait_ge(*out_stored[s].at(64 * it + 8 * (j - 3 - s)))
                nc.vector.tensor_tensor(o_sb[:, s, :], k.ps[0:WIDE, 6, :], inv[:, s, :], ALU.mult).then_inc(o_out.sem, 1)

            def step(it, j):
                if due(8 * it + j - 2):
                    divide(it, j)
                maxima(it, j)

            for j in range(8):
                step(0, j)
            with dve.Fori(1, groups // 2) as it:
                for j in range(8):
                    step(it, j)
            for j in range(3):
                divide(groups // 2, j)

        @block.scalar
        def _(act):
            def exps(it, j):
                n = 8 * it + j - 1
                u, h, s = (j - 1) // 4 % 2, (j - 1) % 4, (j - 1) % slots
                act.wait_ge(*max_turned.at(n + 1))
                nc.scalar.activation(q_st[WIDE:WIDE + 1, u, h, :], k.ps[WIDE:WIDE + 1, 7, :], ACT.Copy).then_inc(max_rows.sem, 1)
                if due(n - slots + 1):
                    act.wait_ge(*summed.at(n - slots + 1))
                for e in range(exp_units):
                    act.wait_ge(*scores_t.at(n * exp_units + e + 1))
                    if context:
                        nc.scalar.activation(probs[0:M, s, 0, :], k.ps[0:M, 2 + (j - 1) % 2, :], ACT.Exp,
                                             scale=WIDE ** -0.5).then_inc(exped.sem, 1)
                    else:
                        nc.scalar.activation(probs[:, s, 2 * e:2 * e + 2, :], k.ps[:, 2 + 2 * e:4 + 2 * e, :], ACT.Exp,
                                             scale=WIDE ** -0.5).then_inc(exped.sem, 1)

            for j in range(1, 8):
                exps(0, j)
            with act.Fori(1, groups // 2) as it:
                for j in range(8):
                    exps(it, j)
            exps(groups // 2, 0)
    for s in (q_in + k_in):
        s.passed(8 * groups)
    for s in out_stored:
        s.passed(8 * HEADS)
    for s, n in ((ones, 2), (v_in, HEADS),
                 (scores, HEADS * score_units), (maxed, HEADS * score_units), (max_split, 2 * HEADS), (max_turned, HEADS),
                 (max_rows, HEADS), (scores_t, HEADS * exp_units), (exped, HEADS * exp_units), (summed, HEADS),
                 (inverted, HEADS), (o_out, HEADS)):
        s.passed(n)
    k.end_stage()


def stages():
    out = []

    def add(f, weights, *args):
        out.append((f, weights, args))

    def chunk(block, n):
        return MOD_AT[block] + 2 * n

    if "0" in BLOCKS:
        def norm0(i):
            add(normalise, [], chunk("L0", 2 * i - 2), chunk("L0", 2 * i - 1), f"L0_ln{i}_w", f"L0_ln{i}_b", 0)

        norm0(1)
        add(project_qkv, ["L0_Wqkv"], "L0_Wqkv", "L0_bqkv")
        add(attend, [], False)
        add(project_out, ["L0_Wos"], "L0_Wos", "L0_bos", None, False)
        norm0(2)
        add(project_cross, ["L0_Wq", "L0_Wk", "L0_Wv"], None, "L0_Wq", "L0_Wk", "L0_Wv", ("L0_bq", 0), ("L0_bk", 0), ("L0_bv", 0))
        add(attend, [], True)
        add(project_out, ["L0_Woc"], "L0_Woc", "L0_boc", None, False)
        norm0(3)
        add(feed_forward, ["L0_W1", "L0_W2"], "L0_W1", None, "L0_W2", "L0_b1", "L0_b2", ACT.Gelu, None)
    if "1" in BLOCKS:
        def norm1(i):
            add(normalise, [], chunk("L1", 2 * i - 1), chunk("L1", 2 * i - 2), f"L1_ln{i}_w", f"L1_ln{i}_b", 0)

        norm1(1)
        add(project_wide, ["L1_sa_wq", "L1_sa_wk", "L1_sa_wv"], "L1_sa_wq", "L1_sa_wk", "L1_sa_wv", False)
        add(attend_wide, [], False)
        add(project_out, ["L1_sa_wo"], "L1_sa_wo", "L1_sa_bo", None, True)
        norm1(1)
        add(normalise_context, [], "L1_ca_lnc_w", "L1_ca_lnc_b")
        add(project_wide, ["L1_ca_wq", "L1_ca_wk", "L1_ca_wv"], "L1_ca_wq", "L1_ca_wk", "L1_ca_wv", True)
        add(attend_wide, [], True)
        add(project_out, ["L1_ca_wo"], "L1_ca_wo", "L1_ca_bo", None, True)
        norm1(2)
        add(feed_forward, ["L1_ff_w1", "L1_ff_w2"], "L1_ff_w1", None, "L1_ff_w2", "L1_ff_b1", "L1_ff_b2", ACT.Gelu, None)
    if "2" in BLOCKS:
        def norm2(i):
            add(normalise, [], chunk("L2", 2 * i - 2), chunk("L2", 2 * i - 1), None, None, 1)

        norm2(1)
        add(project_qkv, ["L2_W_qkv"], "L2_W_qkv", "L2_b_qkv")
        add(attend, [], False)
        add(project_out, ["L2_W_proj"], "L2_W_proj", "L2_b_proj", None, False)
        norm2(2)
        add(project_cross, ["L2_W_ctx", "L2_W_q", "L2_W_k", "L2_W_v"], ("L2_W_ctx", "L2_b_ctx"), "L2_W_q", "L2_W_k", "L2_W_v",
            None, None, None)
        add(attend, [], True)
        add(project_out, ["L2_W_out"], "L2_W_out", "L2_b_out", None, False)
        norm2(3)
        add(feed_forward, ["L2_W_fc1", "L2_W_fc2"], "L2_W_fc1", None, "L2_W_fc2", "L2_b_fc1", "L2_b_fc2", ACT.Gelu_apprx_tanh, None)
    if "3" in BLOCKS:
        add(normalise_heads, [], chunk("L3", 0), chunk("L3", 1), 1)
        add(attend, [], False)
        add(project_out, [], None, None, chunk("L3", 2), False)
        add(normalise, [], chunk("L3", 3), chunk("L3", 4), None, None, 1)
        add(project_cross, ["L3_cond_w", "L3_ca_q", "L3_ca_k", "L3_ca_v"], ("L3_cond_w", "L3_cond_b"), "L3_ca_q", "L3_ca_k", "L3_ca_v",
            ("L3_ca_in_b", 0), ("L3_ca_in_b", 2), ("L3_ca_in_b", 4))
        add(attend, [], True)
        add(project_out, ["L3_ca_out_w"], "L3_ca_out_w", "L3_ca_out_b", chunk("L3", 5), False)
        add(normalise, [], chunk("L3", 6), chunk("L3", 7), None, None, 1)
        add(feed_forward, ["L3_w1", "L3_w3", "L3_w2"], "L3_w1", "L3_w3", "L3_w2", None, None, ACT.Silu, chunk("L3", 8))
    return out


def program(nc, ins, out):
    with ExitStack() as ctx:
        k = Chip(nc, ctx, ins, out)
        todo = stages()
        setup(k, todo[0][1])
        for i, (f, _, args) in enumerate(todo):
            f(k, todo[i + 1][1] if i + 1 < len(todo) else None, *args)


BLOCKS = "0123"


def kernel(**inputs):
    import concourse.bacc as _bacc
    from concourse.bass_utils import run_bass_kernel_spmd as _run

    a = {n.replace("_xcond", ""): np.asarray(v) for n, v in inputs.items()}
    a["L3_adaln_w"] = a["L3_adaln_w"].T
    order = np.arange(MID).reshape(4, 4, WIDE // 2, 2).transpose(0, 3, 1, 2).reshape(MID)
    mixed = np.arange(D).reshape(4, 4, NARROW).transpose(0, 2, 1).reshape(D)
    for n in ("L0_Wqkv", "L0_bqkv", "L2_W_qkv", "L2_b_qkv"):
        a[n] = a[n][..., np.concatenate([mixed, D + mixed, 2 * D + np.arange(D)])]
    for n in ("L0_Wq", "L0_bq", "L0_Wk", "L0_bk", "L2_W_q", "L2_W_k"):
        a[n] = a[n][..., mixed]
    wk, wv = a["L1_sa_wkv"][:, :MID], a["L1_sa_wkv"][:, MID:]
    a["L1_sa_wq"], a["L1_sa_wk"], a["L1_sa_wv"] = a["L1_sa_wq"][:, order], wk[:, order], wv
    wk, wv = a["L1_ca_wkv"][:, :MID], a["L1_ca_wkv"][:, MID:]
    a["L1_ca_wq"], a["L1_ca_wk"], a["L1_ca_wv"] = a["L1_ca_wq"][:, order], wk[:, order], wv
    a["L3_ca_q"], a["L3_ca_k"], a["L3_ca_v"] = (a["L3_ca_in_w"][i * D:(i + 1) * D].T for i in range(3))
    a["L3_ca_q"], a["L3_ca_k"] = a["L3_ca_q"][:, mixed], a["L3_ca_k"][:, mixed]
    a["L3_ca_in_b"] = a["L3_ca_in_b"][np.concatenate([mixed, D + mixed, 2 * D + np.arange(D)])]
    for n in ("L3_cond_w", "L3_ca_out_w", "L3_w1", "L3_w3", "L3_w2"):
        a[n] = a[n].T
    for n in ("L1_ca_lnc_w", "L1_ca_lnc_b"):
        a[n] = np.concatenate([a[n], np.zeros(2 * P - DC, np.float32)])
    for n in ("L3_qn_w", "L3_qn_b", "L3_kn_w", "L3_kn_b"):
        a[n] = np.tile(np.repeat(a[n], 4), 2)
    arrays = {n: a[n] for n in WEIGHTS}
    arrays["vectors"] = np.concatenate([a[n].reshape(c, P) for n, c in VECTORS]).T
    arrays["mods"] = np.concatenate([a[n] for n, _ in MODS], axis=1)
    arrays["x"] = a["x"].reshape(T, D)
    arrays["ctx"] = a["ctx_768"].reshape(B * M, DC)
    arrays["condT"] = a["cond_1024"].T
    inv = (1.0 / 10000.0 ** (np.arange(0, WIDE, 2, dtype=np.float32) / np.float32(WIDE))).astype(np.float32)
    angle = np.arange(N, dtype=np.float32)[None, :] * inv[:, None]
    arrays["rotary"] = np.concatenate([np.stack([np.cos(angle), np.sin(angle)])] * 4, axis=1).astype(np.float32)

    nc = _bacc.Bacc("TRN2", target_bir_lowering=False, num_devices=1)
    ins = {}
    for n in arrays:
        arrays[n] = np.ascontiguousarray(arrays[n])
        ins[n] = nc.dram_tensor(f"in_{n}", arrays[n].shape, mybir.dt.from_np(arrays[n].dtype), kind="ExternalInput").ap()
    out = nc.dram_tensor("out_0", (B, N, D), F32, kind="ExternalOutput").ap()
    program(nc, ins, out)
    r = _run(nc, [{f"in_{n}": v for n, v in arrays.items()}], core_ids=[0])
    return r.results[0]["out_0"]
```

```python
from contextlib import ExitStack

import concourse.bass as bass
from concourse import mybir
import numpy as np

F32 = mybir.dt.float32
BF16 = mybir.dt.bfloat16
ACT = mybir.ActivationFunctionType
ALU = mybir.AluOpType
AX = mybir.AxisListType

B, N, D, H = 4, 512, 256, 16
M, DC = 64, 192
T = B * N
P = 128
TILES = T // P
TB = N // P
C = D // P
FF = 4 * D
FC = FF // P
HEADS = B * H
MID = 1024
WIDE = MID // H
NARROW = D // H

VECTORS = (
    [("L0_bmod", 12), ("L1_g1_b", 2), ("L1_b1_b", 2), ("L1_g2_b", 2), ("L1_b2_b", 2), ("L2_b_ada", 12), ("L3_adaln_b", 18)]
    + [(f"L0_ln{i}_{v}", 2) for i in (1, 2, 3) for v in "wb"]
    + [(f"L1_ln{i}_{v}", 2) for i in (1, 2) for v in "wb"]
    + [("L0_bqkv", 6), ("L0_bos", 2), ("L0_bq", 2), ("L0_bk", 2), ("L0_bv", 2), ("L0_boc", 2), ("L0_b1", 8), ("L0_b2", 2)]
    + [("L1_sa_bo", 2), ("L1_ca_lnc_w", 2), ("L1_ca_lnc_b", 2), ("L1_ca_bo", 2), ("L1_ff_b1", 8), ("L1_ff_b2", 2)]
    + [("L2_b_qkv", 6), ("L2_b_proj", 2), ("L2_b_ctx", 2), ("L2_b_out", 2), ("L2_b_fc1", 8), ("L2_b_fc2", 2)]
    + [("L3_qn_w", 1), ("L3_qn_b", 1), ("L3_kn_w", 1), ("L3_kn_b", 1), ("L3_ca_in_b", 6), ("L3_ca_out_b", 2), ("L3_cond_b", 2)]
)
OFFSET = {}
for _name, _n in VECTORS:
    OFFSET[_name] = sum(n for k, n in VECTORS if k in OFFSET)
NVEC = sum(n for _, n in VECTORS)

MODS = [("L0_Wmod", 1536), ("L1_g1_w", 256), ("L1_b1_w", 256), ("L1_g2_w", 256), ("L1_b2_w", 256), ("L2_W_ada", 1536), ("L3_adaln_w", 2304)]
MOD_AT = {"L0": 0, "L1": 12, "L2": 20, "L3": 32}
NMOD = sum(n for _, n in MODS) // P

WEIGHTS = {
    "L0_Wqkv": (D, 3 * D), "L0_Wos": (D, D), "L0_Wq": (D, D), "L0_Wk": (DC, D), "L0_Wv": (DC, D), "L0_Woc": (D, D),
    "L0_W1": (D, FF), "L0_W2": (FF, D),
    "L1_sa_wq": (D, MID), "L1_sa_wk": (D, MID), "L1_sa_wv": (D, MID), "L1_sa_wo": (MID, D),
    "L1_ca_wq": (D, MID), "L1_ca_wk": (DC, MID), "L1_ca_wv": (DC, MID), "L1_ca_wo": (MID, D),
    "L1_ff_w1": (D, FF), "L1_ff_w2": (FF, D),
    "L2_W_qkv": (D, 3 * D), "L2_W_proj": (D, D), "L2_W_ctx": (DC, D), "L2_W_q": (D, D), "L2_W_k": (D, D), "L2_W_v": (D, D),
    "L2_W_out": (D, D), "L2_W_fc1": (D, FF), "L2_W_fc2": (FF, D),
    "L3_cond_w": (DC, D), "L3_ca_q": (D, D), "L3_ca_k": (D, D), "L3_ca_v": (D, D), "L3_ca_out_w": (D, D),
    "L3_w1": (D, FF), "L3_w3": (D, FF), "L3_w2": (FF, D),
}


class Counted:

    def __init__(self, sem):
        self.sem, self.base = sem, 0

    def at(self, n):
        return self.sem, self.base + n

    def passed(self, n):
        self.base += n


class Chip:

    def __init__(self, nc, ctx, ins, out):
        self.nc, self.ins, self.out = nc, ins, out
        self._ctx, self._named = ctx, {}

        def sb(name, shape, dt=F32):
            return ctx.enter_context(nc.sbuf_tensor(name, shape, dt))

        self.x = sb("x", [P, TILES, D])
        self.hT = sb("hT", [P, C, T])
        self.w = [sb(f"w{i}", [P, 2048]) for i in range(4)]
        self.big1 = sb("big1", [P, 16384])
        self.big2 = sb("big2", [P, 16384])
        self.ident = sb("ident", [P, P])
        self.identb = sb("identb", [P, P], BF16)
        self.vec = sb("vec", [P, NVEC])
        self.mod = sb("mod", [P, NMOD, B])
        self.scale = sb("scale", [P, C, B])
        self.shift = sb("shift", [P, C, B])
        self.ctxT = sb("ctxT", [P, 2, B * M])
        self.ctx2T = sb("ctx2T", [P, 2, B * M])
        self.rows = sb("rows", [P, 4, D])
        self.small = sb("small", [P, 512])
        self.eps = sb("eps", [P, 2])
        self.ps = ctx.enter_context(nc.psum_tensor("ps", [P, 8, 512], F32))

        def dram(name, shape, dt):
            return nc.dram_tensor(name, shape, dt, kind="Internal").ap()

        self.q_parts = dram("q_parts", [HEADS // 4, 3, 4 * NARROW, N], BF16)
        self.k_parts = dram("k_parts", [HEADS // 4, 3, 4 * NARROW, N], BF16)
        self.kx_parts = dram("kx_parts", [HEADS // 4, 3, 4 * NARROW, M], BF16)
        self.q_wide = dram("q_wide", [HEADS, WIDE, N], F32)
        self.k_wide = dram("k_wide", [HEADS, WIDE, N], F32)
        self.kx_wide = dram("kx_wide", [HEADS, WIDE, M], F32)
        self.o_sums = dram("o_sums", [HEADS, 2 * NARROW, N], F32)
        self.o_wide = dram("o_wide", [HEADS, WIDE + 1, N], F32)
        self.w_turn = 0
        self.where = {}
        self.weights_in = [self.semaphore("weights_in_even"), self.semaphore("weights_in_odd")]
        self.stage, self.due, self.coming = 0, 0, 0

    def semaphore(self, name):
        if name not in self._named:
            self._named[name] = Counted(self._ctx.enter_context(self.nc.semaphore(name)))
        return self._named[name]

    def v(self, name, c=0, n=1):
        return self.vec[:, OFFSET[name] + c:OFFSET[name] + c + n]

    def load_weights(self, sp, names):
        sig = self.weights_in[(self.stage + 1) % 2]
        n = 0
        for name in names:
            rows, cols = WEIGHTS[name]
            slot = self.w[self.w_turn % 4]
            self.w_turn += 1
            src = self.ins[name]
            chunks = -(-rows // P)
            view = slot[:, 0:chunks * cols].rearrange("p (c n) -> p c n", c=chunks)
            self.where[name] = view
            whole = rows // P
            sp.dma_start(view[:, 0:whole, :], src[0:whole * P, :].rearrange("(c p) n -> p c n", p=P)).then_inc(sig.sem, 16)
            n += 16
            if rows % P:
                sp.dma_start(view[0:rows % P, whole, :], src[whole * P:rows, :]).then_inc(sig.sem, 16)
                n += 16
        self.coming = n

    def weights_due(self):
        return self.weights_in[self.stage % 2].at(self.due)

    def end_stage(self):
        self.weights_in[self.stage % 2].passed(self.due)
        self.stage += 1
        self.due, self.coming = self.coming, 0


def setup(k, next_weights):
    nc = k.nc
    ins = k.ins
    loaded, mods_loaded = k.semaphore("inputs_loaded"), k.semaphore("mod_weights_loaded")
    made, masked, cond_ready = k.semaphore("constants_made"), k.semaphore("identity_ready"), k.semaphore("cond_ready")
    modded, done, trans = k.semaphore("mod_products"), k.semaphore("mod_done"), k.semaphore("ctx_transposed")
    wmod = k.big1[:, 0:C * NMOD * P].rearrange("p (c n) -> p c n", c=C)
    ctx_tok = k.big2[:, 0:2 * DC].rearrange("p (t d) -> p t d", t=2)
    condT = k.big2[:, 400:400 + C * B].rearrange("p (c b) -> p c b", c=C)
    siluT = k.big2[:, 416:416 + C * B].rearrange("p (c b) -> p c b", c=C)
    with nc.Block() as block:
        @block.sync
        def _(sp):
            sp.dma_start(k.vec[:, :], ins["vectors"]).then_inc(loaded.sem, 16)
            sp.dma_start(condT, ins["condT"].rearrange("(c p) b -> p c b", p=P)).then_inc(loaded.sem, 16)
            sp.dma_start(ctx_tok, ins["ctx"].rearrange("(t p) d -> p t d", p=P)).then_inc(loaded.sem, 16)
            for c in range(C):
                sp.dma_start(wmod[:, c, :], ins["mods"][c * P:(c + 1) * P, :]).then_inc(mods_loaded.sem, 16)
            sp.dma_start(k.x[:, :, :], ins["x"].rearrange("(t p) d -> p t d", p=P)).then_inc(loaded.sem, 16)
            k.load_weights(sp, next_weights)

        @block.gpsimd
        def _(pool):
            nc.gpsimd.memset(k.ident[:, :], 0.0).then_inc(made.sem, 1)
            nc.gpsimd.memset(k.identb[:, :], 0.0).then_inc(made.sem, 1)
            nc.gpsimd.memset(k.eps[:, 0:1], 1e-5).then_inc(made.sem, 1)
            nc.gpsimd.memset(k.eps[:, 1:2], 1e-6).then_inc(made.sem, 1)
            pool.wait_ge(*made.at(4))
            for m in (k.ident, k.identb):
                nc.gpsimd.affine_select(out=m[:, :], in_=m[:, :], compare_op=ALU.not_equal, fill=1.0, base=0,
                                        pattern=[[-1, P]], channel_multiplier=1).then_inc(masked.sem, 1)

        @block.scalar
        def _(act):
            act.wait_ge(*loaded.at(64))
            nc.scalar.activation(siluT, condT, ACT.Silu).then_inc(cond_ready.sem, 1)

        @block.tensor
        def _(pe):
            pe.wait_ge(*masked.at(2))
            pe.wait_ge(*loaded.at(64))
            for t in range(2):
                nc.tensor.transpose(k.ps[:, 1, t * P:(t + 1) * P], ctx_tok[:, t, 0:P], k.ident[:, :])
                last = nc.tensor.transpose(k.ps[0:DC - P, 2, t * P:(t + 1) * P], ctx_tok[:, t, P:DC], k.ident[:, :])
            last.then_inc(trans.sem, 1)
            pe.wait_ge(*cond_ready.at(1))
            pe.wait_ge(*mods_loaded.at(32))
            for m in range(NMOD):
                src = condT if MOD_AT["L1"] <= m < MOD_AT["L2"] else siluT
                for c in range(C):
                    last = nc.tensor.matmul(k.ps[:, 0, m * B:(m + 1) * B], wmod[:, c, m * P:(m + 1) * P], src[:, c, :],
                                            start=c == 0, stop=c == C - 1)
            last.then_inc(modded.sem, 1)

        @block.vector
        def _(dve):
            dve.wait_ge(*trans.at(1))
            nc.vector.tensor_copy(k.ctxT[:, 0, :], k.ps[:, 1, 0:B * M])
            nc.vector.tensor_copy(k.ctxT[0:DC - P, 1, :], k.ps[0:DC - P, 2, 0:B * M])
            dve.wait_ge(*modded.at(1))
            nc.vector.tensor_tensor(k.mod[:, :, :], k.ps[:, 0, 0:NMOD * B].rearrange("p (m b) -> p m b", b=B),
                                    k.vec[:, 0:NMOD].unsqueeze(2).broadcast_to([P, NMOD, B]), ALU.add).then_inc(done.sem, 1)
    for s, n in ((loaded, 64), (mods_loaded, 32), (made, 4), (masked, 2), (cond_ready, 1), (modded, 1), (done, 1), (trans, 1)):
        s.passed(n)
    k.end_stage()


def normalise(k, next_weights, shift_at, scale_at, w, b, eps):
    nc = k.nc
    coef, stats, var = k.semaphore("coefficients"), k.semaphore("stats"), k.semaphore("variances")
    root, rstd, rows = k.semaphore("roots"), k.semaphore("rstd"), k.semaphore("normed_rows")
    turned, out = k.semaphore("transposed"), k.semaphore("modulated")
    st = k.small[:, 0:96].rearrange("p (t s) -> p t s", s=6)
    mv = k.small[:, 96:128].rearrange("p (t s) -> p t s", s=2)
    sd, rs = k.small[:, 128:144], k.small[:, 144:160]
    xn = k.big1[:, 0:2 * TB * D].rearrange("p (s t d) -> p s t d", s=2, t=TB)
    with nc.Block() as block:
        @block.sync
        def _(sp):
            k.load_weights(sp, next_weights)

        @block.vector
        def _(dve):
            g = k.mod[:, scale_at:scale_at + C, :]
            s = k.mod[:, shift_at:shift_at + C, :]
            if w is None:
                nc.vector.tensor_scalar(k.scale[:, :, :], g, 1.0, None, ALU.add).then_inc(coef.sem, 1)
                nc.vector.tensor_copy(k.shift[:, :, :], s).then_inc(coef.sem, 1)
            else:
                wv = k.v(w, 0, C).unsqueeze(2).broadcast_to([P, C, B])
                bv = k.v(b, 0, C).unsqueeze(2).broadcast_to([P, C, B])
                nc.vector.scalar_tensor_tensor(k.scale[:, :, :], g, 1.0, wv, ALU.add, ALU.mult).then_inc(coef.sem, 1)
                nc.vector.scalar_tensor_tensor(k.shift[:, :, :], g, 1.0, bv, ALU.add, ALU.mult).then_inc(coef.sem, 1)
                dve.wait_ge(*coef.at(2))
                nc.vector.tensor_tensor(k.shift[:, :, :], k.shift[:, :, :], s, ALU.add).then_inc(coef.sem, 1)
            for t in range(TILES):
                nc.vector.bn_stats(st[:, t, :], k.x[:, t, :]).then_inc(stats.sem, 1)
            for t in range(TILES):
                dve.wait_ge(*stats.at(t + 1))
                nc.vector.bn_aggr(mv[:, t, :], st[:, t, :]).then_inc(var.sem, 1)
            dve.wait_ge(*root.at(1))
            nc.vector.reciprocal(rs, sd).then_inc(rstd.sem, 1)
            dve.wait_ge(*rstd.at(1))
            for bb in range(B):
                if bb >= 2:
                    dve.wait_ge(*turned.at(bb - 1))
                for i in range(TB):
                    t = bb * TB + i
                    nc.vector.tensor_scalar(xn[:, bb % 2, i, :], k.x[:, t, :], mv[:, t, 0:1], rs[:, t:t + 1],
                                            ALU.subtract, ALU.mult).then_inc(rows.sem, 1)

        @block.scalar
        def _(act):
            act.wait_ge(*var.at(TILES))
            nc.scalar.activation(sd, mv[:, :, 1], ACT.Sqrt, bias=k.eps[:, eps:eps + 1]).then_inc(root.sem, 1)
            act.wait_ge(*coef.at(2 if w is None else 3))
            for bb in range(B):
                act.wait_ge(*turned.at(bb + 1))
                for c in range(C):
                    nc.scalar.activation(k.hT[:, c, bb * N:(bb + 1) * N], k.ps[:, 2 * (bb % 2) + c, :], ACT.Identity,
                                         bias=k.shift[:, c, bb:bb + 1], scale=k.scale[:, c, bb:bb + 1]).then_inc(out.sem, 1)

        @block.tensor
        def _(pe):
            for bb in range(B):
                pe.wait_ge(*rows.at((bb + 1) * TB))
                if bb >= 2:
                    pe.wait_ge(*out.at(C * (bb - 1)))
                for c in range(C):
                    for i in range(TB):
                        last = nc.tensor.transpose(k.ps[:, 2 * (bb % 2) + c, i * P:(i + 1) * P],
                                                   xn[:, bb % 2, i, c * P:(c + 1) * P], k.ident[:, :])
                last.then_inc(turned.sem, 1)
    for s, n in ((coef, 2 if w is None else 3), (stats, TILES), (var, TILES), (root, 1), (rstd, 1), (rows, TILES),
                 (turned, B), (out, B * C)):
        s.passed(n)
    k.end_stage()


def row_of(k, pe, out, columns):
    for c in range(C):
        last = k.nc.tensor.matmul(out[:, c * P:(c + 1) * P], columns[c].broadcast_to([P, P]), k.ident[:, :],
                                  start=True, stop=True)
    return last



def set_row(k, bank, columns):
    for c in range(C):
        last = k.nc.tensor.matmul(bank[:, c * P:(c + 1) * P], columns[c].broadcast_to([P, P]), k.ident[:, :],
                                  start=True, stop=True)
    return last


class Split:

    SLOTS = 3

    def __init__(self, k):
        n = self.SLOTS
        self.k = k
        self.whole_ready, self.first_ready = k.semaphore("whole_ready"), k.semaphore("part_1_ready")
        self.left_ready, self.second_ready = k.semaphore("remainder_ready"), k.semaphore("part_2_ready")
        self.third_ready = k.semaphore("part_3_ready")
        self.stored = [k.semaphore(f"parts_stored_{i}") for i in range(n)]
        self.stores = [0] * n
        self.before = []
        self.whole = k.big1[:, 0:n * 512].rearrange("p (s n) -> p s n", s=n)
        self.left = k.big1[:, n * 512:2 * n * 512].rearrange("p (s n) -> p s n", s=n)
        self.parts = k.big1[:, 2 * n * 512:2 * n * 512 + n * 768].bitcast(BF16).rearrange("p (s c n) -> p s c n", s=n, c=3)

    def plan(self, stores):
        for u, n in enumerate(stores):
            self.before.append(self.stores[u % self.SLOTS])
            self.stores[u % self.SLOTS] += 16 * n

    def act_whole(self, act, u, source, bias, width, scale=1.0):
        if u >= self.SLOTS:
            act.wait_ge(*self.third_ready.at(u - self.SLOTS + 1))
        self.k.nc.scalar.activation(self.whole[:, u % self.SLOTS, 0:width], source, ACT.Identity, bias=bias,
                                    scale=scale).then_inc(self.whole_ready.sem, 1)

    def act_first(self, act, u, width):
        act.wait_ge(*self.whole_ready.at(u + 1))
        if u >= self.SLOTS:
            act.wait_ge(*self.stored[u % self.SLOTS].at(self.before[u]))
        self.k.nc.scalar.activation(self.parts[:, u % self.SLOTS, 0, 0:width], self.whole[:, u % self.SLOTS, 0:width],
                                    ACT.Copy).then_inc(self.first_ready.sem, 1)

    def dve_rest(self, dve, u, width):
        vector = self.k.nc.vector
        s, w = u % self.SLOTS, slice(0, width)
        dve.wait_ge(*self.first_ready.at(u + 1))
        vector.tensor_tensor(self.left[:, s, w], self.whole[:, s, w], self.parts[:, s, 0, w],
                             ALU.subtract).then_inc(self.left_ready.sem, 1)
        dve.wait_ge(*self.left_ready.at(u + 1))
        vector.tensor_copy(self.parts[:, s, 1, w], self.left[:, s, w]).then_inc(self.second_ready.sem, 1)
        dve.wait_ge(*self.second_ready.at(u + 1))
        vector.tensor_tensor(self.parts[:, s, 2, w], self.left[:, s, w], self.parts[:, s, 1, w],
                             ALU.subtract).then_inc(self.third_ready.sem, 1)

    def store(self, sp, u, dst, g):
        sp.wait_ge(*self.third_ready.at(u + 1))
        for half in range(2):
            sp.dma_start(dst[g + half].rearrange("c r t -> r c t"),
                         self.parts[64 * half:64 * half + 64, u % self.SLOTS, :, :]).then_inc(self.stored[u % self.SLOTS].sem, 16)

    def store_context(self, sp, u, m):
        sp.wait_ge(*self.third_ready.at(u + 1))
        by_batch = self.k.kx_parts.rearrange("(b g) c r t -> b g c r t", b=B)
        for half in range(2):
            for c in range(3):
                src = self.parts[64 * half:64 * half + 64, u % self.SLOTS, c, 0:B * M].rearrange("r (b t) -> r b t", b=B)
                sp.dma_start(by_batch[:, m * 2 + half, c, :, :].rearrange("b r t -> r b t"),
                             src).then_inc(self.stored[u % self.SLOTS].sem, 16)

    def all_stored(self, sp):
        for s in range(self.SLOTS):
            sp.wait_ge(*self.stored[s].at(self.stores[s]))

    def passed(self):
        units = len(self.before)
        for s in (self.whole_ready, self.first_ready, self.left_ready, self.second_ready, self.third_ready):
            s.passed(units)
        for s in range(self.SLOTS):
            self.stored[s].passed(self.stores[s])


def v_narrow(k):
    return k.big2[:, 0:TILES * D].rearrange("p (b g i d) -> p b g i d", b=B, g=4, i=TB)


def vx_narrow(k):
    return k.big2[0:M, 0:B * D].rearrange("p (b g d) -> p b g d", b=B, g=4)


def project_qkv(k, next_weights, w, bias):
    nc = k.nc
    split = Split(k)
    product, v_product, v_read = k.semaphore("product"), k.semaphore("v_product"), k.semaphore("v_read")
    row_made, row_in = k.semaphore("row_made"), k.semaphore("row_in")
    units = [(m, b) for m in range(4) for b in range(B)]
    split.plan([2] * len(units))
    v = v_narrow(k)
    with nc.Block() as block:
        @block.sync
        def _(sp):
            k.load_weights(sp, next_weights)
            for u, (m, b) in enumerate(units):
                split.store(sp, u, (k.q_parts, k.k_parts)[m // 2], b * 4 + (m % 2) * 2)
            split.all_stored(sp)

        @block.tensor
        def _(pe):
            wt = k.where[w]
            pe.wait_ge(*k.weights_due())
            set_row(k, k.ps[:, 7, :], [k.v(bias, 4 + c) for c in range(C)]).then_inc(row_made.sem, 1)
            for u, (m, b) in enumerate(units):
                if u >= 4:
                    pe.wait_ge(*split.whole_ready.at(u - 3))
                for c in range(C):
                    last = nc.tensor.matmul(k.ps[:, u % 4, :], wt[:, c, m * P:(m + 1) * P], k.hT[:, c, b * N:(b + 1) * N],
                                            start=c == 0, stop=c == C - 1)
                last.then_inc(product.sem, 1)
            for t in range(TILES):
                if t >= 3:
                    pe.wait_ge(*v_read.at(t - 2))
                for c in range(C):
                    last = nc.tensor.matmul(k.ps[:, 4 + t % 3, 0:D], k.hT[:, c, t * P:(t + 1) * P], wt[:, c, 2 * D:3 * D],
                                            start=c == 0, stop=c == C - 1)
                last.then_inc(v_product.sem, 1)

        @block.scalar
        def _(act):
            for u, (m, b) in enumerate(units):
                act.wait_ge(*product.at(u + 1))
                split.act_whole(act, u, k.ps[:, u % 4, :], k.v(bias, m), N)
                split.act_first(act, u, N)

        @block.vector
        def _(dve):
            dve.wait_ge(*row_made.at(1))
            nc.vector.tensor_copy(k.rows[:, 0, :], k.ps[:, 7, 0:D]).then_inc(row_in.sem, 1)
            for u in range(len(units)):
                split.dve_rest(dve, u, N)
            dve.wait_ge(*row_in.at(1))
            for t in range(TILES):
                dve.wait_ge(*v_product.at(t + 1))
                nc.vector.tensor_tensor(v[:, t // TB, :, t % TB, :], k.ps[:, 4 + t % 3, 0:D].rearrange("p (g d) -> p g d", g=4),
                                        k.rows[:, 0, :].rearrange("p (g d) -> p g d", g=4), ALU.add).then_inc(v_read.sem, 1)
    for s, n in ((product, len(units)), (v_product, TILES), (v_read, TILES), (row_made, 1), (row_in, 1)):
        s.passed(n)
    split.passed()
    k.end_stage()


def due(n):
    return not isinstance(n, int) or n > 0


def attend(k, next_weights, context):
    nc = k.nc
    keys = M if context else N
    blocks, width = (1, M) if context else (TB, P)
    score_units, exp_units = (1, 1) if context else (TB, 2)
    groups = HEADS // 4
    turn, first = (4, 1) if context else (2, 2)
    heads, turns = 4 * turn, groups // turn
    rows, stack = 6 * NARROW, 6 * NARROW + 2
    block_at = {2: 0} if context else {2: 0, 3: 1, 0: 2, 1: 3}
    k_dram = k.kx_parts if context else k.k_parts
    v = vx_narrow(k).rearrange("p b g d -> p (b g) d").unsqueeze(2) if context else \
        v_narrow(k).rearrange("p b g i d -> p (b g) i d")

    q_st = k.big1[0:stack, 0:turn * 1024].bitcast(BF16).rearrange("p (u h t) -> p u h t", u=turn, h=4)
    k_st = k.big1[0:stack, 4096:4096 + 2 * turn * keys].bitcast(BF16).rearrange("p (u h t) -> p u h t", u=turn, h=4)
    probs = [z[:, 8192:8192 + 4 * blocks * N].rearrange("p (h i t) -> p h i t", h=4, i=blocks) for z in (k.big1, k.big2)]
    spare = k.hT[:, :, :].rearrange("p c t -> p (c t)")
    v_st = spare[:, 0:2 * blocks * P].rearrange("p (u i h d) -> p u i h d", u=2, i=blocks, h=4)
    o_sb = spare[:, 1024:2048].rearrange("p (u t) -> p u t", u=2)
    neg_max = k.small[:, 0:8].rearrange("p (s a) -> p s a", s=2)
    max_parts = k.small[:, 8:16].bitcast(BF16).rearrange("p (s a c) -> p s a c", s=2, c=2)

    q_in, k_in = [k.semaphore(f"q_in_{u}") for u in range(turn)], [k.semaphore(f"k_in_{u}") for u in range(turn)]
    out_stored = [k.semaphore(f"out_stored_{u}") for u in range(2)]
    ones, v_in = k.semaphore("ones_made"), k.semaphore("v_staged")
    scores, maxed, max_split = k.semaphore("scores"), k.semaphore("maxed"), k.semaphore("max_split")
    max_turned, max_rows = k.semaphore("max_turned"), k.semaphore("max_rows")
    scores_t, exped, summed, o_out = k.semaphore("scores_t"), k.semaphore("exped"), k.semaphore("summed"), k.semaphore("o_out")

    with nc.Block() as block:
        @block.sync
        def _(sp):
            def load(it, u):
                g = turn * it + u
                if due(g - turn + 1):
                    sp.wait_ge(*scores_t.at((g - turn + 1) * 4 * exp_units))
                for p0, parts in ((0, 3), (3, 2), (5, 1)):
                    sp.dma_start(q_st[p0 * NARROW:(p0 + parts) * NARROW, u, :, :],
                                 k.q_parts[bass.ds(g, 1), 0:parts].rearrange("g c (d h) t -> (g c d) h t", h=4)).then_inc(q_in[u].sem, 16)
                    src = k_dram[bass.ds(g, 1), (0, 3, 5).index(p0)].rearrange("g (d h) t -> g d (h t)", h=4)
                    sp.dma_start(k_st[p0 * NARROW:(p0 + parts) * NARROW, u, :, :].rearrange("p h t -> p (h t)"),
                                 src.broadcast_to([parts, NARROW, 4 * keys])).then_inc(k_in[u].sem, 16)

            def store(g, u):
                sp.wait_ge(*o_out.at(g + 1))
                sp.dma_start(k.o_sums[bass.ds(g * 4, 4)].rearrange("h r t -> (h r) t"), o_sb[:, u, :]).then_inc(out_stored[u].sem, 16)

            def groups_of(it):
                for u in range(turn):
                    load(it, u)
                    if due(turn * it + u - behind + 1):
                        store(turn * it + u - behind, (u - behind) % 2)

            behind = turn + 1
            for u in range(turn):
                load(0, u)
            k.load_weights(sp, next_weights)
            for it in range(1, first + 1):
                groups_of(it)
            with sp.Fori(first + 1, turns) as it:
                groups_of(it)
            for g in range(groups - behind, groups):
                store(g, g % 2)
            for u in range(2):
                sp.wait_ge(*out_stored[u].at(16 * (groups // 2)))

        @block.gpsimd
        def _(pool):
            nc.gpsimd.memset(k_st[rows:stack, :, :, :], 1.0).then_inc(ones.sem, 1)
            pool.wait_ge(*ones.at(1))
            nc.gpsimd.memset(v_st[:, :, :, :, NARROW:2 * NARROW], 1.0).then_inc(ones.sem, 1)

            def stage(it, u):
                g = turn * it + u
                if due(g - 1):
                    pool.wait_ge(*summed.at(g - 1))
                src = v[0:width, bass.ds(g, 1), :, :].rearrange("p g i (h d) -> p (g i) h d", h=4)
                nc.gpsimd.tensor_copy(v_st[0:width, u % 2, :, :, 0:NARROW], src).then_inc(v_in.sem, 1)

            for it in range(first):
                for u in range(turn):
                    stage(it, u)
            with pool.Fori(first, turns) as it:
                for u in range(turn):
                    stage(it, u)

        @block.tensor
        def _(pe):
            def score(it, j, i):
                u, h = j // 4, j % 4
                if h == 0 and i == 0:
                    pe.wait_ge(*q_in[u].at(48 * it + 48))
                    pe.wait_ge(*k_in[u].at(48 * it + 48))
                m = (heads * it + j) * score_units + i
                if due(m - 1):
                    pe.wait_ge(*maxed.at(m - 1))
                if context:
                    for a in range(TB):
                        last = nc.tensor.matmul(k.ps[:, j % 2, a * M:(a + 1) * M], q_st[0:rows, u, h, a * P:(a + 1) * P],
                                                k_st[0:rows, u, h, :], start=True, stop=True)
                    last.then_inc(scores.sem, 1)
                else:
                    nc.tensor.matmul(k.ps[:, i % 2, :], q_st[0:rows, u, h, i * P:(i + 1) * P], k_st[0:rows, u, h, :],
                                     start=True, stop=True).then_inc(scores.sem, 1)

            def turn_max(it, j):
                n = heads * it + j - 1
                pe.wait_ge(*max_split.at(2 * n + 2))
                if due(n):
                    pe.wait_ge(*max_rows.at(n))
                for a in range(TB):
                    last = nc.tensor.matmul(k.ps[rows:stack, 7, a * P:(a + 1) * P], max_parts[:, (j - 1) % 2, a, :],
                                            k.identb[:, :], start=True, stop=True)
                last.then_inc(max_turned.sem, 1)

            def score_t(it, j, e):
                n = heads * it + j - 2
                u, h = (j - 2) // 4 % turn, (j - 2) % 4
                if e == 0:
                    pe.wait_ge(*max_rows.at(n + 1))
                m = n * exp_units + e
                if due(m - 1):
                    pe.wait_ge(*exped.at(m - 1))
                if context:
                    last = nc.tensor.matmul(k.ps[0:M, 2 + j % 2, :], k_st[:, u, h, :], q_st[:, u, h, :],
                                            start=True, stop=True)
                else:
                    for i in (2 * e, 2 * e + 1):
                        last = nc.tensor.matmul(k.ps[:, 2 + i, :], k_st[:, u, h, i * P:(i + 1) * P], q_st[:, u, h, :],
                                                start=True, stop=True)
                last.then_inc(scores_t.sem, 1)

            def sum_ready(it, j):
                g = turn * it + j // 4 - 1
                if j % 4 == 2 and due(g + 1):
                    pe.wait_ge(*exped.at((g + 1) * 4 * exp_units))
                    pe.wait_ge(*v_in.at(g + 1))
                    if due(g):
                        pe.wait_ge(*o_out.at(g))

            def sum_up(it, j):
                back = 1 if j % 4 >= 2 else 2
                if j % 4 not in block_at or not due(turn * it + j // 4 - back + 1):
                    return
                i, s = block_at[j % 4], (j // 4 - back) % 2
                for h in range(4):
                    last = nc.tensor.matmul(k.ps[32 * h:32 * h + 32, 6, :], v_st[0:width, s, i, h, :],
                                            probs[s][0:width, h, i, :], start=i == 0, stop=i == blocks - 1)
                if i == blocks - 1:
                    last.then_inc(summed.sem, 1)

            def step(it, j):
                n = heads * it + j
                score(it, j, 0)
                if context:
                    sum_ready(it, j)
                    if due(n):
                        turn_max(it, j)
                if due(n - 1):
                    score_t(it, j, 0)
                if context:
                    sum_up(it, j)
                else:
                    score(it, j, 1)
                    sum_ready(it, j)
                    sum_up(it, j)
                    if due(n):
                        turn_max(it, j)
                    score(it, j, 2)
                    if due(n - 1):
                        score_t(it, j, 1)
                    score(it, j, 3)

            pe.wait_ge(*ones.at(2))
            for it in range(first):
                for j in range(heads):
                    step(it, j)
            with pe.Fori(first, turns) as it:
                for j in range(heads):
                    step(it, j)
            for j in range(2):
                if j == 0:
                    turn_max(turns, 0)
                for e in range(exp_units):
                    score_t(turns, j, e)
                sum_up(turns, j)
            for j in range(2, 4 if context else 6):
                sum_ready(turns, j)
                sum_up(turns, j)

        @block.vector
        def _(dve):
            def step(it, j):
                n, s = heads * it + j, j % 2
                if due(n - 1):
                    dve.wait_ge(*max_split.at(2 * n - 2))
                    dve.wait_ge(*max_turned.at(n - 1))
                for i in range(score_units):
                    dve.wait_ge(*scores.at(n * score_units + i + 1))
                    if context:
                        nc.vector.tensor_reduce(neg_max[:, s, :], k.ps[:, s, 0:TB * M].rearrange("p (a m) -> p a m", a=TB),
                                                axis=AX.X, op=ALU.max, negate=True).then_inc(maxed.sem, 1)
                    else:
                        nc.vector.tensor_reduce(neg_max[:, s, i:i + 1], k.ps[:, i % 2, :], axis=AX.X, op=ALU.max,
                                                negate=True).then_inc(maxed.sem, 1)
                dve.wait_ge(*maxed.at((n + 1) * score_units))
                nc.vector.tensor_copy(max_parts[:, s, :, 0], neg_max[:, s, :]).then_inc(max_split.sem, 1)
                dve.wait_ge(*max_split.at(2 * n + 1))
                nc.vector.tensor_tensor(max_parts[:, s, :, 1], neg_max[:, s, :], max_parts[:, s, :, 0],
                                        ALU.subtract).then_inc(max_split.sem, 1)

            for it in range(first):
                for j in range(heads):
                    step(it, j)
            with dve.Fori(first, turns) as it:
                for j in range(heads):
                    step(it, j)

        @block.scalar
        def _(act):
            def max_row(it, j):
                n = heads * it + j - 1
                u, h = (j - 1) // 4 % turn, (j - 1) % 4
                act.wait_ge(*max_turned.at(n + 1))
                nc.scalar.activation(q_st[rows:stack, u, h, :], k.ps[rows:stack, 7, :], ACT.Copy).then_inc(max_rows.sem, 1)

            def exps(it, j, e):
                n, g = heads * it + j - 2, turn * it + (j - 2) // 4
                u, h = (j - 2) // 4 % turn, (j - 2) % 4
                if h == 0 and e == 0 and due(g - 1):
                    act.wait_ge(*summed.at(g - 1))
                act.wait_ge(*scores_t.at(n * exp_units + e + 1))
                if context:
                    nc.scalar.activation(probs[u % 2][0:M, h, 0, :], k.ps[0:M, 2 + j % 2, :], ACT.Exp,
                                         scale=NARROW ** -0.5).then_inc(exped.sem, 1)
                else:
                    nc.scalar.activation(probs[u % 2][:, h, 2 * e:2 * e + 2, :], k.ps[:, 2 + 2 * e:4 + 2 * e, :], ACT.Exp,
                                         scale=NARROW ** -0.5).then_inc(exped.sem, 1)

            def out(it, u, back):
                g, s = turn * it + u - back, (u - back) % 2
                act.wait_ge(*summed.at(g + 1))
                if due(g - 1):
                    act.wait_ge(*out_stored[s].at(8 * (turn * it + u - back - s)))
                nc.scalar.activation(o_sb[:, s, :], k.ps[:, 6, :], ACT.Copy).then_inc(o_out.sem, 1)

            def outs(it, j):
                if context and j % 4 == 3 and due(turn * it + j // 4):
                    out(it, j // 4, 1)
                if not context and j % 4 == 2 and due(turn * it + j // 4 - 1):
                    out(it, j // 4, 2)

            def step(it, j):
                n = heads * it + j
                outs(it, j)
                if due(n - 1) and not context:
                    exps(it, j, 0)
                if due(n):
                    max_row(it, j)
                if due(n - 1):
                    exps(it, j, exp_units - 1)

            for it in range(first):
                for j in range(heads):
                    step(it, j)
            with act.Fori(first, turns) as it:
                for j in range(heads):
                    step(it, j)
            for j in range(2):
                if j == 0:
                    max_row(turns, j)
                for e in range(exp_units):
                    exps(turns, j, e)
            for j in range(2, 7):
                outs(turns, j)
    for s, n in (*((z, 48 * turns) for z in q_in + k_in), (out_stored[0], 8 * groups), (out_stored[1], 8 * groups), (ones, 2), (v_in, groups),
                 (scores, HEADS * score_units), (maxed, HEADS * score_units), (max_split, 2 * HEADS), (max_turned, HEADS),
                 (max_rows, HEADS), (scores_t, HEADS * exp_units), (exped, HEADS * exp_units), (summed, groups), (o_out, groups)):
        s.passed(n)
    k.end_stage()


def rows_at(k, n):
    return k.big2[:, 12288:12288 + n * D].rearrange("p (n d) -> p n d", n=n)


def chunks_beside(t, per_tile):
    b, i = t // TB + 1, t % TB
    return [(b, c) for c in range(int(i * per_tile), int((i + 1) * per_tile))] if b < B else []


def project_out(k, next_weights, w, bias, gate, wide):
    nc = k.nc
    chunks = MID // P if wide else C
    loaded = [k.semaphore(f"out_loaded_{b}") for b in range(B)]
    sums_in, inverse, spread, divided = k.semaphore("sums_loaded"), k.semaphore("inverse"), k.semaphore("inverse_spread"), k.semaphore("divided")
    row_made, row_in, row_scaled, biased = k.semaphore("row_made"), k.semaphore("row_in"), k.semaphore("row_scaled"), k.semaphore("biased")
    product, scaled, added = k.semaphore("product"), k.semaphore("scaled"), k.semaphore("added")
    o = k.big1[:, 0:chunks * T].rearrange("p (c t) -> p c t", c=chunks)
    sums = k.hT[0:HEADS, 0, 0:N]
    size = WIDE if wide else NARROW
    select = k.big2[0:HEADS, 4096:4096 + HEADS * size]
    select_made = k.semaphore("select_made")
    per_tile = chunks / TB
    gates, gated_bias = rows_at(k, 2 * B)[:, 0:B, :], rows_at(k, 2 * B)[:, B:2 * B, :]
    tmp = k.big2[:, 0:2 * D].rearrange("p (s d) -> p s d", s=2)
    bias_row = k.rows[:, 0, :]
    n_rows = (bias is not None) + (B if gate is not None else 0)
    with nc.Block() as block:
        @block.sync
        def _(sp):
            sp.dma_start(sums, (k.o_wide if wide else k.o_sums)[:, size, :]).then_inc(sums_in.sem, 16)
            for b in range(B):
                cols = slice(b * N, (b + 1) * N)
                for c in range(2):
                    if wide:
                        src = k.o_wide[b * H + c:(b + 1) * H:2, 0:WIDE, :].rearrange("h d t -> d h t")
                        sp.dma_start(o[c * WIDE:(c + 1) * WIDE, :, cols], src).then_inc(loaded[b].sem, 16)
                    else:
                        h = b * H + c * 8
                        sp.dma_start(o[:, c, cols], k.o_sums[h:h + 8, 0:NARROW, :]).then_inc(loaded[b].sem, 16)
            k.load_weights(sp, next_weights)

        @block.tensor
        def _(pe):
            pe.wait_ge(*k.weights_due()) if k.due else None
            n = 0
            if bias is not None:
                set_row(k, k.ps[:, 7, :], [k.v(bias, c) for c in range(C)]).then_inc(row_made.sem, 1)
                n += 1
            if gate is not None:
                for b in range(B):
                    if n:
                        pe.wait_ge(*row_in.at(n))
                    set_row(k, k.ps[:, 7, :], [k.mod[:, gate + c, b:b + 1] for c in range(C)]).then_inc(row_made.sem, 1)
                    n += 1
            wt = k.where[w] if w else None
            pe.wait_ge(*inverse.at(1))

            def spread_out(b, c):
                u = b * chunks + c
                if u >= 2:
                    pe.wait_ge(*divided.at(u - 1))
                h = b * H + c * (P // size)
                if c == 0:
                    pe.wait_ge(*select_made.at(b + 1))
                nc.tensor.matmul(k.ps[:, 4 + u % 2, :], select[:, h * size:h * size + P], sums, start=True, stop=True).then_inc(spread.sem, 1)

            for c in range(chunks):
                spread_out(0, c)
            for t in range(TILES):
                for b, c in chunks_beside(t, per_tile):
                    spread_out(b, c)
                if t % TB == 0:
                    pe.wait_ge(*divided.at(chunks * (t // TB + 1)))
                if t >= 4:
                    pe.wait_ge(*added.at(t - 3))
                for c in range(chunks):
                    if w:
                        last = nc.tensor.matmul(k.ps[:, t % 4, 0:D], o[:, c, t * P:(t + 1) * P], wt[:, c, :],
                                                start=c == 0, stop=c == chunks - 1)
                    else:
                        last = nc.tensor.transpose(k.ps[:, t % 4, c * P:(c + 1) * P], o[:, c, t * P:(t + 1) * P], k.ident[:, :])
                last.then_inc(product.sem, 1)

        @block.gpsimd
        def _(pool):
            if bias is None:
                return
            pool.wait_ge(*row_in.at(n_rows))
            for b in range(B):
                row = bias_row
                if gate is not None:
                    nc.gpsimd.tensor_tensor(gated_bias[:, b, :], gates[:, b, :], bias_row, ALU.mult).then_inc(row_scaled.sem, 1)
                    pool.wait_ge(*row_scaled.at(b + 1))
                    row = gated_bias[:, b, :]
                xb = k.x[:, b * TB:(b + 1) * TB, :]
                nc.gpsimd.tensor_tensor(xb, xb, row.unsqueeze(1).broadcast_to([P, TB, D]), ALU.add).then_inc(biased.sem, 1)

        @block.scalar
        def _(act):
            for b in range(B):
                nc.scalar.activation(select[:, b * H * size:(b + 1) * H * size].rearrange("p (h i) -> p h i", i=size),
                                     k.ident[0:HEADS, b * H:(b + 1) * H].unsqueeze(2).broadcast_to([HEADS, H, size]),
                                     ACT.Copy).then_inc(select_made.sem, 1)
            for r in range(n_rows):
                act.wait_ge(*row_made.at(r + 1))
                dst = bias_row if bias is not None and r == 0 else gates[:, r - (bias is not None), :]
                nc.scalar.activation(dst, k.ps[:, 7, 0:D], ACT.Copy).then_inc(row_in.sem, 1)

        @block.vector
        def _(dve):
            dve.wait_ge(*sums_in.at(16))
            nc.vector.reciprocal(sums, sums).then_inc(inverse.sem, 1)

            def divide(b, c):
                u, cols = b * chunks + c, slice(b * N, (b + 1) * N)
                if c == 0:
                    dve.wait_ge(*loaded[b].at(32))
                dve.wait_ge(*spread.at(u + 1))
                nc.vector.tensor_tensor(o[:, c, cols], o[:, c, cols], k.ps[:, 4 + u % 2, :], ALU.mult).then_inc(divided.sem, 1)

            for c in range(chunks):
                divide(0, c)
            if gate is not None:
                dve.wait_ge(*row_in.at(n_rows))
            for t in range(TILES):
                for b, c in chunks_beside(t, per_tile):
                    divide(b, c)
                if bias is not None and t % TB == 0:
                    dve.wait_ge(*biased.at(t // TB + 1))
                dve.wait_ge(*product.at(t + 1))
                src = k.ps[:, t % 4, 0:D]
                if gate is not None:
                    if t >= 2:
                        dve.wait_ge(*added.at(t - 1))
                    nc.vector.tensor_tensor(tmp[:, t % 2, :], src, gates[:, t // TB, :], ALU.mult).then_inc(scaled.sem, 1)
                    dve.wait_ge(*scaled.at(t + 1))
                    src = tmp[:, t % 2, :]
                nc.vector.tensor_tensor(k.x[:, t, :], src, k.x[:, t, :], ALU.add).then_inc(added.sem, 1)
    for b in range(B):
        loaded[b].passed(32)
    for s, n in ((sums_in, 16), (select_made, B), (inverse, 1), (spread, B * chunks), (divided, B * chunks), (row_made, n_rows), (row_in, n_rows),
                 (row_scaled, B if bias is not None and gate is not None else 0), (biased, B if bias is not None else 0),
                 (product, TILES), (scaled, TILES if gate is not None else 0), (added, TILES)):
        s.passed(n)
    k.end_stage()


def project_cross(k, next_weights, pre, wq, wk, wv, bq, bk, bv):
    nc = k.nc
    split = Split(k)
    product, v_product, v_read = k.semaphore("product"), k.semaphore("v_product"), k.semaphore("v_read")
    row_made, row_in, pre_made, pre_in = k.semaphore("row_made"), k.semaphore("row_in"), k.semaphore("pre_made"), k.semaphore("pre_in")
    units = [("k", m, 0) for m in range(C)] + [("q", m, b) for m in range(C) for b in range(B)]
    split.plan([6 if kind == "k" else 2 for kind, _, _ in units])
    source = k.ctx2T if pre else k.ctxT
    depth = [P, P] if pre else [P, DC - P]
    v = vx_narrow(k)

    def width(kind):
        return B * M if kind == "k" else N

    with nc.Block() as block:
        @block.sync
        def _(sp):
            k.load_weights(sp, next_weights)
            for u, (kind, m, b) in enumerate(units):
                if kind == "k":
                    split.store_context(sp, u, m)
                else:
                    split.store(sp, u, k.q_parts, b * 4 + m * 2)
            split.all_stored(sp)

        @block.tensor
        def _(pe):
            pe.wait_ge(*k.weights_due())
            if bv:
                set_row(k, k.ps[:, 7, :], [k.v(bv[0], bv[1] + c) for c in range(C)]).then_inc(row_made.sem, 1)
            if pre:
                wt = k.where[pre[0]]
                for m in range(C):
                    for c, r in enumerate((P, DC - P)):
                        last = nc.tensor.matmul(k.ps[:, 6, m * B * M:(m + 1) * B * M], wt[0:r, c, m * P:(m + 1) * P],
                                                k.ctxT[0:r, c, :], start=c == 0, stop=c == 1)
                last.then_inc(pre_made.sem, 1)
                pe.wait_ge(*pre_in.at(C))
            for u, (kind, m, b) in enumerate(units):
                if u >= 4:
                    pe.wait_ge(*split.whole_ready.at(u - 3))
                for c in range(C):
                    if kind == "k":
                        r = depth[c]
                        last = nc.tensor.matmul(k.ps[:, u % 4, 0:B * M], k.where[wk][0:r, c, m * P:(m + 1) * P], source[0:r, c, :],
                                                start=c == 0, stop=c == C - 1)
                    else:
                        last = nc.tensor.matmul(k.ps[:, u % 4, :], k.where[wq][:, c, m * P:(m + 1) * P],
                                                k.hT[:, c, b * N:(b + 1) * N], start=c == 0, stop=c == C - 1)
                last.then_inc(product.sem, 1)
            for b in range(B):
                if b >= 2:
                    pe.wait_ge(*v_read.at(b - 1))
                for c in range(C):
                    r = depth[c]
                    last = nc.tensor.matmul(k.ps[0:M, 4 + b % 2, 0:D], source[0:r, c, b * M:(b + 1) * M], k.where[wv][0:r, c, :],
                                            start=c == 0, stop=c == C - 1)
                last.then_inc(v_product.sem, 1)

        @block.scalar
        def _(act):
            if pre:
                act.wait_ge(*pre_made.at(1))
                for m in range(C):
                    nc.scalar.activation(k.ctx2T[:, m, :], k.ps[:, 6, m * B * M:(m + 1) * B * M], ACT.Identity,
                                         bias=k.v(pre[1], m)).then_inc(pre_in.sem, 1)
            for u, (kind, m, b) in enumerate(units):
                bias = bk if kind == "k" else bq
                act.wait_ge(*product.at(u + 1))
                split.act_whole(act, u, k.ps[:, u % 4, 0:width(kind)], k.v(bias[0], bias[1] + m) if bias else 0.0, width(kind))
                split.act_first(act, u, width(kind))

        @block.vector
        def _(dve):
            if bv:
                dve.wait_ge(*row_made.at(1))
                nc.vector.tensor_copy(k.rows[:, 0, :], k.ps[:, 7, 0:D]).then_inc(row_in.sem, 1)
            for u, (kind, _, _) in enumerate(units):
                split.dve_rest(dve, u, width(kind))
            if bv:
                dve.wait_ge(*row_in.at(1))
            for b in range(B):
                dve.wait_ge(*v_product.at(b + 1))
                src = k.ps[0:M, 4 + b % 2, 0:D].rearrange("p (g d) -> p g d", g=4)
                if bv:
                    nc.vector.tensor_tensor(v[:, b, :, :], src, k.rows[0:M, 0, :].rearrange("p (g d) -> p g d", g=4),
                                            ALU.add).then_inc(v_read.sem, 1)
                else:
                    nc.vector.tensor_copy(v[:, b, :, :], src).then_inc(v_read.sem, 1)
    for s, n in ((product, len(units)), (v_product, B), (v_read, B), (row_made, 1 if bv else 0), (row_in, 1 if bv else 0),
                 (pre_made, 1 if pre else 0), (pre_in, C if pre else 0)):
        s.passed(n)
    split.passed()
    k.end_stage()


def feed_forward(k, next_weights, up, gate_up, down, b_up, b_down, func, gate):
    nc = k.nc
    product, halved, hidden_ready = k.semaphore("product"), k.semaphore("activated"), k.semaphore("hidden")
    row_made, row_in, biased = k.semaphore("row_made"), k.semaphore("row_in"), k.semaphore("biased")
    down_product, scaled, added, final = k.semaphore("down_product"), k.semaphore("scaled"), k.semaphore("added"), k.semaphore("final_stored")
    hidden = k.big1[:, 0:2 * FC * N].rearrange("p (s m t) -> p s m t", s=2, m=FC)
    half = k.big1[:, 8192:8192 + 2 * N].rearrange("p (s t) -> p s t", s=2)
    gates = rows_at(k, B)
    tmp = k.big2[:, 0:2 * D].rearrange("p (s d) -> p s d", s=2)
    n_rows = (b_down is not None) + (B if gate is not None else 0)
    last_stage = next_weights is None
    with nc.Block() as block:
        @block.sync
        def _(sp):
            if not last_stage:
                k.load_weights(sp, next_weights)
                return
            out = k.out.rearrange("b (t p) d -> p (b t) d", p=P)
            for t in range(0, TILES, 2):
                sp.wait_ge(*added.at(t + 2))
                sp.dma_start(out[:, t:t + 2, :], k.x[:, t:t + 2, :]).then_inc(final.sem, 16)
            sp.wait_ge(*final.at(16 * TILES // 2))

        @block.tensor
        def _(pe):
            pe.wait_ge(*k.weights_due())
            n = 0
            if b_down is not None:
                set_row(k, k.ps[:, 7, :], [k.v(b_down, c) for c in range(C)]).then_inc(row_made.sem, 1)
                n += 1
            if gate is not None:
                for b in range(B):
                    if n:
                        pe.wait_ge(*row_in.at(n))
                    set_row(k, k.ps[:, 7, :], [k.mod[:, gate + c, b:b + 1] for c in range(C)]).then_inc(row_made.sem, 1)
                    n += 1

            def ups(b):
                for m in range(FC):
                    u = b * FC + m
                    if gate_up:
                        if u >= 2:
                            pe.wait_ge(*hidden_ready.at(u - 1))
                    elif u >= 4:
                        pe.wait_ge(*hidden_ready.at(u - 3))
                    for i, name in enumerate((up, gate_up) if gate_up else (up,)):
                        bank = 2 * (u % 2) + i if gate_up else u % 4
                        for c in range(C):
                            last = nc.tensor.matmul(k.ps[:, bank, :], k.where[name][:, c, m * P:(m + 1) * P],
                                                    k.hT[:, c, b * N:(b + 1) * N], start=c == 0, stop=c == C - 1)
                    last.then_inc(product.sem, 1)

            def downs(b):
                pe.wait_ge(*hidden_ready.at((b + 1) * FC))
                for i in range(TB):
                    t = b * TB + i
                    if t >= 2:
                        pe.wait_ge(*added.at(t - 1))
                    for m in range(FC):
                        last = nc.tensor.matmul(k.ps[:, 4 + t % 2, 0:D], hidden[:, b % 2, m, i * P:(i + 1) * P], k.where[down][:, m, :],
                                                start=m == 0, stop=m == FC - 1)
                    last.then_inc(down_product.sem, 1)

            for b in range(B):
                ups(b)
                if b:
                    downs(b - 1)
            downs(B - 1)

        @block.gpsimd
        def _(pool):
            if b_down is None:
                return
            pool.wait_ge(*row_in.at(1))
            for b in range(B):
                xb = k.x[:, b * TB:(b + 1) * TB, :]
                nc.gpsimd.tensor_tensor(xb, xb, k.rows[:, 0:1, :].broadcast_to([P, TB, D]), ALU.add).then_inc(biased.sem, 1)

        @block.scalar
        def _(act):
            for r in range(n_rows):
                act.wait_ge(*row_made.at(r + 1))
                dst = k.rows[:, 0, :] if b_down is not None and r == 0 else gates[:, r - (b_down is not None), :]
                nc.scalar.activation(dst, k.ps[:, 7, 0:D], ACT.Copy).then_inc(row_in.sem, 1)
            for b in range(B):
                if b >= 2:
                    act.wait_ge(*down_product.at((b - 1) * TB))
                for m in range(FC):
                    u = b * FC + m
                    act.wait_ge(*product.at(u + 1))
                    if gate_up:
                        if u >= 2:
                            act.wait_ge(*hidden_ready.at(u - 1))
                        nc.scalar.activation(half[:, u % 2, :], k.ps[:, 2 * (u % 2), :], func).then_inc(halved.sem, 1)
                    else:
                        nc.scalar.activation(hidden[:, b % 2, m, :], k.ps[:, u % 4, :], func,
                                             bias=k.v(b_up, m)).then_inc(hidden_ready.sem, 1)

        @block.vector
        def _(dve):
            def mix(b):
                for m in range(FC):
                    u = b * FC + m
                    dve.wait_ge(*halved.at(u + 1))
                    nc.vector.tensor_tensor(hidden[:, b % 2, m, :], k.ps[:, 2 * (u % 2) + 1, :], half[:, u % 2, :],
                                            ALU.mult).then_inc(hidden_ready.sem, 1)

            def add(b):
                for i in range(TB):
                    t = b * TB + i
                    if b_down is not None and i == 0:
                        dve.wait_ge(*biased.at(b + 1))
                    dve.wait_ge(*down_product.at(t + 1))
                    src = k.ps[:, 4 + t % 2, 0:D]
                    if gate is not None:
                        if t >= 2:
                            dve.wait_ge(*added.at(t - 1))
                        nc.vector.tensor_tensor(tmp[:, t % 2, :], src, gates[:, b, :], ALU.mult).then_inc(scaled.sem, 1)
                        dve.wait_ge(*scaled.at(t + 1))
                        src = tmp[:, t % 2, :]
                    nc.vector.tensor_tensor(k.x[:, t, :], src, k.x[:, t, :], ALU.add).then_inc(added.sem, 1)

            if gate is not None:
                dve.wait_ge(*row_in.at(n_rows))
            for b in range(B):
                if gate_up:
                    mix(b)
                if b:
                    add(b - 1)
            add(B - 1)
    for s, n in ((product, B * FC), (halved, B * FC if gate_up else 0), (hidden_ready, B * FC), (row_made, n_rows), (row_in, n_rows),
                 (biased, B if b_down is not None else 0), (down_product, TILES), (scaled, TILES if gate is not None else 0),
                 (added, TILES), (final, 8 * TILES if last_stage else 0)):
        s.passed(n)
    k.end_stage()


def normalise_heads(k, next_weights, shift_at, scale_at, eps):
    nc = k.nc
    split = Split(k)
    row_made, row_in = k.semaphore("row_made"), k.semaphore("row_in")
    stats, var, root, rstd, normed = k.semaphore("stats"), k.semaphore("variances"), k.semaphore("roots"), k.semaphore("rstd"), k.semaphore("normed_rows")
    h_scaled, h_ready, v_copied = k.semaphore("h_scaled"), k.semaphore("h_ready"), k.semaphore("v_copied")
    h_sum, h_mean, h_centred, h_squared = k.semaphore("h_sum"), k.semaphore("h_mean"), k.semaphore("h_centred"), k.semaphore("h_squared")
    h_var, h_root, h_rstd, h_normed, turned = k.semaphore("h_var"), k.semaphore("h_root"), k.semaphore("h_rstd"), k.semaphore("h_normed"), k.semaphore("transposed")
    st = k.small[:, 0:96].rearrange("p (t s) -> p t s", s=6)
    mv = k.small[:, 96:128].rearrange("p (t s) -> p t s", s=2)
    sd, rs = k.small[:, 128:144], k.small[:, 144:160]
    hs, hm, hv, hsd, hr = (k.small[:, 160 + 64 * i:224 + 64 * i] for i in range(5))
    xn = k.big1[:, 6144:7168].rearrange("p (i d) -> p i d", i=TB)
    h1 = k.big1[:, 7168:8192].rearrange("p (i d) -> p i d", i=TB)
    h = k.big1[:, 8192:10240].rearrange("p (s i d) -> p s i d", s=2, i=TB)
    hc = k.big1[:, 10240:11264]
    sq = k.big1[:, 11264:12288]
    hn = k.big1[:, 12288:14336].rearrange("p (s j) -> p s j", s=2)
    rows = rows_at(k, 2 * B)
    v = v_narrow(k)
    units = [(b, c, kind) for b in range(B) for c in range(C) for kind in range(2)]
    split.plan([2] * len(units))

    def per_head(flat):
        return flat.unsqueeze(2).broadcast_to([P, TB * H, NARROW])

    with nc.Block() as block:
        @block.sync
        def _(sp):
            k.load_weights(sp, next_weights)
            for u, (b, c, kind) in enumerate(units):
                split.store(sp, u, (k.q_parts, k.k_parts)[kind], b * 4 + c * 2)
            split.all_stored(sp)

        @block.tensor
        def _(pe):
            for r in range(2 * B):
                b, at = r // 2, (scale_at, shift_at)[r % 2]
                if r >= 2:
                    pe.wait_ge(*row_in.at(r - 1))
                set_row(k, k.ps[:, 6 + r % 2, :], [k.mod[:, at + c, b:b + 1] for c in range(C)]).then_inc(row_made.sem, 1)
            for b in range(B):
                pe.wait_ge(*h_normed.at(b + 1))
                if b >= 2:
                    pe.wait_ge(*split.whole_ready.at(4 * (b - 1)))
                for c in range(C):
                    for i in range(TB):
                        src = hn[:, b % 2, i * D + c * P:i * D + (c + 1) * P]
                        last = nc.tensor.transpose(k.ps[:, 2 * (b % 2) + c, i * P:(i + 1) * P], src, k.ident[:, :])
                last.then_inc(turned.sem, 1)

        @block.gpsimd
        def _(pool):
            for b in range(B):
                pool.wait_ge(*h_ready.at(b + 1))
                nc.gpsimd.tensor_copy(v[:, b].rearrange("p g i d -> p i g d"),
                                      h[:, b % 2].rearrange("p i (g d) -> p i g d", g=4)).then_inc(v_copied.sem, 1)

        @block.scalar
        def _(act):
            for r in range(2 * B):
                act.wait_ge(*row_made.at(r + 1))
                nc.scalar.activation(rows[:, r, :], k.ps[:, 6 + r % 2, 0:D], ACT.Identity, bias=1.0 if r % 2 == 0 else 0.0).then_inc(row_in.sem, 1)
            act.wait_ge(*var.at(TILES))
            nc.scalar.activation(sd, mv[:, :, 1], ACT.Sqrt, bias=k.eps[:, eps:eps + 1]).then_inc(root.sem, 1)

            def parts(b):
                act.wait_ge(*turned.at(b + 1))
                for u in range(4 * b, 4 * b + 4):
                    _, c, kind = units[u]
                    w, bias = (("L3_qn_w", "L3_qn_b"), ("L3_kn_w", "L3_kn_b"))[kind]
                    split.act_whole(act, u, k.ps[:, 2 * (b % 2) + c, :], k.v(bias), N, scale=k.v(w))
                    split.act_first(act, u, N)

            for b in range(B):
                act.wait_ge(*h_centred.at(b + 1))
                nc.scalar.activation(sq, hc, ACT.Square).then_inc(h_squared.sem, 1)
                act.wait_ge(*h_var.at(b + 1))
                nc.scalar.activation(hsd, hv, ACT.Sqrt, bias=k.eps[:, eps:eps + 1], scale=1.0 / NARROW).then_inc(h_root.sem, 1)
                if b:
                    parts(b - 1)
            parts(B - 1)

        @block.vector
        def _(dve):
            for t in range(TILES):
                nc.vector.bn_stats(st[:, t, :], k.x[:, t, :]).then_inc(stats.sem, 1)
            for t in range(TILES):
                dve.wait_ge(*stats.at(t + 1))
                nc.vector.bn_aggr(mv[:, t, :], st[:, t, :]).then_inc(var.sem, 1)
            dve.wait_ge(*root.at(1))
            nc.vector.reciprocal(rs, sd).then_inc(rstd.sem, 1)
            dve.wait_ge(*rstd.at(1))
            dve.wait_ge(*row_in.at(2 * B))
            for b in range(B):
                if b:
                    dve.wait_ge(*h_scaled.at(b))
                for i in range(TB):
                    t = b * TB + i
                    nc.vector.tensor_scalar(xn[:, i, :], k.x[:, t, :], mv[:, t, 0:1], rs[:, t:t + 1],
                                            ALU.subtract, ALU.mult).then_inc(normed.sem, 1)
                dve.wait_ge(*normed.at((b + 1) * TB))
                if b:
                    dve.wait_ge(*h_ready.at(b))
                nc.vector.tensor_tensor(h1, xn, rows[:, 2 * b:2 * b + 1, :].broadcast_to([P, TB, D]), ALU.mult).then_inc(h_scaled.sem, 1)
                dve.wait_ge(*h_scaled.at(b + 1))
                if b >= 2:
                    dve.wait_ge(*v_copied.at(b - 1))
                nc.vector.tensor_tensor(h[:, b % 2], h1, rows[:, 2 * b + 1:2 * b + 2, :].broadcast_to([P, TB, D]), ALU.add).then_inc(h_ready.sem, 1)
                dve.wait_ge(*h_ready.at(b + 1))
                heads = h[:, b % 2].rearrange("p i (h d) -> p (i h) d", d=NARROW)
                if b:
                    dve.wait_ge(*h_mean.at(b))
                nc.vector.tensor_reduce(hs, heads, axis=AX.X, op=ALU.add).then_inc(h_sum.sem, 1)
                dve.wait_ge(*h_sum.at(b + 1))
                if b:
                    dve.wait_ge(*h_centred.at(b))
                nc.vector.tensor_scalar(hm, hs, 1.0 / NARROW, None, ALU.mult).then_inc(h_mean.sem, 1)
                dve.wait_ge(*h_mean.at(b + 1))
                if b:
                    dve.wait_ge(*h_normed.at(b))
                nc.vector.tensor_tensor(hc.rearrange("p (j d) -> p j d", d=NARROW), heads, per_head(hm),
                                        ALU.subtract).then_inc(h_centred.sem, 1)
                dve.wait_ge(*h_squared.at(b + 1))
                if b:
                    dve.wait_ge(*h_root.at(b))
                nc.vector.tensor_reduce(hv, sq.rearrange("p (j d) -> p j d", d=NARROW), axis=AX.X, op=ALU.add).then_inc(h_var.sem, 1)
                dve.wait_ge(*h_root.at(b + 1))
                nc.vector.reciprocal(hr, hsd).then_inc(h_rstd.sem, 1)
                dve.wait_ge(*h_rstd.at(b + 1))
                if b >= 2:
                    dve.wait_ge(*turned.at(b - 1))
                nc.vector.tensor_tensor(hn[:, b % 2].rearrange("p (j d h) -> p j h d", h=4, d=NARROW),
                                        hc.rearrange("p (j h d) -> p j h d", h=4, d=NARROW),
                                        hr.rearrange("p (j h) -> p j h", h=4).unsqueeze(3).broadcast_to([P, TB * 4, 4, NARROW]),
                                        ALU.mult).then_inc(h_normed.sem, 1)
                if b:
                    for u in range(4 * b - 4, 4 * b):
                        split.dve_rest(dve, u, N)
            for u in range(4 * B - 4, 4 * B):
                split.dve_rest(dve, u, N)
    for s, n in ((row_made, 2 * B), (row_in, 2 * B), (stats, TILES), (var, TILES), (root, 1), (rstd, 1), (normed, TILES),
                 (h_scaled, B), (h_ready, B), (v_copied, B), (h_sum, B), (h_mean, B), (h_centred, B), (h_squared, B), (h_var, B),
                 (h_root, B), (h_rstd, B), (h_normed, B), (turned, B)):
        s.passed(n)
    split.passed()
    k.end_stage()


def normalise_context(k, next_weights, w, b):
    nc = k.nc
    loaded, stats, var, root, rstd = k.semaphore("context_loaded"), k.semaphore("stats"), k.semaphore("variances"), k.semaphore("roots"), k.semaphore("rstd")
    rows, turned, out = k.semaphore("normed_rows"), k.semaphore("transposed"), k.semaphore("modulated")
    tok = k.big2[:, 0:2 * DC].rearrange("p (t d) -> p t d", t=2)
    xn = k.big2[:, 512:512 + 2 * DC].rearrange("p (t d) -> p t d", t=2)
    st, mv = k.small[:, 0:12].rearrange("p (t s) -> p t s", s=6), k.small[:, 12:16].rearrange("p (t s) -> p t s", s=2)
    sd, rs = k.small[:, 16:18], k.small[:, 18:20]
    depth = (P, DC - P)
    with nc.Block() as block:
        @block.sync
        def _(sp):
            sp.dma_start(tok, k.ins["ctx"].rearrange("(t p) d -> p t d", p=P)).then_inc(loaded.sem, 16)
            k.load_weights(sp, next_weights)

        @block.vector
        def _(dve):
            dve.wait_ge(*loaded.at(16))
            for t in range(2):
                nc.vector.bn_stats(st[:, t, :], tok[:, t, :]).then_inc(stats.sem, 1)
            dve.wait_ge(*stats.at(2))
            for t in range(2):
                nc.vector.bn_aggr(mv[:, t, :], st[:, t, :]).then_inc(var.sem, 1)
            dve.wait_ge(*root.at(1))
            nc.vector.reciprocal(rs, sd).then_inc(rstd.sem, 1)
            dve.wait_ge(*rstd.at(1))
            for t in range(2):
                nc.vector.tensor_scalar(xn[:, t, :], tok[:, t, :], mv[:, t, 0:1], rs[:, t:t + 1],
                                        ALU.subtract, ALU.mult).then_inc(rows.sem, 1)

        @block.scalar
        def _(act):
            act.wait_ge(*var.at(2))
            nc.scalar.activation(sd, mv[:, :, 1], ACT.Sqrt, bias=k.eps[:, 0:1]).then_inc(root.sem, 1)
            act.wait_ge(*turned.at(1))
            for c, r in enumerate(depth):
                nc.scalar.activation(k.ctx2T[0:r, c, :], k.ps[0:r, c, 0:B * M], ACT.Identity, bias=k.v(b, c)[0:r],
                                     scale=k.v(w, c)[0:r]).then_inc(out.sem, 1)

        @block.tensor
        def _(pe):
            pe.wait_ge(*rows.at(2))
            for c, r in enumerate(depth):
                for t in range(2):
                    last = nc.tensor.transpose(k.ps[0:r, c, t * P:(t + 1) * P], xn[:, t, c * P:c * P + r], k.ident[:, :])
            last.then_inc(turned.sem, 1)
    for s, n in ((loaded, 16), (stats, 2), (var, 2), (root, 1), (rstd, 1), (rows, 2), (turned, 1), (out, 2)):
        s.passed(n)
    k.end_stage()


def project_wide(k, next_weights, wq, wk, wv, context):
    nc = k.nc
    product, turned, joined = k.semaphore("product"), k.semaphore("rotated"), k.semaphore("joined")
    tables = k.semaphore("tables_in")
    stored = [k.semaphore(f"parts_stored_{i}") for i in range(2)]
    v_product, v_read = k.semaphore("v_product"), k.semaphore("v_read")
    table = k.big1[:, 0:2 * N].rearrange("p (a t) -> p a t", a=2)
    terms = k.big1[:, 1024:1024 + 8 * N].rearrange("p (s a t) -> p s a t", s=2, a=4)
    both = k.big1[:, 5120:5120 + 4 * N].rearrange("p (s a t) -> p s a t", s=2, a=2)
    units = ([("k", p, 0) for p in range(4)] if context else [("k", p, b) for p in range(4) for b in range(B)]) \
        + [("q", p, b) for p in range(4) for b in range(B)]
    dmas = [8 if context and kind == "k" else 2 for kind, _, _ in units]
    before = [16 * sum(dmas[i] for i in range(u % 2, u, 2)) for u in range(len(units))]
    depth = (P, DC - P) if context else (P, P)
    if context:
        v = k.big2[0:M, 0:B * MID].rearrange("p (b h d) -> p b h d", b=B, d=WIDE)
        v_units = [(b, half) for b in range(B) for half in range(2)]
    else:
        v = k.big2[:, :].rearrange("p (b h i d) -> p b h i d", b=B, h=H, i=TB)
        v_units = [(t, half) for t in range(TILES) for half in range(2)]

    def width(kind):
        return B * M if context and kind == "k" else N

    def angles(a, kind):
        return table[:, a, 0:M].unsqueeze(1).broadcast_to([P, B, M]) if width(kind) < N else table[:, a, :]

    def cut(ap, kind):
        return ap[:, 0:B * M].rearrange("p (b t) -> p b t", b=B) if width(kind) < N else ap

    with nc.Block() as block:
        @block.sync
        def _(sp):
            for a in range(2):
                sp.dma_start(table[:, a, :], k.ins["rotary"][a]).then_inc(tables.sem, 16)
            k.load_weights(sp, next_weights)
            for u, (kind, p, b) in enumerate(units):
                sp.wait_ge(*joined.at(2 * u + 2))
                for a in range(2):
                    rows = slice(a * WIDE // 2, (a + 1) * WIDE // 2)
                    if width(kind) == N:
                        h = b * H + 4 * p
                        dst = (k.q_wide if kind == "q" else k.k_wide)[h:h + 4, rows, :]
                        sp.dma_start(dst, both[:, u % 2, a, :]).then_inc(stored[u % 2].sem, 16)
                        continue
                    for bb in range(B):
                        h = bb * H + 4 * p
                        sp.dma_start(k.kx_wide[h:h + 4, rows, :], both[:, u % 2, a, bb * M:(bb + 1) * M]).then_inc(stored[u % 2].sem, 16)
            for s in range(2):
                sp.wait_ge(*stored[s].at(16 * sum(dmas[s::2])))

        @block.tensor
        def _(pe):
            pe.wait_ge(*k.weights_due())
            for u, (kind, p, b) in enumerate(units):
                if u >= 3:
                    pe.wait_ge(*turned.at(4 * (u - 2)))
                wt = k.where[wq if kind == "q" else wk]
                for a in range(2):
                    for c in range(C):
                        cols = slice((2 * p + a) * P, (2 * p + a + 1) * P)
                        if context and kind == "k":
                            r = depth[c]
                            lhs, rhs = wt[0:r, c, cols], k.ctx2T[0:r, c, :]
                        else:
                            lhs, rhs = wt[:, c, cols], k.hT[:, c, b * N:(b + 1) * N]
                        last = nc.tensor.matmul(k.ps[:, 2 * (u % 3) + a, 0:width(kind)], lhs, rhs, start=c == 0, stop=c == C - 1)
                last.then_inc(product.sem, 1)
            for u, (t, half) in enumerate(v_units):
                if u >= 2:
                    pe.wait_ge(*v_read.at(u - 1))
                for c in range(C):
                    r = depth[c]
                    lhs = k.ctx2T[0:r, c, t * M:(t + 1) * M] if context else k.hT[:, c, t * P:(t + 1) * P]
                    last = nc.tensor.matmul(k.ps[0:M if context else P, 6 + u % 2, :], lhs,
                                            k.where[wv][0:r, c, half * 512:(half + 1) * 512], start=c == 0, stop=c == C - 1)
                last.then_inc(v_product.sem, 1)

        @block.vector
        def _(dve):
            dve.wait_ge(*tables.at(32))
            for u, (kind, p, b) in enumerate(units):
                dve.wait_ge(*product.at(u + 1))
                if u >= 2:
                    dve.wait_ge(*joined.at(2 * (u - 1)))
                for i, (a, f) in enumerate(((0, 0), (1, 1), (0, 1), (1, 0))):
                    nc.vector.tensor_tensor(cut(terms[:, u % 2, i, :], kind), cut(k.ps[:, 2 * (u % 3) + a, :], kind),
                                            angles(f, kind), ALU.mult).then_inc(turned.sem, 1)

        @block.gpsimd
        def _(pool):
            for u, (kind, p, b) in enumerate(units):
                w = slice(0, width(kind))
                pool.wait_ge(*turned.at(4 * u + 4))
                if u >= 2:
                    pool.wait_ge(*stored[u % 2].at(before[u]))
                nc.gpsimd.tensor_tensor(both[:, u % 2, 0, w], terms[:, u % 2, 0, w], terms[:, u % 2, 1, w],
                                        ALU.subtract).then_inc(joined.sem, 1)
                nc.gpsimd.tensor_tensor(both[:, u % 2, 1, w], terms[:, u % 2, 2, w], terms[:, u % 2, 3, w],
                                        ALU.add).then_inc(joined.sem, 1)

        @block.scalar
        def _(act):
            for u, (t, half) in enumerate(v_units):
                act.wait_ge(*v_product.at(u + 1))
                src = k.ps[0:M if context else P, 6 + u % 2, :].rearrange("p (h d) -> p h d", d=WIDE)
                hs = slice(half * 8, half * 8 + 8)
                dst = v[:, t, hs, :] if context else v[:, t // TB, hs, t % TB, :]
                nc.scalar.activation(dst, src, ACT.Copy).then_inc(v_read.sem, 1)
    for s in range(2):
        stored[s].passed(16 * sum(dmas[s::2]))
    for s, n in ((product, len(units)), (turned, 4 * len(units)), (joined, 2 * len(units)), (tables, 32),
                 (v_product, len(v_units)), (v_read, len(v_units))):
        s.passed(n)
    k.end_stage()


def attend_wide(k, next_weights, context):
    nc = k.nc
    keys = M if context else N
    blocks, width = (1, M) if context else (TB, P)
    score_units, exp_units = (1, 1) if context else (TB, 2)
    k_dram = k.kx_wide if context else k.k_wide
    groups, slots = HEADS // 4, 4
    turn = 4 if context else 2
    heads, turns = 4 * turn, groups // turn
    sum_bank = (4, 5) if context else (6, 6)
    if context:
        v = k.big2[0:M, 0:B * MID].rearrange("p (n i d) -> p n i d", n=HEADS, i=1)
    else:
        v = k.big2[:, :].rearrange("p (n i d) -> p n i d", n=HEADS, i=TB)
    q_words, k_words = turn * 4 * N, turn * 4 * keys
    q_st = k.big1[0:WIDE + 1, 0:q_words].rearrange("p (u h t) -> p u h t", u=turn, h=4)
    k_st = k.big1[0:WIDE + 1, q_words:q_words + k_words].rearrange("p (u h t) -> p u h t", u=turn, h=4)
    probs = k.big1[:, q_words + k_words:q_words + k_words + slots * blocks * N].rearrange("p (s i t) -> p s i t", s=slots, i=blocks)
    spare = k.hT[:, :, :].rearrange("p c t -> p (c t)")
    v_st = spare[:, 0:slots * blocks * P].rearrange("p (s i d) -> p s i d", s=slots, i=blocks)
    o_sb = spare[0:WIDE + 1, 2048:3072].rearrange("p (s t) -> p s t", s=2)
    neg_max = k.small[:, 0:8].rearrange("p (s a) -> p s a", s=2)
    max_parts = k.small[:, 8:16].bitcast(BF16).rearrange("p (s a c) -> p s a c", s=2, c=2)

    q_in, k_in = [k.semaphore(f"q_in_{u}") for u in range(turn)], [k.semaphore(f"k_in_{u}") for u in range(turn)]
    out_stored = [k.semaphore(f"out_stored_{u}") for u in range(2)]
    ones, v_in = k.semaphore("ones_made"), k.semaphore("v_staged")
    scores, maxed, max_split = k.semaphore("scores"), k.semaphore("maxed"), k.semaphore("max_split")
    max_turned, max_rows = k.semaphore("max_turned"), k.semaphore("max_rows")
    scores_t, exped, summed, o_out = k.semaphore("scores_t"), k.semaphore("exped"), k.semaphore("summed"), k.semaphore("o_out")

    with nc.Block() as block:
        @block.sync
        def _(sp):
            def load(it, u):
                g = turn * it + u
                if due(g - turn + 1):
                    sp.wait_ge(*scores_t.at((g - turn + 1) * 4 * exp_units))
                sp.dma_start(q_st[0:WIDE, u, :, :], k.q_wide[bass.ds(g * 4, 4)].rearrange("h d t -> d h t")).then_inc(q_in[u].sem, 16)
                sp.dma_start(k_st[0:WIDE, u, :, :], k_dram[bass.ds(g * 4, 4)].rearrange("h d t -> d h t")).then_inc(k_in[u].sem, 16)

            def store(n, s):
                sp.wait_ge(*o_out.at(n + 1))
                sp.dma_start(k.o_wide[bass.ds(n, 1)].rearrange("h d t -> (h d) t"), o_sb[:, s, :]).then_inc(out_stored[s].sem, 16)

            def groups_of(it):
                for u in range(turn):
                    load(it, u)
                    for h in range(4):
                        store(heads * (it - 1) + 4 * u + h, h % 2)

            for u in range(turn):
                load(0, u)
            k.load_weights(sp, next_weights)
            groups_of(1)
            with sp.Fori(2, turns) as it:
                groups_of(it)
            for n in range(heads):
                store(HEADS - heads + n, n % 2)
            for s in range(2):
                sp.wait_ge(*out_stored[s].at(16 * HEADS // 2))

        @block.gpsimd
        def _(pool):
            nc.gpsimd.memset(k_st[WIDE:WIDE + 1, :, :, :], 1.0).then_inc(ones.sem, 1)
            pool.wait_ge(*ones.at(1))
            nc.gpsimd.memset(v_st[:, :, :, WIDE:WIDE + 1], 1.0).then_inc(ones.sem, 1)

            def stage(it, j):
                n = heads * it + j
                if due(n - slots + 1):
                    pool.wait_ge(*summed.at(n - slots + 1))
                nc.gpsimd.tensor_copy(v_st[0:width, j % slots, :, 0:WIDE],
                                      v[0:width, bass.ds(n, 1), :, :].rearrange("p n i d -> p (n i) d")).then_inc(v_in.sem, 1)

            for j in range(heads):
                stage(0, j)
            with pool.Fori(1, turns) as it:
                for j in range(heads):
                    stage(it, j)

        @block.tensor
        def _(pe):
            def score(it, j, i):
                u, h = j // 4, j % 4
                if h == 0 and i == 0:
                    pe.wait_ge(*q_in[u].at(16 * it + 16))
                    pe.wait_ge(*k_in[u].at(16 * it + 16))
                m = (heads * it + j) * score_units + i
                if due(m - 1):
                    pe.wait_ge(*maxed.at(m - 1))
                if context:
                    for a in range(TB):
                        last = nc.tensor.matmul(k.ps[:, j % 2, a * M:(a + 1) * M], q_st[0:WIDE, u, h, a * P:(a + 1) * P],
                                                k_st[0:WIDE, u, h, :], start=True, stop=True)
                    last.then_inc(scores.sem, 1)
                else:
                    nc.tensor.matmul(k.ps[:, i % 2, :], q_st[0:WIDE, u, h, i * P:(i + 1) * P], k_st[0:WIDE, u, h, :],
                                     start=True, stop=True).then_inc(scores.sem, 1)

            def turn_max(it, j):
                n = heads * it + j - 1
                pe.wait_ge(*max_split.at(2 * n + 2))
                if due(n):
                    pe.wait_ge(*max_rows.at(n))
                for a in range(TB):
                    for c in range(2):
                        last = nc.tensor.matmul(k.ps[WIDE:WIDE + 1, 7, a * P:(a + 1) * P], max_parts[:, (j - 1) % 2, a, c:c + 1],
                                                k.identb[:, :], start=c == 0, stop=c == 1)
                last.then_inc(max_turned.sem, 1)

            def score_t(it, j, e):
                n = heads * it + j - 2
                u, h = (j - 2) // 4 % turn, (j - 2) % 4
                if e == 0:
                    pe.wait_ge(*max_rows.at(n + 1))
                m = n * exp_units + e
                if due(m - 1):
                    pe.wait_ge(*exped.at(m - 1))
                if context:
                    last = nc.tensor.matmul(k.ps[0:M, 2 + j % 2, :], k_st[:, u, h, :], q_st[:, u, h, :],
                                            start=True, stop=True)
                else:
                    for i in (2 * e, 2 * e + 1):
                        last = nc.tensor.matmul(k.ps[:, 2 + i, :], k_st[:, u, h, i * P:(i + 1) * P], q_st[:, u, h, :],
                                                start=True, stop=True)
                last.then_inc(scores_t.sem, 1)

            def sum_up(it, j, part):
                n = heads * it + j - 3
                s, bank = (j - 3) % slots, sum_bank[(j - 3) % 2]
                if part == 0:
                    pe.wait_ge(*exped.at((n + 1) * exp_units))
                    pe.wait_ge(*v_in.at(n + 1))
                    banks = len(set(sum_bank))
                    if due(n - banks + 1):
                        pe.wait_ge(*o_out.at(n - banks + 1))
                for i in range(part * 2, min(part * 2 + 2, blocks)):
                    last = nc.tensor.matmul(k.ps[0:WIDE + 1, bank, :], v_st[0:width, s, i, 0:WIDE + 1], probs[0:width, s, i, :],
                                            start=i == 0, stop=i == blocks - 1)
                if i == blocks - 1:
                    last.then_inc(summed.sem, 1)

            def step(it, j):
                n = heads * it + j
                score(it, j, 0)
                if context:
                    if due(n):
                        turn_max(it, j)
                    if due(n - 1):
                        score_t(it, j, 0)
                    if due(n - 2):
                        sum_up(it, j, 0)
                    return
                if due(n - 1):
                    score_t(it, j, 0)
                score(it, j, 1)
                if due(n - 2):
                    sum_up(it, j, 0)
                if due(n):
                    turn_max(it, j)
                score(it, j, 2)
                if due(n - 1):
                    score_t(it, j, 1)
                score(it, j, 3)
                if due(n - 2):
                    sum_up(it, j, 1)

            pe.wait_ge(*ones.at(2))
            for j in range(heads):
                step(0, j)
            with pe.Fori(1, turns) as it:
                for j in range(heads):
                    step(it, j)
            for j in range(3):
                if j == 0:
                    turn_max(turns, 0)
                if j < 2:
                    for e in range(exp_units):
                        score_t(turns, j, e)
                for part in range(exp_units):
                    sum_up(turns, j, part)

        @block.vector
        def _(dve):
            def out(it, j):
                n, s = heads * it + j - 4, j % 2
                dve.wait_ge(*summed.at(n + 1))
                if due(n - 1):
                    dve.wait_ge(*out_stored[s].at(8 * (n - s)))
                nc.vector.tensor_copy(o_sb[:, s, :], k.ps[0:WIDE + 1, sum_bank[s], :]).then_inc(o_out.sem, 1)

            def maxima(it, j):
                n, s = heads * it + j, j % 2
                if due(n - 1):
                    dve.wait_ge(*max_split.at(2 * n - 2))
                    dve.wait_ge(*max_turned.at(n - 1))
                for i in range(score_units):
                    dve.wait_ge(*scores.at(n * score_units + i + 1))
                    if context:
                        nc.vector.tensor_reduce(neg_max[:, s, :], k.ps[:, s, 0:TB * M].rearrange("p (a m) -> p a m", a=TB),
                                                axis=AX.X, op=ALU.max, negate=True).then_inc(maxed.sem, 1)
                    else:
                        nc.vector.tensor_reduce(neg_max[:, s, i:i + 1], k.ps[:, i % 2, :], axis=AX.X, op=ALU.max,
                                                negate=True).then_inc(maxed.sem, 1)
                dve.wait_ge(*maxed.at((n + 1) * score_units))
                nc.vector.tensor_copy(max_parts[:, s, :, 0], neg_max[:, s, :]).then_inc(max_split.sem, 1)
                dve.wait_ge(*max_split.at(2 * n + 1))
                nc.vector.tensor_tensor(max_parts[:, s, :, 1], neg_max[:, s, :], max_parts[:, s, :, 0],
                                        ALU.subtract).then_inc(max_split.sem, 1)

            def step(it, j):
                if due(heads * it + j - 3):
                    out(it, j)
                maxima(it, j)

            for j in range(heads):
                step(0, j)
            with dve.Fori(1, turns) as it:
                for j in range(heads):
                    step(it, j)
            for j in range(4):
                out(turns, j)

        @block.scalar
        def _(act):
            def max_row(it, j):
                n = heads * it + j - 1
                u, h = (j - 1) // 4 % turn, (j - 1) % 4
                act.wait_ge(*max_turned.at(n + 1))
                nc.scalar.activation(q_st[WIDE:WIDE + 1, u, h, :], k.ps[WIDE:WIDE + 1, 7, :], ACT.Copy).then_inc(max_rows.sem, 1)

            def exps(it, j, e):
                n, s = heads * it + j - 2, (j - 2) % slots
                if e == 0 and due(n - slots + 1):
                    act.wait_ge(*summed.at(n - slots + 1))
                act.wait_ge(*scores_t.at(n * exp_units + e + 1))
                if context:
                    nc.scalar.activation(probs[0:M, s, 0, :], k.ps[0:M, 2 + j % 2, :], ACT.Exp,
                                         scale=WIDE ** -0.5).then_inc(exped.sem, 1)
                else:
                    nc.scalar.activation(probs[:, s, 2 * e:2 * e + 2, :], k.ps[:, 2 + 2 * e:4 + 2 * e, :], ACT.Exp,
                                         scale=WIDE ** -0.5).then_inc(exped.sem, 1)

            def step(it, j):
                n = heads * it + j
                if due(n - 1) and not context:
                    exps(it, j, 0)
                if due(n):
                    max_row(it, j)
                if due(n - 1):
                    exps(it, j, exp_units - 1)

            for j in range(heads):
                step(0, j)
            with act.Fori(1, turns) as it:
                for j in range(heads):
                    step(it, j)
            for j in range(2):
                if j == 0:
                    max_row(turns, j)
                for e in range(exp_units):
                    exps(turns, j, e)
    for s in q_in + k_in:
        s.passed(16 * turns)
    for s in out_stored:
        s.passed(8 * HEADS)
    for s, n in ((ones, 2), (v_in, HEADS),
                 (scores, HEADS * score_units), (maxed, HEADS * score_units), (max_split, 2 * HEADS), (max_turned, HEADS),
                 (max_rows, HEADS), (scores_t, HEADS * exp_units), (exped, HEADS * exp_units), (summed, HEADS), (o_out, HEADS)):
        s.passed(n)
    k.end_stage()


def stages():
    out = []

    def add(f, weights, *args):
        out.append((f, weights, args))

    def chunk(block, n):
        return MOD_AT[block] + 2 * n

    if "0" in BLOCKS:
        def norm0(i):
            add(normalise, [], chunk("L0", 2 * i - 2), chunk("L0", 2 * i - 1), f"L0_ln{i}_w", f"L0_ln{i}_b", 0)

        norm0(1)
        add(project_qkv, ["L0_Wqkv"], "L0_Wqkv", "L0_bqkv")
        add(attend, [], False)
        add(project_out, ["L0_Wos"], "L0_Wos", "L0_bos", None, False)
        norm0(2)
        add(project_cross, ["L0_Wq", "L0_Wk", "L0_Wv"], None, "L0_Wq", "L0_Wk", "L0_Wv", ("L0_bq", 0), ("L0_bk", 0), ("L0_bv", 0))
        add(attend, [], True)
        add(project_out, ["L0_Woc"], "L0_Woc", "L0_boc", None, False)
        norm0(3)
        add(feed_forward, ["L0_W1", "L0_W2"], "L0_W1", None, "L0_W2", "L0_b1", "L0_b2", ACT.Gelu, None)
    if "1" in BLOCKS:
        def norm1(i):
            add(normalise, [], chunk("L1", 2 * i - 1), chunk("L1", 2 * i - 2), f"L1_ln{i}_w", f"L1_ln{i}_b", 0)

        norm1(1)
        add(project_wide, ["L1_sa_wq", "L1_sa_wk", "L1_sa_wv"], "L1_sa_wq", "L1_sa_wk", "L1_sa_wv", False)
        add(attend_wide, [], False)
        add(project_out, ["L1_sa_wo"], "L1_sa_wo", "L1_sa_bo", None, True)
        norm1(1)
        add(normalise_context, [], "L1_ca_lnc_w", "L1_ca_lnc_b")
        add(project_wide, ["L1_ca_wq", "L1_ca_wk", "L1_ca_wv"], "L1_ca_wq", "L1_ca_wk", "L1_ca_wv", True)
        add(attend_wide, [], True)
        add(project_out, ["L1_ca_wo"], "L1_ca_wo", "L1_ca_bo", None, True)
        norm1(2)
        add(feed_forward, ["L1_ff_w1", "L1_ff_w2"], "L1_ff_w1", None, "L1_ff_w2", "L1_ff_b1", "L1_ff_b2", ACT.Gelu, None)
    if "2" in BLOCKS:
        def norm2(i):
            add(normalise, [], chunk("L2", 2 * i - 2), chunk("L2", 2 * i - 1), None, None, 1)

        norm2(1)
        add(project_qkv, ["L2_W_qkv"], "L2_W_qkv", "L2_b_qkv")
        add(attend, [], False)
        add(project_out, ["L2_W_proj"], "L2_W_proj", "L2_b_proj", None, False)
        norm2(2)
        add(project_cross, ["L2_W_ctx", "L2_W_q", "L2_W_k", "L2_W_v"], ("L2_W_ctx", "L2_b_ctx"), "L2_W_q", "L2_W_k", "L2_W_v",
            None, None, None)
        add(attend, [], True)
        add(project_out, ["L2_W_out"], "L2_W_out", "L2_b_out", None, False)
        norm2(3)
        add(feed_forward, ["L2_W_fc1", "L2_W_fc2"], "L2_W_fc1", None, "L2_W_fc2", "L2_b_fc1", "L2_b_fc2", ACT.Gelu_apprx_tanh, None)
    if "3" in BLOCKS:
        add(normalise_heads, [], chunk("L3", 0), chunk("L3", 1), 1)
        add(attend, [], False)
        add(project_out, [], None, None, chunk("L3", 2), False)
        add(normalise, [], chunk("L3", 3), chunk("L3", 4), None, None, 1)
        add(project_cross, ["L3_cond_w", "L3_ca_q", "L3_ca_k", "L3_ca_v"], ("L3_cond_w", "L3_cond_b"), "L3_ca_q", "L3_ca_k", "L3_ca_v",
            ("L3_ca_in_b", 0), ("L3_ca_in_b", 2), ("L3_ca_in_b", 4))
        add(attend, [], True)
        add(project_out, ["L3_ca_out_w"], "L3_ca_out_w", "L3_ca_out_b", chunk("L3", 5), False)
        add(normalise, [], chunk("L3", 6), chunk("L3", 7), None, None, 1)
        add(feed_forward, ["L3_w1", "L3_w3", "L3_w2"], "L3_w1", "L3_w3", "L3_w2", None, None, ACT.Silu, chunk("L3", 8))
    return out


def program(nc, ins, out):
    with ExitStack() as ctx:
        k = Chip(nc, ctx, ins, out)
        todo = stages()
        setup(k, todo[0][1])
        for i, (f, _, args) in enumerate(todo):
            f(k, todo[i + 1][1] if i + 1 < len(todo) else None, *args)


BLOCKS = "0123"


def kernel(**inputs):
    import concourse.bacc as _bacc
    from concourse.bass_utils import run_bass_kernel_spmd as _run

    a = {n.replace("_xcond", ""): np.asarray(v) for n, v in inputs.items()}
    a["L3_adaln_w"] = a["L3_adaln_w"].T
    order = np.arange(MID).reshape(4, 4, WIDE // 2, 2).transpose(0, 3, 1, 2).reshape(MID)
    mixed = np.arange(D).reshape(4, 4, NARROW).transpose(0, 2, 1).reshape(D)
    for n in ("L0_Wqkv", "L0_bqkv", "L2_W_qkv", "L2_b_qkv"):
        a[n] = a[n][..., np.concatenate([mixed, D + mixed, 2 * D + np.arange(D)])]
    for n in ("L0_Wq", "L0_bq", "L0_Wk", "L0_bk", "L2_W_q", "L2_W_k"):
        a[n] = a[n][..., mixed]
    wk, wv = a["L1_sa_wkv"][:, :MID], a["L1_sa_wkv"][:, MID:]
    a["L1_sa_wq"], a["L1_sa_wk"], a["L1_sa_wv"] = a["L1_sa_wq"][:, order], wk[:, order], wv
    wk, wv = a["L1_ca_wkv"][:, :MID], a["L1_ca_wkv"][:, MID:]
    a["L1_ca_wq"], a["L1_ca_wk"], a["L1_ca_wv"] = a["L1_ca_wq"][:, order], wk[:, order], wv
    a["L3_ca_q"], a["L3_ca_k"], a["L3_ca_v"] = (a["L3_ca_in_w"][i * D:(i + 1) * D].T for i in range(3))
    a["L3_ca_q"], a["L3_ca_k"] = a["L3_ca_q"][:, mixed], a["L3_ca_k"][:, mixed]
    a["L3_ca_in_b"] = a["L3_ca_in_b"][np.concatenate([mixed, D + mixed, 2 * D + np.arange(D)])]
    for n in ("L3_cond_w", "L3_ca_out_w", "L3_w1", "L3_w3", "L3_w2"):
        a[n] = a[n].T
    for n in ("L1_ca_lnc_w", "L1_ca_lnc_b"):
        a[n] = np.concatenate([a[n], np.zeros(2 * P - DC, np.float32)])
    for n in ("L3_qn_w", "L3_qn_b", "L3_kn_w", "L3_kn_b"):
        a[n] = np.tile(np.repeat(a[n], 4), 2)
    arrays = {n: a[n] for n in WEIGHTS}
    arrays["vectors"] = np.concatenate([a[n].reshape(c, P) for n, c in VECTORS]).T
    arrays["mods"] = np.concatenate([a[n] for n, _ in MODS], axis=1)
    arrays["x"] = a["x"].reshape(T, D)
    arrays["ctx"] = a["ctx_768"].reshape(B * M, DC)
    arrays["condT"] = a["cond_1024"].T
    inv = (1.0 / 10000.0 ** (np.arange(0, WIDE, 2, dtype=np.float32) / np.float32(WIDE))).astype(np.float32)
    angle = np.arange(N, dtype=np.float32)[None, :] * inv[:, None]
    arrays["rotary"] = np.concatenate([np.stack([np.cos(angle), np.sin(angle)])] * 4, axis=1).astype(np.float32)

    nc = _bacc.Bacc("TRN2", target_bir_lowering=False, num_devices=1)
    ins = {}
    for n in arrays:
        arrays[n] = np.ascontiguousarray(arrays[n])
        ins[n] = nc.dram_tensor(f"in_{n}", arrays[n].shape, mybir.dt.from_np(arrays[n].dtype), kind="ExternalInput").ap()
    out = nc.dram_tensor("out_0", (B, N, D), F32, kind="ExternalOutput").ap()
    program(nc, ins, out)
    r = _run(nc, [{f"in_{n}": v for n, v in arrays.items()}], core_ids=[0])
    return r.results[0]["out_0"]
```

```python
from contextlib import ExitStack

import concourse.bass as bass
from concourse import mybir
import numpy as np

F32 = mybir.dt.float32
BF16 = mybir.dt.bfloat16
ACT = mybir.ActivationFunctionType
ALU = mybir.AluOpType
AX = mybir.AxisListType

B, N, D, H = 4, 512, 256, 16
M, DC = 64, 192
T = B * N
P = 128
TILES = T // P
TB = N // P
C = D // P
FF = 4 * D
FC = FF // P
HEADS = B * H
MID = 1024
WIDE = MID // H
NARROW = D // H

VECTORS = (
    [("L0_bmod", 12), ("L1_g1_b", 2), ("L1_b1_b", 2), ("L1_g2_b", 2), ("L1_b2_b", 2), ("L2_b_ada", 12), ("L3_adaln_b", 18)]
    + [(f"L0_ln{i}_{v}", 2) for i in (1, 2, 3) for v in "wb"]
    + [(f"L1_ln{i}_{v}", 2) for i in (1, 2) for v in "wb"]
    + [("L0_bqkv", 6), ("L0_bos", 2), ("L0_bq", 2), ("L0_bk", 2), ("L0_bv", 2), ("L0_boc", 2), ("L0_b1", 8), ("L0_b2", 2)]
    + [("L1_sa_bo", 2), ("L1_ca_lnc_w", 2), ("L1_ca_lnc_b", 2), ("L1_ca_bo", 2), ("L1_ff_b1", 8), ("L1_ff_b2", 2)]
    + [("L2_b_qkv", 6), ("L2_b_proj", 2), ("L2_b_ctx", 2), ("L2_b_out", 2), ("L2_b_fc1", 8), ("L2_b_fc2", 2)]
    + [("L3_qn_w", 1), ("L3_qn_b", 1), ("L3_kn_w", 1), ("L3_kn_b", 1), ("L3_ca_in_b", 6), ("L3_ca_out_b", 2), ("L3_cond_b", 2)]
)
OFFSET = {}
for _name, _n in VECTORS:
    OFFSET[_name] = sum(n for k, n in VECTORS if k in OFFSET)
NVEC = sum(n for _, n in VECTORS)

MODS = [("L0_Wmod", 1536), ("L1_g1_w", 256), ("L1_b1_w", 256), ("L1_g2_w", 256), ("L1_b2_w", 256), ("L2_W_ada", 1536), ("L3_adaln_w", 2304)]
MOD_AT = {"L0": 0, "L1": 12, "L2": 20, "L3": 32}
NMOD = sum(n for _, n in MODS) // P

WEIGHTS = {
    "L0_Wqkv": (D, 3 * D), "L0_Wos": (D, D), "L0_Wq": (D, D), "L0_Wk": (DC, D), "L0_Wv": (DC, D), "L0_Woc": (D, D),
    "L0_W1": (D, FF), "L0_W2": (FF, D),
    "L1_sa_wq": (D, MID), "L1_sa_wk": (D, MID), "L1_sa_wv": (D, MID), "L1_sa_wo": (MID, D),
    "L1_ca_wq": (D, MID), "L1_ca_wk": (DC, MID), "L1_ca_wv": (DC, MID), "L1_ca_wo": (MID, D),
    "L1_ff_w1": (D, FF), "L1_ff_w2": (FF, D),
    "L2_W_qkv": (D, 3 * D), "L2_W_proj": (D, D), "L2_W_ctx": (DC, D), "L2_W_q": (D, D), "L2_W_k": (D, D), "L2_W_v": (D, D),
    "L2_W_out": (D, D), "L2_W_fc1": (D, FF), "L2_W_fc2": (FF, D),
    "L3_cond_w": (DC, D), "L3_ca_q": (D, D), "L3_ca_k": (D, D), "L3_ca_v": (D, D), "L3_ca_out_w": (D, D),
    "L3_w1": (D, FF), "L3_w3": (D, FF), "L3_w2": (FF, D),
}


class Counted:

    def __init__(self, sem):
        self.sem, self.base = sem, 0

    def at(self, n):
        return self.sem, self.base + n

    def passed(self, n):
        self.base += n


class Chip:

    def __init__(self, nc, ctx, ins, out):
        self.nc, self.ins, self.out = nc, ins, out
        self._ctx, self._named = ctx, {}

        def sb(name, shape, dt=F32):
            return ctx.enter_context(nc.sbuf_tensor(name, shape, dt))

        self.x = sb("x", [P, TILES, D])
        self.hT = sb("hT", [P, C, T])
        self.w = [sb(f"w{i}", [P, 2048]) for i in range(4)]
        self.big1 = sb("big1", [P, 16384])
        self.big2 = sb("big2", [P, 16384])
        self.ident = sb("ident", [P, P])
        self.identb = sb("identb", [P, P], BF16)
        self.vec = sb("vec", [P, NVEC])
        self.mod = sb("mod", [P, NMOD, B])
        self.scale = sb("scale", [P, C, B])
        self.shift = sb("shift", [P, C, B])
        self.ctxT = sb("ctxT", [P, 2, B * M])
        self.ctx2T = sb("ctx2T", [P, 2, B * M])
        self.rows = sb("rows", [P, 4, D])
        self.small = sb("small", [P, 512])
        self.eps = sb("eps", [P, 2])
        self.ps = ctx.enter_context(nc.psum_tensor("ps", [P, 8, 512], F32))

        def dram(name, shape, dt):
            return nc.dram_tensor(name, shape, dt, kind="Internal").ap()

        self.q_parts = dram("q_parts", [HEADS // 4, 3, 4 * NARROW, N], BF16)
        self.k_parts = dram("k_parts", [HEADS // 4, 3, 4 * NARROW, N], BF16)
        self.kx_parts = dram("kx_parts", [HEADS // 4, 3, 4 * NARROW, M], BF16)
        self.q_wide = dram("q_wide", [HEADS, WIDE, N], F32)
        self.k_wide = dram("k_wide", [HEADS, WIDE, N], F32)
        self.kx_wide = dram("kx_wide", [HEADS, WIDE, M], F32)
        self.q_wide_parts = dram("q_wide_parts", [HEADS, WIDE, 2, N], BF16)
        self.k_wide_parts = dram("k_wide_parts", [HEADS, WIDE, 2, N], BF16)
        self.o_sums = dram("o_sums", [HEADS, 2 * NARROW, N], F32)
        self.o_wide = dram("o_wide", [HEADS, WIDE + 1, N], F32)
        self.w_turn = 0
        self.where = {}
        self.weights_in = [self.semaphore("weights_in_even"), self.semaphore("weights_in_odd")]
        self.stage, self.due, self.coming = 0, 0, 0

    def semaphore(self, name):
        if name not in self._named:
            self._named[name] = Counted(self._ctx.enter_context(self.nc.semaphore(name)))
        return self._named[name]

    def v(self, name, c=0, n=1):
        return self.vec[:, OFFSET[name] + c:OFFSET[name] + c + n]

    def load_weights(self, sp, names):
        sig = self.weights_in[(self.stage + 1) % 2]
        n = taken = 0
        for name in names:
            rows, cols = WEIGHTS[name]
            src = self.ins[name]
            chunks = -(-rows // P)
            if not taken or taken + chunks * cols > 2048:
                slot, taken = self.w[self.w_turn % 4], 0
                self.w_turn += 1
            view = slot[:, taken:taken + chunks * cols].rearrange("p (c n) -> p c n", c=chunks)
            taken += chunks * cols
            self.where[name] = view
            whole = rows // P
            sp.dma_start(view[:, 0:whole, :], src[0:whole * P, :].rearrange("(c p) n -> p c n", p=P)).then_inc(sig.sem, 16)
            n += 16
            if rows % P:
                sp.dma_start(view[0:rows % P, whole, :], src[whole * P:rows, :]).then_inc(sig.sem, 16)
                n += 16
        self.coming = n

    def weights_due(self):
        return self.weights_in[self.stage % 2].at(self.due)

    def end_stage(self):
        self.weights_in[self.stage % 2].passed(self.due)
        self.stage += 1
        self.due, self.coming = self.coming, 0


def setup(k, next_weights):
    nc = k.nc
    ins = k.ins
    loaded, mods_loaded = k.semaphore("inputs_loaded"), {b: k.semaphore(f"mod_weights_loaded_{b}") for b in MOD_AT}
    x_in = k.semaphore("x_loaded")
    made, masked, cond_ready = k.semaphore("constants_made"), k.semaphore("identity_ready"), k.semaphore("cond_ready")
    modded, done, trans = k.semaphore("mod_products"), k.semaphore("mod_done"), k.semaphore("ctx_transposed")
    wmod = k.big1[:, 0:C * NMOD * P].rearrange("p (c n) -> p c n", c=C)
    ends = [*MOD_AT.values(), NMOD]
    columns = {b: slice(at * P, end * P) for (b, at), end in zip(MOD_AT.items(), ends[1:])}
    ctx_tok = k.big2[:, 0:2 * DC].rearrange("p (t d) -> p t d", t=2)
    condT = k.big2[:, 400:400 + C * B].rearrange("p (c b) -> p c b", c=C)
    siluT = k.big2[:, 416:416 + C * B].rearrange("p (c b) -> p c b", c=C)
    with nc.Block() as block:
        @block.sync
        def _(sp):
            sp.dma_start(k.vec[:, :], ins["vectors"]).then_inc(loaded.sem, 16)
            sp.dma_start(condT, ins["condT"].rearrange("(c p) b -> p c b", p=P)).then_inc(loaded.sem, 16)
            sp.dma_start(ctx_tok, ins["ctx"].rearrange("(t p) d -> p t d", p=P)).then_inc(loaded.sem, 16)
            for b, cols in columns.items():
                sp.dma_start(wmod[:, :, cols], ins["mods"].rearrange("(c p) n -> p c n", p=P)[:, :, cols]).then_inc(mods_loaded[b].sem, 16)
            sp.dma_start(k.x[:, :, :], ins["x"].rearrange("(t p) d -> p t d", p=P)).then_inc(x_in.sem, 16)
            k.load_weights(sp, next_weights)

        @block.gpsimd
        def _(pool):
            nc.gpsimd.memset(k.ident[:, :], 0.0).then_inc(made.sem, 1)
            nc.gpsimd.memset(k.identb[:, :], 0.0).then_inc(made.sem, 1)
            nc.gpsimd.memset(k.eps[:, 0:1], 1e-5).then_inc(made.sem, 1)
            nc.gpsimd.memset(k.eps[:, 1:2], 1e-6).then_inc(made.sem, 1)
            pool.wait_ge(*made.at(4))
            for m in (k.ident, k.identb):
                nc.gpsimd.affine_select(out=m[:, :], in_=m[:, :], compare_op=ALU.not_equal, fill=1.0, base=0,
                                        pattern=[[-1, P]], channel_multiplier=1).then_inc(masked.sem, 1)

        @block.scalar
        def _(act):
            act.wait_ge(*loaded.at(48))
            nc.scalar.activation(siluT, condT, ACT.Silu).then_inc(cond_ready.sem, 1)

        @block.tensor
        def _(pe):
            pe.wait_ge(*masked.at(2))
            pe.wait_ge(*loaded.at(48))
            for t in range(2):
                nc.tensor.transpose(k.ps[:, 1, t * P:(t + 1) * P], ctx_tok[:, t, 0:P], k.ident[:, :])
                last = nc.tensor.transpose(k.ps[0:DC - P, 2, t * P:(t + 1) * P], ctx_tok[:, t, P:DC], k.ident[:, :])
            last.then_inc(trans.sem, 1)
            pe.wait_ge(*cond_ready.at(1))
            for m in range(NMOD):
                for b in MOD_AT:
                    if MOD_AT[b] == m:
                        pe.wait_ge(*mods_loaded[b].at(16))
                src = condT if MOD_AT["L1"] <= m < MOD_AT["L2"] else siluT
                for c in range(C):
                    last = nc.tensor.matmul(k.ps[:, 0, m * B:(m + 1) * B], wmod[:, c, m * P:(m + 1) * P], src[:, c, :],
                                            start=c == 0, stop=c == C - 1)
            last.then_inc(modded.sem, 1)

        @block.vector
        def _(dve):
            dve.wait_ge(*trans.at(1))
            nc.vector.tensor_copy(k.ctxT[:, 0, :], k.ps[:, 1, 0:B * M])
            nc.vector.tensor_copy(k.ctxT[0:DC - P, 1, :], k.ps[0:DC - P, 2, 0:B * M])
            dve.wait_ge(*x_in.at(16))
            dve.wait_ge(*modded.at(1))
            nc.vector.tensor_tensor(k.mod[:, :, :], k.ps[:, 0, 0:NMOD * B].rearrange("p (m b) -> p m b", b=B),
                                    k.vec[:, 0:NMOD].unsqueeze(2).broadcast_to([P, NMOD, B]), ALU.add).then_inc(done.sem, 1)
    for s, n in ((loaded, 48), (x_in, 16), *((z, 16) for z in mods_loaded.values()), (made, 4), (masked, 2), (cond_ready, 1), (modded, 1), (done, 1), (trans, 1)):
        s.passed(n)
    k.end_stage()


class Norm:

    def __init__(self, k, spec, banks):
        self.k, self.banks = k, banks
        self.shift_at, self.scale_at, self.w, self.b, self.eps = spec
        self.coef, self.stats, self.var = k.semaphore("coefficients"), k.semaphore("stats"), k.semaphore("variances")
        self.root, self.rstd, self.rows = k.semaphore("roots"), k.semaphore("rstd"), k.semaphore("normed_rows")
        self.turned, self.out = k.semaphore("transposed"), k.semaphore("modulated")
        self.st = k.small[:, 0:96].rearrange("p (t s) -> p t s", s=6)
        self.mv = k.small[:, 96:128].rearrange("p (t s) -> p t s", s=2)
        self.sd, self.rs = k.small[:, 128:144], k.small[:, 144:160]
        self.xn = k.big2[:, 8192:8192 + 2 * TB * D].rearrange("p (s t d) -> p s t d", s=2, t=TB)

    def dve_coefficients(self, dve):
        k, vector = self.k, self.k.nc.vector
        g = k.mod[:, self.scale_at:self.scale_at + C, :]
        s = k.mod[:, self.shift_at:self.shift_at + C, :]
        if self.w is None:
            vector.tensor_scalar(k.scale[:, :, :], g, 1.0, None, ALU.add).then_inc(self.coef.sem, 1)
            vector.tensor_copy(k.shift[:, :, :], s).then_inc(self.coef.sem, 1)
            return
        wv = k.v(self.w, 0, C).unsqueeze(2).broadcast_to([P, C, B])
        bv = k.v(self.b, 0, C).unsqueeze(2).broadcast_to([P, C, B])
        vector.scalar_tensor_tensor(k.scale[:, :, :], g, 1.0, wv, ALU.add, ALU.mult).then_inc(self.coef.sem, 1)
        vector.scalar_tensor_tensor(k.shift[:, :, :], g, 1.0, bv, ALU.add, ALU.mult).then_inc(self.coef.sem, 1)
        dve.wait_ge(*self.coef.at(2))
        vector.tensor_tensor(k.shift[:, :, :], k.shift[:, :, :], s, ALU.add).then_inc(self.coef.sem, 1)

    def dve_stats(self, t):
        self.k.nc.vector.bn_stats(self.st[:, t, :], self.k.x[:, t, :]).then_inc(self.stats.sem, 1)

    def dve_variances(self, dve, b):
        for t in range(b * TB, (b + 1) * TB):
            dve.wait_ge(*self.stats.at(t + 1))
            self.k.nc.vector.bn_aggr(self.mv[:, t, :], self.st[:, t, :]).then_inc(self.var.sem, 1)

    def act_root(self, act, b):
        ts = slice(b * TB, (b + 1) * TB)
        act.wait_ge(*self.var.at((b + 1) * TB))
        self.k.nc.scalar.activation(self.sd[:, ts], self.mv[:, ts, 1], ACT.Sqrt,
                                    bias=self.k.eps[:, self.eps:self.eps + 1]).then_inc(self.root.sem, 1)

    def dve_rows(self, dve, b):
        vector = self.k.nc.vector
        ts = range(b * TB, (b + 1) * TB)
        dve.wait_ge(*self.root.at(b + 1))
        vector.reciprocal(self.rs[:, b * TB:(b + 1) * TB], self.sd[:, b * TB:(b + 1) * TB]).then_inc(self.rstd.sem, 1)
        dve.wait_ge(*self.rstd.at(b + 1))
        if b >= 2:
            dve.wait_ge(*self.turned.at(b - 1))
        for t in ts:
            vector.tensor_scalar(self.xn[:, b % 2, t % TB, :], self.k.x[:, t, :], self.mv[:, t, 0:1], self.rs[:, t:t + 1],
                                 ALU.subtract, ALU.mult).then_inc(self.rows.sem, 1)

    def pe_turn(self, pe, b):
        pe.wait_ge(*self.rows.at((b + 1) * TB))
        if b >= len(self.banks):
            pe.wait_ge(*self.out.at((b - len(self.banks) + 1) * C))
        for c in range(C):
            bank = self.banks[b % len(self.banks)][c]
            for i in range(TB):
                last = self.k.nc.tensor.transpose(self.k.ps[:, bank, i * P:(i + 1) * P], self.xn[:, b % 2, i, c * P:(c + 1) * P],
                                                  self.k.ident[:, :])
        last.then_inc(self.turned.sem, 1)

    def act_modulate(self, act, b):
        k = self.k
        act.wait_ge(*self.coef.at(2 if self.w is None else 3))
        act.wait_ge(*self.turned.at(b + 1))
        for c in range(C):
            k.nc.scalar.activation(k.hT[:, c, b * N:(b + 1) * N], k.ps[:, self.banks[b % len(self.banks)][c], :], ACT.Identity,
                                   bias=k.shift[:, c, b:b + 1], scale=k.scale[:, c, b:b + 1]).then_inc(self.out.sem, 1)

    def passed(self):
        for s, n in ((self.coef, 2 if self.w is None else 3), (self.stats, TILES), (self.var, TILES), (self.root, B), (self.rstd, B),
                     (self.rows, TILES), (self.turned, B), (self.out, C * B)):
            s.passed(n)


def normalise(k, next_weights, norm):
    norm = Norm(k, norm, ((0, 1), (2, 3)))
    with k.nc.Block() as block:
        @block.sync
        def _(sp):
            k.load_weights(sp, next_weights)

        @block.vector
        def _(dve):
            norm.dve_coefficients(dve)
            for t in range(TILES):
                norm.dve_stats(t)
            for b in range(B):
                norm.dve_variances(dve, b)
            for b in range(B):
                norm.dve_rows(dve, b)

        @block.scalar
        def _(act):
            for b in range(B):
                norm.act_root(act, b)
            for b in range(B):
                norm.act_modulate(act, b)

        @block.tensor
        def _(pe):
            for b in range(B):
                norm.pe_turn(pe, b)
    norm.passed()
    k.end_stage()


def set_row(k, bank, columns):
    for c in range(C):
        last = k.nc.tensor.matmul(bank[:, c * P:(c + 1) * P], columns[c].broadcast_to([P, P]), k.ident[:, :],
                                  start=True, stop=True)
    return last


class Split:

    SLOTS = 3

    def __init__(self, k):
        n = self.SLOTS
        self.k = k
        self.whole_ready, self.first_ready = k.semaphore("whole_ready"), k.semaphore("part_1_ready")
        self.left_ready, self.second_ready = k.semaphore("remainder_ready"), k.semaphore("part_2_ready")
        self.third_ready = k.semaphore("part_3_ready")
        self.stored = [k.semaphore(f"parts_stored_{i}") for i in range(n)]
        self.stores = [0] * n
        self.before = []
        self.whole = k.big1[:, 0:n * 512].rearrange("p (s n) -> p s n", s=n)
        self.left = k.big1[:, n * 512:2 * n * 512].rearrange("p (s n) -> p s n", s=n)
        self.parts = k.big1[:, 2 * n * 512:2 * n * 512 + n * 768].bitcast(BF16).rearrange("p (s c n) -> p s c n", s=n, c=3)

    def plan(self, stores):
        for u, n in enumerate(stores):
            self.before.append(self.stores[u % self.SLOTS])
            self.stores[u % self.SLOTS] += 16 * n

    def act_whole(self, act, u, source, bias, width, scale=1.0):
        if u >= self.SLOTS:
            act.wait_ge(*self.third_ready.at(u - self.SLOTS + 1))
        self.k.nc.scalar.activation(self.whole[:, u % self.SLOTS, 0:width], source, ACT.Identity, bias=bias,
                                    scale=scale).then_inc(self.whole_ready.sem, 1)

    def act_first(self, act, u, width):
        act.wait_ge(*self.whole_ready.at(u + 1))
        if u >= self.SLOTS:
            act.wait_ge(*self.stored[u % self.SLOTS].at(self.before[u]))
        self.k.nc.scalar.activation(self.parts[:, u % self.SLOTS, 0, 0:width], self.whole[:, u % self.SLOTS, 0:width],
                                    ACT.Copy).then_inc(self.first_ready.sem, 1)

    def dve_rest(self, dve, u, width):
        vector = self.k.nc.vector
        s, w = u % self.SLOTS, slice(0, width)
        dve.wait_ge(*self.first_ready.at(u + 1))
        vector.tensor_tensor(self.left[:, s, w], self.whole[:, s, w], self.parts[:, s, 0, w],
                             ALU.subtract).then_inc(self.left_ready.sem, 1)
        dve.wait_ge(*self.left_ready.at(u + 1))
        vector.tensor_copy(self.parts[:, s, 1, w], self.left[:, s, w]).then_inc(self.second_ready.sem, 1)
        dve.wait_ge(*self.second_ready.at(u + 1))
        vector.tensor_tensor(self.parts[:, s, 2, w], self.left[:, s, w], self.parts[:, s, 1, w],
                             ALU.subtract).then_inc(self.third_ready.sem, 1)

    def store(self, sp, u, dst, g):
        sp.wait_ge(*self.third_ready.at(u + 1))
        for half in range(2):
            sp.dma_start(dst[g + half].rearrange("c r t -> r c t"),
                         self.parts[64 * half:64 * half + 64, u % self.SLOTS, :, :]).then_inc(self.stored[u % self.SLOTS].sem, 16)

    def store_context(self, sp, u, m):
        sp.wait_ge(*self.third_ready.at(u + 1))
        by_batch = self.k.kx_parts.rearrange("(b g) c r t -> b g c r t", b=B)
        for half in range(2):
            for c in range(3):
                src = self.parts[64 * half:64 * half + 64, u % self.SLOTS, c, 0:B * M].rearrange("r (b t) -> r b t", b=B)
                sp.dma_start(by_batch[:, m * 2 + half, c, :, :].rearrange("b r t -> r b t"),
                             src).then_inc(self.stored[u % self.SLOTS].sem, 16)

    def all_stored(self, sp):
        for s in range(self.SLOTS):
            sp.wait_ge(*self.stored[s].at(self.stores[s]))

    def passed(self):
        units = len(self.before)
        for s in (self.whole_ready, self.first_ready, self.left_ready, self.second_ready, self.third_ready):
            s.passed(units)
        for s in range(self.SLOTS):
            self.stored[s].passed(self.stores[s])


def v_narrow(k):
    return k.big2[:, 0:TILES * D].rearrange("p (b g i d) -> p b g i d", b=B, g=4, i=TB)


def vx_narrow(k):
    return k.big2[:, 0:HEADS // 2 * NARROW].rearrange("p (n d) -> p n d", d=NARROW)


def project_qkv(k, next_weights, w, bias):
    nc = k.nc
    split = Split(k)
    product, v_product, v_read = k.semaphore("product"), k.semaphore("v_product"), k.semaphore("v_read")
    row_made, row_in = k.semaphore("row_made"), k.semaphore("row_in")
    units = [(m, b) for m in range(4) for b in range(B)]
    split.plan([2] * len(units))
    v = v_narrow(k)
    with nc.Block() as block:
        @block.sync
        def _(sp):
            k.load_weights(sp, next_weights)
            for u, (m, b) in enumerate(units):
                split.store(sp, u, (k.q_parts, k.k_parts)[m // 2], b * 4 + (m % 2) * 2)
            split.all_stored(sp)

        @block.tensor
        def _(pe):
            wt = k.where[w]
            pe.wait_ge(*k.weights_due())
            set_row(k, k.ps[:, 7, :], [k.v(bias, 4 + c) for c in range(C)]).then_inc(row_made.sem, 1)
            for u, (m, b) in enumerate(units):
                if u >= 4:
                    pe.wait_ge(*split.whole_ready.at(u - 3))
                for c in range(C):
                    last = nc.tensor.matmul(k.ps[:, u % 4, :], wt[:, c, m * P:(m + 1) * P], k.hT[:, c, b * N:(b + 1) * N],
                                            start=c == 0, stop=c == C - 1)
                last.then_inc(product.sem, 1)
            for t in range(TILES):
                if t >= 3:
                    pe.wait_ge(*v_read.at(t - 2))
                for c in range(C):
                    last = nc.tensor.matmul(k.ps[:, 4 + t % 3, 0:D], k.hT[:, c, t * P:(t + 1) * P], wt[:, c, 2 * D:3 * D],
                                            start=c == 0, stop=c == C - 1)
                last.then_inc(v_product.sem, 1)

        @block.scalar
        def _(act):
            for u, (m, b) in enumerate(units):
                act.wait_ge(*product.at(u + 1))
                split.act_whole(act, u, k.ps[:, u % 4, :], k.v(bias, m), N)
                split.act_first(act, u, N)

        @block.vector
        def _(dve):
            dve.wait_ge(*row_made.at(1))
            nc.vector.tensor_copy(k.rows[:, 0, :], k.ps[:, 7, 0:D]).then_inc(row_in.sem, 1)
            for u in range(len(units)):
                split.dve_rest(dve, u, N)
            dve.wait_ge(*row_in.at(1))
            for t in range(TILES):
                dve.wait_ge(*v_product.at(t + 1))
                nc.vector.tensor_tensor(v[:, t // TB, :, t % TB, :], k.ps[:, 4 + t % 3, 0:D].rearrange("p (g d) -> p g d", g=4),
                                        k.rows[:, 0, :].rearrange("p (g d) -> p g d", g=4), ALU.add).then_inc(v_read.sem, 1)
    for s, n in ((product, len(units)), (v_product, TILES), (v_read, TILES), (row_made, 1), (row_in, 1)):
        s.passed(n)
    split.passed()
    k.end_stage()


def due(n):
    return not isinstance(n, int) or n > 0


def attend(k, next_weights):
    nc = k.nc
    groups, turn, first = HEADS // 4, 2, 2
    heads, turns = 4 * turn, groups // turn
    rows, stack = 6 * NARROW, 6 * NARROW + 2
    block_at = {2: 0, 3: 1, 0: 2, 1: 3}
    score_bank, used_before = ((0, 1, 7, 0), (1, 7, 0, 1)), ((2, 2, 5, 3), (3, 3, 3, 3))
    v = v_narrow(k).rearrange("p b g i d -> p (b g) i d")

    q_st = k.big1[0:stack, 0:turn * 1024].bitcast(BF16).rearrange("p (u h t) -> p u h t", u=turn, h=4)
    k_st = k.big1[0:stack, 4096:4096 + 2 * turn * N].bitcast(BF16).rearrange("p (u h t) -> p u h t", u=turn, h=4)
    probs = [z[:, 8192:8192 + 4 * TB * N].rearrange("p (h i t) -> p h i t", h=4, i=TB) for z in (k.big1, k.big2)]
    spare = k.hT[:, :, :].rearrange("p c t -> p (c t)")
    v_st = spare[:, 0:2 * TB * P].rearrange("p (u i h d) -> p u i h d", u=2, i=TB, h=4)
    o_sb = spare[:, 1024:2048].rearrange("p (u t) -> p u t", u=2)
    neg_max = k.small[:, 0:8].rearrange("p (s a) -> p s a", s=2)
    max_parts = k.small[:, 8:16].bitcast(BF16).rearrange("p (s a c) -> p s a c", s=2, c=2)

    q_in, k_in = [k.semaphore(f"q_in_{u}") for u in range(turn)], [k.semaphore(f"k_in_{u}") for u in range(turn)]
    out_stored = [k.semaphore(f"out_stored_{u}") for u in range(2)]
    ones, v_in = k.semaphore("ones_made"), k.semaphore("v_staged")
    scores, maxed, max_split = k.semaphore("scores"), k.semaphore("maxed"), k.semaphore("max_split")
    max_turned, max_rows = k.semaphore("max_turned"), k.semaphore("max_rows")
    scores_t, exped, summed, o_out = k.semaphore("scores_t"), k.semaphore("exped"), k.semaphore("summed"), k.semaphore("o_out")

    with nc.Block() as block:
        @block.sync
        def _(sp):
            def load(it, u):
                g = turn * it + u
                if due(g - turn + 1):
                    sp.wait_ge(*scores_t.at((g - turn + 1) * 8))
                for p0, parts in ((0, 3), (3, 2), (5, 1)):
                    sp.dma_start(q_st[p0 * NARROW:(p0 + parts) * NARROW, u, :, :],
                                 k.q_parts[bass.ds(g, 1), 0:parts].rearrange("g c (d h) t -> (g c d) h t", h=4)).then_inc(q_in[u].sem, 16)
                    src = k.k_parts[bass.ds(g, 1), (0, 3, 5).index(p0)].rearrange("g (d h) t -> g d (h t)", h=4)
                    sp.dma_start(k_st[p0 * NARROW:(p0 + parts) * NARROW, u, :, :].rearrange("p h t -> p (h t)"),
                                 src.broadcast_to([parts, NARROW, 4 * N])).then_inc(k_in[u].sem, 16)

            def store(g, u):
                sp.wait_ge(*o_out.at(g + 1))
                sp.dma_start(k.o_sums[bass.ds(g * 4, 4)].rearrange("h r t -> (h r) t"), o_sb[:, u, :]).then_inc(out_stored[u].sem, 16)

            def groups_of(it):
                for u in range(turn):
                    load(it, u)
                    if due(turn * it + u - behind + 1):
                        store(turn * it + u - behind, (u - behind) % 2)

            behind = turn + 1
            for u in range(turn):
                load(0, u)
            k.load_weights(sp, next_weights)
            for it in range(1, first + 1):
                groups_of(it)
            with sp.Fori(first + 1, turns) as it:
                groups_of(it)
            for g in range(groups - behind, groups):
                store(g, g % 2)
            for u in range(2):
                sp.wait_ge(*out_stored[u].at(16 * (groups // 2)))

        @block.gpsimd
        def _(pool):
            nc.gpsimd.memset(k_st[rows:stack, :, :, :], 1.0).then_inc(ones.sem, 1)
            pool.wait_ge(*ones.at(1))
            nc.gpsimd.memset(v_st[:, :, :, :, NARROW:2 * NARROW], 1.0).then_inc(ones.sem, 1)

            def stage(it, u):
                g = turn * it + u
                if due(g - 1):
                    pool.wait_ge(*summed.at(g - 1))
                src = v[:, bass.ds(g, 1), :, :].rearrange("p g i (h d) -> p (g i) h d", h=4)
                nc.gpsimd.tensor_copy(v_st[:, u % 2, :, :, 0:NARROW], src).then_inc(v_in.sem, 1)

            for it in range(first):
                for u in range(turn):
                    stage(it, u)
            with pool.Fori(first, turns) as it:
                for u in range(turn):
                    stage(it, u)

        @block.tensor
        def _(pe):
            def score(it, j, i):
                u, h = j // 4, j % 4
                if h == 0 and i == 0:
                    pe.wait_ge(*q_in[u].at(48 * it + 48))
                    pe.wait_ge(*k_in[u].at(48 * it + 48))
                m = (heads * it + j) * TB + i
                ago = used_before[j % 2][i]
                if due(m - ago + 1):
                    pe.wait_ge(*maxed.at(m - ago + 1))
                nc.tensor.matmul(k.ps[:, score_bank[j % 2][i], :], q_st[0:rows, u, h, i * P:(i + 1) * P], k_st[0:rows, u, h, :],
                                 start=True, stop=True).then_inc(scores.sem, 1)

            def turn_max(it, j):
                n = heads * it + j - 1
                pe.wait_ge(*max_split.at(2 * n + 2))
                if due(n):
                    pe.wait_ge(*exped.at(2 * n - 1))
                for a in range(TB):
                    last = nc.tensor.matmul(k.ps[rows:stack, 2, a * P:(a + 1) * P], max_parts[:, (j - 1) % 2, a, :],
                                            k.identb[:, :], start=True, stop=True)
                last.then_inc(max_turned.sem, 1)

            def score_t(it, j, e):
                n = heads * it + j - 2
                u, h = (j - 2) // 4 % turn, (j - 2) % 4
                if e == 0:
                    pe.wait_ge(*max_rows.at(n + 1))
                m = n * 2 + e
                if due(m - 1):
                    pe.wait_ge(*exped.at(m - 1))
                for i in (2 * e, 2 * e + 1):
                    last = nc.tensor.matmul(k.ps[:, 2 + i, :], k_st[:, u, h, i * P:(i + 1) * P], q_st[:, u, h, :],
                                            start=True, stop=True)
                last.then_inc(scores_t.sem, 1)

            def sum_ready(it, j):
                g = turn * it + j // 4 - 1
                if j % 4 == 2 and due(g + 1):
                    pe.wait_ge(*exped.at((g + 1) * 8))
                    pe.wait_ge(*v_in.at(g + 1))
                    if due(g):
                        pe.wait_ge(*o_out.at(g))

            def sum_up(it, j):
                back = 1 if j % 4 >= 2 else 2
                if not due(turn * it + j // 4 - back + 1):
                    return
                i, s = block_at[j % 4], (j // 4 - back) % 2
                for h in range(4):
                    last = nc.tensor.matmul(k.ps[32 * h:32 * h + 32, 6, :], v_st[:, s, i, h, :],
                                            probs[s][:, h, i, :], start=i == 0, stop=i == TB - 1)
                if i == TB - 1:
                    last.then_inc(summed.sem, 1)

            def step(it, j):
                n = heads * it + j
                score(it, j, 0)
                if due(n - 1):
                    score_t(it, j, 0)
                score(it, j, 1)
                sum_ready(it, j)
                sum_up(it, j)
                score(it, j, 2)
                if due(n):
                    turn_max(it, j)
                if due(n - 1):
                    score_t(it, j, 1)
                score(it, j, 3)

            pe.wait_ge(*ones.at(2))
            for it in range(first):
                for j in range(heads):
                    step(it, j)
            with pe.Fori(first, turns) as it:
                for j in range(heads):
                    step(it, j)
            for j in range(2):
                score_t(turns, j, 0)
                if j == 0:
                    turn_max(turns, 0)
                score_t(turns, j, 1)
                sum_up(turns, j)
            for j in range(2, 6):
                sum_ready(turns, j)
                sum_up(turns, j)

        @block.vector
        def _(dve):
            def split(it, j, c):
                n, s = heads * it + j - 1, (j - 1) % 2
                if c == 0:
                    dve.wait_ge(*maxed.at((n + 1) * TB))
                    if due(n - 1):
                        dve.wait_ge(*max_turned.at(n - 1))
                    nc.vector.tensor_copy(max_parts[:, s, :, 0], neg_max[:, s, :]).then_inc(max_split.sem, 1)
                    return
                dve.wait_ge(*max_split.at(2 * n + 1))
                nc.vector.tensor_tensor(max_parts[:, s, :, 1], neg_max[:, s, :], max_parts[:, s, :, 0],
                                        ALU.subtract).then_inc(max_split.sem, 1)

            def step(it, j):
                n, s = heads * it + j, j % 2
                if due(n - 1):
                    dve.wait_ge(*max_split.at(2 * n - 2))
                if due(n):
                    split(it, j, 0)
                for i in range(TB):
                    dve.wait_ge(*scores.at(n * TB + i + 1))
                    nc.vector.tensor_reduce(neg_max[:, s, i:i + 1], k.ps[:, score_bank[j % 2][i], :], axis=AX.X, op=ALU.max,
                                            negate=True).then_inc(maxed.sem, 1)
                    if i == 0 and due(n):
                        split(it, j, 1)

            for it in range(first):
                for j in range(heads):
                    step(it, j)
            with dve.Fori(first, turns) as it:
                for j in range(heads):
                    step(it, j)
            split(turns, 0, 0)
            split(turns, 0, 1)

        @block.scalar
        def _(act):
            def max_row(it, j):
                n = heads * it + j - 1
                u, h = (j - 1) // 4 % turn, (j - 1) % 4
                act.wait_ge(*max_turned.at(n + 1))
                nc.scalar.activation(q_st[rows:stack, u, h, :], k.ps[rows:stack, 2, :], ACT.Copy).then_inc(max_rows.sem, 1)

            def exps(it, j, e):
                n, g = heads * it + j - 2, turn * it + (j - 2) // 4
                u, h = (j - 2) // 4 % turn, (j - 2) % 4
                if h == 0 and e == 0 and due(g - 1):
                    act.wait_ge(*summed.at(g - 1))
                act.wait_ge(*scores_t.at(n * 2 + e + 1))
                nc.scalar.activation(probs[u % 2][:, h, 2 * e:2 * e + 2, :], k.ps[:, 2 + 2 * e:4 + 2 * e, :], ACT.Exp,
                                     scale=NARROW ** -0.5).then_inc(exped.sem, 1)

            def out(it, u, back):
                g, s = turn * it + u - back, (u - back) % 2
                act.wait_ge(*summed.at(g + 1))
                if due(g - 1):
                    act.wait_ge(*out_stored[s].at(8 * (turn * it + u - back - s)))
                nc.scalar.activation(o_sb[:, s, :], k.ps[:, 6, :], ACT.Copy).then_inc(o_out.sem, 1)

            def outs(it, j):
                if j % 4 == 2 and due(turn * it + j // 4 - 1):
                    out(it, j // 4, 2)

            def step(it, j):
                n = heads * it + j
                outs(it, j)
                if due(n - 1):
                    exps(it, j, 0)
                if due(n):
                    max_row(it, j)
                if due(n - 1):
                    exps(it, j, 1)

            for it in range(first):
                for j in range(heads):
                    step(it, j)
            with act.Fori(first, turns) as it:
                for j in range(heads):
                    step(it, j)
            for j in range(2):
                outs(turns, j)
                exps(turns, j, 0)
                if j == 0:
                    max_row(turns, j)
                exps(turns, j, 1)
            for j in range(2, 7):
                outs(turns, j)
    for s, n in (*((z, 48 * turns) for z in q_in + k_in), (out_stored[0], 8 * groups), (out_stored[1], 8 * groups), (ones, 2), (v_in, groups),
                 (scores, HEADS * TB), (maxed, HEADS * TB), (max_split, 2 * HEADS), (max_turned, HEADS),
                 (max_rows, HEADS), (scores_t, HEADS * 2), (exped, HEADS * 2), (summed, groups), (o_out, groups)):
        s.passed(n)
    k.end_stage()


def attend_context(k, next_weights):
    nc = k.nc
    pairs, groups, turn = HEADS // 2, HEADS // 4, 4
    per, turns, slots = 2 * turn, groups // turn, 8
    rows, stack = 6 * NARROW, 6 * NARROW + 2
    v = vx_narrow(k)
    q_st = k.big1[0:stack, 0:4096].bitcast(BF16).rearrange("p (u h t) -> p u h t", u=turn, h=4)
    k_st = k.big1[0:stack, 4096:4608].bitcast(BF16).rearrange("p (u h t) -> p u h t", u=turn, h=4)
    probs = k.big1[:, 5120:5120 + slots * N].rearrange("p (s t) -> p s t", s=slots)
    spare = k.hT[:, :, :].rearrange("p c t -> p (c t)")
    v_st = spare[:, 0:256].rearrange("p (u i d) -> p u i d", u=2, i=2)
    o_sb = spare[:, 1024:2048].rearrange("p (u t) -> p u t", u=2)
    neg_max = k.small[:, 0:16].rearrange("p (s x) -> p s x", s=2)
    max_parts = k.small[:, 16:32].bitcast(BF16).rearrange("p (s x c) -> p s x c", s=2, c=2)

    q_in, k_in = [k.semaphore(f"q_in_{u}") for u in range(turn)], [k.semaphore(f"k_in_{u}") for u in range(turn)]
    out_stored = [k.semaphore(f"out_stored_{u}") for u in range(2)]
    cleared, ones, v_in = k.semaphore("cleared"), k.semaphore("ones_made"), k.semaphore("v_staged")
    scores, maxed, max_split = k.semaphore("scores"), k.semaphore("maxed"), k.semaphore("max_split")
    max_turned, max_rows = k.semaphore("max_turned"), k.semaphore("max_rows")
    scores_t, exped, summed, o_out = k.semaphore("scores_t"), k.semaphore("exped"), k.semaphore("summed"), k.semaphore("o_out")

    with nc.Block() as block:
        @block.sync
        def _(sp):
            def load(it, u):
                g = turn * it + u
                if due(g - turn + 1):
                    sp.wait_ge(*scores_t.at((g - turn + 1) * 2))
                for p0, parts in ((0, 3), (3, 2), (5, 1)):
                    sp.dma_start(q_st[p0 * NARROW:(p0 + parts) * NARROW, u, :, :],
                                 k.q_parts[bass.ds(g, 1), 0:parts].rearrange("g c (d h) t -> (g c d) h t", h=4)).then_inc(q_in[u].sem, 16)
                    src = k.kx_parts[bass.ds(g, 1), (0, 3, 5).index(p0)].rearrange("g (d h) t -> g d (h t)", h=4)
                    sp.dma_start(k_st[p0 * NARROW:(p0 + parts) * NARROW, u, :, :].rearrange("p h t -> p (h t)"),
                                 src.broadcast_to([parts, NARROW, 4 * M])).then_inc(k_in[u].sem, 16)

            def store(g, s):
                sp.wait_ge(*o_out.at(g + 1))
                sp.dma_start(k.o_sums[bass.ds(g * 4, 4)].rearrange("h r t -> (h r) t"), o_sb[:, s, :]).then_inc(out_stored[s].sem, 16)

            def groups_of(it):
                for u in range(turn):
                    load(it, u)
                    if due(turn * it + u - turn):
                        store(turn * it + u - turn - 1, (u + 1) % 2)

            for u in range(turn):
                load(0, u)
            k.load_weights(sp, next_weights)
            groups_of(1)
            with sp.Fori(2, turns) as it:
                groups_of(it)
            for g in range(groups - turn - 1, groups):
                store(g, g % 2)
            for s in range(2):
                sp.wait_ge(*out_stored[s].at(16 * (groups // 2)))

        @block.gpsimd
        def _(pool):
            nc.gpsimd.memset(k_st[rows:stack, :, :, :], 1.0).then_inc(ones.sem, 1)
            pool.wait_ge(*ones.at(1))
            nc.gpsimd.memset(v_st, 0.0).then_inc(cleared.sem, 1)
            pool.wait_ge(*cleared.at(1))
            for a in range(2):
                nc.gpsimd.memset(v_st[a * M:(a + 1) * M, :, :, (2 * a + 1) * NARROW:(2 * a + 2) * NARROW], 1.0).then_inc(ones.sem, 1)
            pool.wait_ge(*ones.at(3))

            def stage(it, u):
                g = turn * it + u
                if due(g - 1):
                    pool.wait_ge(*summed.at(g - 1))
                for a in range(2):
                    nc.gpsimd.tensor_copy(v_st[a * M:(a + 1) * M, u % 2, :, 2 * a * NARROW:(2 * a + 1) * NARROW],
                                          v[a * M:(a + 1) * M, bass.ds(g * 2, 2), :]).then_inc(v_in.sem, 1)

            for u in range(turn):
                stage(0, u)
            with pool.Fori(1, turns) as it:
                for u in range(turn):
                    stage(it, u)

        @block.tensor
        def _(pe):
            def score(it, j):
                n, u, i = per * it + j, j // 2, j % 2
                if i == 0:
                    pe.wait_ge(*q_in[u].at(48 * it + 48))
                    pe.wait_ge(*k_in[u].at(48 * it + 48))
                if due(n - 1):
                    pe.wait_ge(*maxed.at(n - 1))
                for x in range(2 * TB):
                    h, a = 2 * i + x // TB, x % TB
                    last = nc.tensor.matmul(k.ps[:, j % 2, x * M:(x + 1) * M], q_st[0:rows, u, h, a * P:(a + 1) * P],
                                            k_st[0:rows, u, h, :], start=True, stop=True)
                last.then_inc(scores.sem, 1)

            def turn_max(it, j):
                n = per * it + j - 1
                pe.wait_ge(*max_split.at(2 * n + 2))
                if due(n):
                    pe.wait_ge(*max_rows.at(n))
                for x in range(2 * TB):
                    last = nc.tensor.matmul(k.ps[rows:stack, 4 + x // TB, x % TB * P:(x % TB + 1) * P],
                                            max_parts[:, (j - 1) % 2, x, :], k.identb[:, :], start=True, stop=True)
                last.then_inc(max_turned.sem, 1)

            def score_t(it, j):
                n = per * it + j - 2
                u, i = (j - 2) // 2 % turn, (j - 2) % 2
                pe.wait_ge(*max_rows.at(n + 1))
                if due(n - 1):
                    pe.wait_ge(*exped.at(n - 1))
                for a in range(2):
                    last = nc.tensor.matmul(k.ps[a * M:(a + 1) * M, 2 + j % 2, :], k_st[:, u, 2 * i + a, :], q_st[:, u, 2 * i + a, :],
                                            start=True, stop=True)
                last.then_inc(scores_t.sem, 1)

            def sum_up(it, j):
                g, s, half = turn * it + (j - 5) // 2, (j - 5) // 2 % 2, (j - 5) % 2
                if half == 0:
                    pe.wait_ge(*exped.at(2 * g + 2))
                    pe.wait_ge(*v_in.at(2 * g + 2))
                    if due(g - 1):
                        pe.wait_ge(*o_out.at(g - 1))
                ts = slice(half * N // 2, (half + 1) * N // 2)
                for i in range(2):
                    last = nc.tensor.matmul(k.ps[64 * i:64 * i + 64, 6 + s, ts], v_st[:, s, i, :],
                                            probs[:, ((j - 5) // 2 * 2 + i) % slots, ts], start=True, stop=True)
                if half:
                    last.then_inc(summed.sem, 1)

            def step(it, j, scoring=True):
                n = per * it + j
                if scoring:
                    score(it, j)
                if due(n - 4):
                    sum_up(it, j)
                if due(n) and (scoring or j < 1):
                    turn_max(it, j)
                if due(n - 1) and (scoring or j < 2):
                    score_t(it, j)

            pe.wait_ge(*ones.at(3))
            for j in range(per):
                step(0, j)
            with pe.Fori(1, turns) as it:
                for j in range(per):
                    step(it, j)
            for j in range(5):
                step(turns, j, scoring=False)

        @block.vector
        def _(dve):
            def out(it, j):
                g, s = turn * it + (j - 7) // 2, (j - 7) // 2 % 2
                dve.wait_ge(*summed.at(g + 1))
                if due(g - 1):
                    dve.wait_ge(*out_stored[s].at(8 * (g - s)))
                nc.vector.tensor_copy(o_sb[:, s, :], k.ps[:, 6 + s, :]).then_inc(o_out.sem, 1)

            def maxima(it, j):
                n, s = per * it + j, j % 2
                if due(n - 1):
                    dve.wait_ge(*max_split.at(2 * n - 2))
                    dve.wait_ge(*max_turned.at(n - 1))
                dve.wait_ge(*scores.at(n + 1))
                nc.vector.tensor_reduce(neg_max[:, s, :], k.ps[:, s, :].rearrange("p (x m) -> p x m", m=M), axis=AX.X, op=ALU.max,
                                        negate=True).then_inc(maxed.sem, 1)
                dve.wait_ge(*maxed.at(n + 1))
                nc.vector.tensor_copy(max_parts[:, s, :, 0], neg_max[:, s, :]).then_inc(max_split.sem, 1)
                dve.wait_ge(*max_split.at(2 * n + 1))
                nc.vector.tensor_tensor(max_parts[:, s, :, 1], neg_max[:, s, :], max_parts[:, s, :, 0],
                                        ALU.subtract).then_inc(max_split.sem, 1)

            def step(it, j):
                if j % 2 and due(per * it + j - 6):
                    out(it, j)
                maxima(it, j)

            for it in range(2):
                for j in range(per):
                    step(it, j)
            with dve.Fori(2, turns) as it:
                for j in range(per):
                    step(it, j)
            for j in (1, 3, 5):
                out(turns, j)

        @block.scalar
        def _(act):
            def copy_rows(it, j):
                n = per * it + j - 1
                u, i = (j - 1) // 2 % turn, (j - 1) % 2
                act.wait_ge(*max_turned.at(n + 1))
                nc.scalar.activation(q_st[rows:stack, u, 2 * i:2 * i + 2, :], k.ps[rows:stack, 4:6, :], ACT.Copy).then_inc(max_rows.sem, 1)

            def exps(it, j):
                n = per * it + j - 2
                if due(n - slots + 1):
                    act.wait_ge(*summed.at(turn * it + (j - 2 - slots) // 2 + 1))
                act.wait_ge(*scores_t.at(n + 1))
                nc.scalar.activation(probs[:, (j - 2) % slots, :], k.ps[:, 2 + j % 2, :], ACT.Exp, scale=NARROW ** -0.5).then_inc(exped.sem, 1)

            def step(it, j):
                n = per * it + j
                if due(n):
                    copy_rows(it, j)
                if due(n - 1):
                    exps(it, j)

            for it in range(2):
                for j in range(per):
                    step(it, j)
            with act.Fori(2, turns) as it:
                for j in range(per):
                    step(it, j)
            copy_rows(turns, 0)
            exps(turns, 0)
            exps(turns, 1)
    for s in q_in + k_in:
        s.passed(48 * turns)
    for s in out_stored:
        s.passed(8 * groups)
    for s, n in ((cleared, 1), (ones, 3), (v_in, 2 * groups), (scores, pairs), (maxed, pairs), (max_split, 2 * pairs),
                 (max_turned, pairs), (max_rows, pairs), (scores_t, pairs), (exped, pairs), (summed, groups), (o_out, groups)):
        s.passed(n)
    k.end_stage()


def rows_at(k, n):
    return k.big2[:, 12288:12288 + n * D].rearrange("p (n d) -> p n d", n=n)


def chunks_beside(t, per_tile):
    b, i = t // TB + 1, t % TB
    return [(b, c) for c in range(int(i * per_tile), int((i + 1) * per_tile))] if b < B else []


def project_out(k, next_weights, w, bias, gate, wide, norm):
    nc = k.nc
    chunks = MID // P if wide else C
    loaded = [k.semaphore(f"out_loaded_{b}") for b in range(B)]
    sums_in, inverse, spread, divided = k.semaphore("sums_loaded"), k.semaphore("inverse"), k.semaphore("inverse_spread"), k.semaphore("divided")
    row_made, row_in, row_scaled, biased = k.semaphore("row_made"), k.semaphore("row_in"), k.semaphore("row_scaled"), k.semaphore("biased")
    product, scaled, added = k.semaphore("product"), k.semaphore("scaled"), k.semaphore("added")
    o = k.big1[:, 0:chunks * T].rearrange("p (c t) -> p c t", c=chunks)
    norm = norm and Norm(k, norm, ((6, 7),))
    sums = k.big2[:, 1024:1024 + N]
    upper = slice(HEADS, 2 * HEADS)
    two_parts, third = k.big2[:, 1536:1792].bitcast(BF16), k.big2[upper, 1792:2048].bitcast(BF16)
    left = k.big2[:, 2048:2048 + N]
    parted = k.semaphore("inverse_parted")
    size = WIDE if wide else NARROW
    select = k.big2[:, 4096:4096 + HEADS * size // 2].bitcast(BF16)
    select_made = k.semaphore("select_made")
    per_tile = chunks / TB
    gates, gated_bias = rows_at(k, 2 * B)[:, 0:B, :], rows_at(k, 2 * B)[:, B:2 * B, :]
    tmp = k.big2[:, 0:2 * D].rearrange("p (s d) -> p s d", s=2)
    bias_row = k.rows[:, 0, :]
    n_rows = (bias is not None) + (B if gate is not None else 0)
    with nc.Block() as block:
        @block.sync
        def _(sp):
            for half in (slice(0, HEADS), upper):
                sp.dma_start(sums[half], (k.o_wide if wide else k.o_sums)[:, size, :]).then_inc(sums_in.sem, 16)
            for b in range(B):
                cols = slice(b * N, (b + 1) * N)
                for c in range(2):
                    if wide:
                        src = k.o_wide[b * H + c:(b + 1) * H:2, 0:WIDE, :].rearrange("h d t -> d h t")
                        sp.dma_start(o[c * WIDE:(c + 1) * WIDE, :, cols], src).then_inc(loaded[b].sem, 16)
                    else:
                        h = b * H + c * 8
                        sp.dma_start(o[:, c, cols], k.o_sums[h:h + 8, 0:NARROW, :]).then_inc(loaded[b].sem, 16)
            k.load_weights(sp, next_weights)

        @block.tensor
        def _(pe):
            pe.wait_ge(*k.weights_due()) if k.due else None
            n = 0
            if bias is not None:
                set_row(k, k.ps[:, 7, :], [k.v(bias, c) for c in range(C)]).then_inc(row_made.sem, 1)
                n += 1
            if gate is not None:
                for b in range(B):
                    if n:
                        pe.wait_ge(*row_in.at(n))
                    set_row(k, k.ps[:, 7, :], [k.mod[:, gate + c, b:b + 1] for c in range(C)]).then_inc(row_made.sem, 1)
                    n += 1
            wt = k.where[w] if w else None
            pe.wait_ge(*parted.at(4))

            def spread_out(b, c):
                u = b * chunks + c
                if u >= 2:
                    pe.wait_ge(*divided.at(u - 1))
                h = b * H + c * (P // size)
                if c == 0:
                    pe.wait_ge(*select_made.at(2 * b + 2))
                cols = slice(h * size, h * size + P)
                nc.tensor.matmul(k.ps[:, 4 + u % 2, :], select[:, cols], two_parts, start=True, stop=False)
                nc.tensor.matmul(k.ps[:, 4 + u % 2, :], select[upper, cols], third, start=False, stop=True).then_inc(spread.sem, 1)

            for c in range(chunks):
                spread_out(0, c)
            for t in range(TILES):
                for b, c in chunks_beside(t, per_tile):
                    spread_out(b, c)
                if t % TB == 0:
                    pe.wait_ge(*divided.at(chunks * (t // TB + 1)))
                if t >= 4:
                    pe.wait_ge(*added.at(t - 3))
                for c in range(chunks):
                    if w:
                        last = nc.tensor.matmul(k.ps[:, t % 4, 0:D], o[:, c, t * P:(t + 1) * P], wt[:, c, :],
                                                start=c == 0, stop=c == chunks - 1)
                    else:
                        last = nc.tensor.transpose(k.ps[:, t % 4, c * P:(c + 1) * P], o[:, c, t * P:(t + 1) * P], k.ident[:, :])
                last.then_inc(product.sem, 1)
                if norm and t % TB == TB - 1 and t >= TB:
                    if t < 2 * TB and n_rows:
                        pe.wait_ge(*row_in.at(n_rows))
                    norm.pe_turn(pe, t // TB - 1)
            if norm:
                norm.pe_turn(pe, B - 1)

        @block.gpsimd
        def _(pool):
            if bias is None:
                return
            pool.wait_ge(*row_in.at(n_rows))
            for b in range(B):
                row = bias_row
                if gate is not None:
                    nc.gpsimd.tensor_tensor(gated_bias[:, b, :], gates[:, b, :], bias_row, ALU.mult).then_inc(row_scaled.sem, 1)
                    pool.wait_ge(*row_scaled.at(b + 1))
                    row = gated_bias[:, b, :]
                xb = k.x[:, b * TB:(b + 1) * TB, :]
                nc.gpsimd.tensor_tensor(xb, xb, row.unsqueeze(1).broadcast_to([P, TB, D]), ALU.add).then_inc(biased.sem, 1)

        @block.scalar
        def _(act):
            for b in range(B):
                for at in (0, HEADS):
                    ones = k.identb[at:at + HEADS, at + b * H:at + (b + 1) * H].unsqueeze(2).broadcast_to([HEADS, H, size])
                    nc.scalar.activation(select[at:at + HEADS, b * H * size:(b + 1) * H * size].rearrange("p (h i) -> p h i", i=size),
                                         ones, ACT.Copy).then_inc(select_made.sem, 1)
            for r in range(n_rows):
                act.wait_ge(*row_made.at(r + 1))
                dst = bias_row if bias is not None and r == 0 else gates[:, r - (bias is not None), :]
                nc.scalar.activation(dst, k.ps[:, 7, 0:D], ACT.Copy).then_inc(row_in.sem, 1)
            if norm:
                for b in range(B):
                    norm.act_root(act, b)
                    if b:
                        norm.act_modulate(act, b - 1)
                norm.act_modulate(act, B - 1)

        @block.vector
        def _(dve):
            if norm:
                norm.dve_coefficients(dve)
            dve.wait_ge(*sums_in.at(32))
            nc.vector.reciprocal(sums, sums).then_inc(inverse.sem, 1)
            dve.wait_ge(*inverse.at(1))
            nc.vector.tensor_copy(two_parts, sums).then_inc(parted.sem, 1)
            dve.wait_ge(*parted.at(1))
            nc.vector.tensor_tensor(left, sums, two_parts, ALU.subtract).then_inc(parted.sem, 1)
            dve.wait_ge(*parted.at(2))
            nc.vector.tensor_copy(two_parts[upper], left[upper]).then_inc(parted.sem, 1)
            dve.wait_ge(*parted.at(3))
            nc.vector.tensor_tensor(third, left[upper], two_parts[upper], ALU.subtract).then_inc(parted.sem, 1)

            def divide(b, c):
                u, cols = b * chunks + c, slice(b * N, (b + 1) * N)
                if c == 0:
                    dve.wait_ge(*loaded[b].at(32))
                dve.wait_ge(*spread.at(u + 1))
                nc.vector.tensor_tensor(o[:, c, cols], o[:, c, cols], k.ps[:, 4 + u % 2, :], ALU.mult).then_inc(divided.sem, 1)

            for c in range(chunks):
                divide(0, c)
            if gate is not None:
                dve.wait_ge(*row_in.at(n_rows))
            for t in range(TILES):
                for b, c in chunks_beside(t, per_tile):
                    divide(b, c)
                if bias is not None and t % TB == 0:
                    dve.wait_ge(*biased.at(t // TB + 1))
                dve.wait_ge(*product.at(t + 1))
                src = k.ps[:, t % 4, 0:D]
                if gate is not None:
                    if t >= 2:
                        dve.wait_ge(*added.at(t - 1))
                    nc.vector.tensor_tensor(tmp[:, t % 2, :], src, gates[:, t // TB, :], ALU.mult).then_inc(scaled.sem, 1)
                    dve.wait_ge(*scaled.at(t + 1))
                    src = tmp[:, t % 2, :]
                nc.vector.tensor_tensor(k.x[:, t, :], src, k.x[:, t, :], ALU.add).then_inc(added.sem, 1)
                if norm and t:
                    dve.wait_ge(*added.at(t))
                    norm.dve_stats(t - 1)
                    if t % TB == 0:
                        norm.dve_variances(dve, t // TB - 1)
                    if t % TB == 1 and t > TB:
                        norm.dve_rows(dve, t // TB - 1)
            if norm:
                dve.wait_ge(*added.at(TILES))
                norm.dve_stats(TILES - 1)
                norm.dve_variances(dve, B - 1)
                norm.dve_rows(dve, B - 1)
    for b in range(B):
        loaded[b].passed(32)
    for s, n in ((sums_in, 32), (select_made, 2 * B), (inverse, 1), (parted, 4), (spread, B * chunks), (divided, B * chunks), (row_made, n_rows), (row_in, n_rows),
                 (row_scaled, B if bias is not None and gate is not None else 0), (biased, B if bias is not None else 0),
                 (product, TILES), (scaled, TILES if gate is not None else 0), (added, TILES)):
        s.passed(n)
    if norm:
        norm.passed()
    k.end_stage()


def project_cross(k, next_weights, pre, wq, wk, wv, bq, bk, bv):
    nc = k.nc
    split = Split(k)
    product, v_product, v_read = k.semaphore("product"), k.semaphore("v_product"), k.semaphore("v_read")
    row_made, row_in, pre_made, pre_in = k.semaphore("row_made"), k.semaphore("row_in"), k.semaphore("pre_made"), k.semaphore("pre_in")
    units = [("k", m, 0) for m in range(C)] + [("q", m, b) for m in range(C) for b in range(B)]
    split.plan([6 if kind == "k" else 2 for kind, _, _ in units])
    source = k.ctx2T if pre else k.ctxT
    depth = [P, P] if pre else [P, DC - P]
    v = vx_narrow(k)

    def width(kind):
        return B * M if kind == "k" else N

    with nc.Block() as block:
        @block.sync
        def _(sp):
            k.load_weights(sp, next_weights)
            for u, (kind, m, b) in enumerate(units):
                if kind == "k":
                    split.store_context(sp, u, m)
                else:
                    split.store(sp, u, k.q_parts, b * 4 + m * 2)
            split.all_stored(sp)

        @block.tensor
        def _(pe):
            pe.wait_ge(*k.weights_due())
            if bv:
                set_row(k, k.ps[:, 7, :], [k.v(bv[0], bv[1] + c) for c in range(C)]).then_inc(row_made.sem, 1)
            if pre:
                wt = k.where[pre[0]]
                for m in range(C):
                    for c, r in enumerate((P, DC - P)):
                        last = nc.tensor.matmul(k.ps[:, 6, m * B * M:(m + 1) * B * M], wt[0:r, c, m * P:(m + 1) * P],
                                                k.ctxT[0:r, c, :], start=c == 0, stop=c == 1)
                last.then_inc(pre_made.sem, 1)
                pe.wait_ge(*pre_in.at(C))
            for u, (kind, m, b) in enumerate(units):
                if u >= 4:
                    pe.wait_ge(*split.whole_ready.at(u - 3))
                for c in range(C):
                    if kind == "k":
                        r = depth[c]
                        last = nc.tensor.matmul(k.ps[:, u % 4, 0:B * M], k.where[wk][0:r, c, m * P:(m + 1) * P], source[0:r, c, :],
                                                start=c == 0, stop=c == C - 1)
                    else:
                        last = nc.tensor.matmul(k.ps[:, u % 4, :], k.where[wq][:, c, m * P:(m + 1) * P],
                                                k.hT[:, c, b * N:(b + 1) * N], start=c == 0, stop=c == C - 1)
                last.then_inc(product.sem, 1)
            for b in range(B):
                if b >= 2:
                    pe.wait_ge(*v_read.at(2 * (b - 1)))
                for half in (slice(0, M), slice(M, 2 * M)):
                    for c in range(C):
                        r = depth[c]
                        last = nc.tensor.matmul(k.ps[half, 4 + b % 2, 0:D], source[0:r, c, b * M:(b + 1) * M], k.where[wv][0:r, c, :],
                                                start=c == 0, stop=c == C - 1)
                last.then_inc(v_product.sem, 1)

        @block.scalar
        def _(act):
            if pre:
                act.wait_ge(*pre_made.at(1))
                for m in range(C):
                    nc.scalar.activation(k.ctx2T[:, m, :], k.ps[:, 6, m * B * M:(m + 1) * B * M], ACT.Identity,
                                         bias=k.v(pre[1], m)).then_inc(pre_in.sem, 1)
            for u, (kind, m, b) in enumerate(units):
                bias = bk if kind == "k" else bq
                act.wait_ge(*product.at(u + 1))
                split.act_whole(act, u, k.ps[:, u % 4, 0:width(kind)], k.v(bias[0], bias[1] + m) if bias else 0.0, width(kind))
                split.act_first(act, u, width(kind))

        @block.vector
        def _(dve):
            if bv:
                dve.wait_ge(*row_made.at(1))
                nc.vector.tensor_copy(k.rows[:, 0, :], k.ps[:, 7, 0:D]).then_inc(row_in.sem, 1)
            for u, (kind, _, _) in enumerate(units):
                split.dve_rest(dve, u, width(kind))
            if bv:
                dve.wait_ge(*row_in.at(1))
            for b in range(B):
                dve.wait_ge(*v_product.at(b + 1))
                for a, half in enumerate((slice(0, M), slice(M, 2 * M))):
                    src = k.ps[half, 4 + b % 2, 0:D].rearrange("p (n a d) -> p n a d", a=2, d=NARROW)[:, :, a, :]
                    dst = v[half, b * H // 2:(b + 1) * H // 2, :]
                    if bv:
                        row = k.rows[half, 0, :].rearrange("p (n a d) -> p n a d", a=2, d=NARROW)[:, :, a, :]
                        nc.vector.tensor_tensor(dst, src, row, ALU.add).then_inc(v_read.sem, 1)
                    else:
                        nc.vector.tensor_copy(dst, src).then_inc(v_read.sem, 1)
    for s, n in ((product, len(units)), (v_product, B), (v_read, 2 * B), (row_made, 1 if bv else 0), (row_in, 1 if bv else 0),
                 (pre_made, 1 if pre else 0), (pre_in, C if pre else 0)):
        s.passed(n)
    split.passed()
    k.end_stage()


def feed_forward(k, next_weights, up, gate_up, down, b_up, b_down, func, gate, norm):
    nc = k.nc
    product, halved, hidden_ready = k.semaphore("product"), k.semaphore("activated"), k.semaphore("hidden")
    row_made, row_in, biased = k.semaphore("row_made"), k.semaphore("row_in"), k.semaphore("biased")
    down_product, scaled, added, final = k.semaphore("down_product"), k.semaphore("scaled"), k.semaphore("added"), k.semaphore("final_stored")
    hidden = k.big1[:, 0:2 * FC * N].rearrange("p (s m t) -> p s m t", s=2, m=FC)
    half = k.big1[:, 8192:8192 + 2 * N].rearrange("p (s t) -> p s t", s=2)
    gates = rows_at(k, B)
    tmp = k.big2[:, 0:2 * D].rearrange("p (s d) -> p s d", s=2)
    n_rows = (b_down is not None) + (B if gate is not None else 0)
    last_stage = next_weights is None
    norm = norm and Norm(k, norm, ((6, 7),))
    with nc.Block() as block:
        @block.sync
        def _(sp):
            if not last_stage:
                k.load_weights(sp, next_weights)
                return
            out = k.out.rearrange("b (t p) d -> p (b t) d", p=P)
            for t in range(0, TILES, 2):
                sp.wait_ge(*added.at(t + 2))
                sp.dma_start(out[:, t:t + 2, :], k.x[:, t:t + 2, :]).then_inc(final.sem, 16)
            sp.wait_ge(*final.at(16 * TILES // 2))

        @block.tensor
        def _(pe):
            pe.wait_ge(*k.weights_due())
            n = 0
            if b_down is not None:
                set_row(k, k.ps[:, 7, :], [k.v(b_down, c) for c in range(C)]).then_inc(row_made.sem, 1)
                n += 1
            if gate is not None:
                for b in range(B):
                    if n:
                        pe.wait_ge(*row_in.at(n))
                    set_row(k, k.ps[:, 7, :], [k.mod[:, gate + c, b:b + 1] for c in range(C)]).then_inc(row_made.sem, 1)
                    n += 1

            def ups(b):
                for m in range(FC):
                    u = b * FC + m
                    if gate_up:
                        if u >= 2:
                            pe.wait_ge(*hidden_ready.at(u - 1))
                    elif u >= 4:
                        pe.wait_ge(*hidden_ready.at(u - 3))
                    for i, name in enumerate((up, gate_up) if gate_up else (up,)):
                        bank = 2 * (u % 2) + i if gate_up else u % 4
                        for c in range(C):
                            last = nc.tensor.matmul(k.ps[:, bank, :], k.where[name][:, c, m * P:(m + 1) * P],
                                                    k.hT[:, c, b * N:(b + 1) * N], start=c == 0, stop=c == C - 1)
                    last.then_inc(product.sem, 1)

            def downs(b):
                pe.wait_ge(*hidden_ready.at((b + 1) * FC))
                for i in range(TB):
                    t = b * TB + i
                    if t >= 2:
                        pe.wait_ge(*added.at(t - 1))
                    for m in range(FC):
                        last = nc.tensor.matmul(k.ps[:, 4 + t % 2, 0:D], hidden[:, b % 2, m, i * P:(i + 1) * P], k.where[down][:, m, :],
                                                start=m == 0, stop=m == FC - 1)
                    last.then_inc(down_product.sem, 1)

            for b in range(B):
                ups(b)
                if b:
                    downs(b - 1)
                if norm and b >= 2:
                    if b == 2 and n_rows:
                        pe.wait_ge(*row_in.at(n_rows))
                    norm.pe_turn(pe, b - 2)
            downs(B - 1)
            if norm:
                norm.pe_turn(pe, B - 2)
                norm.pe_turn(pe, B - 1)

        @block.gpsimd
        def _(pool):
            if b_down is None:
                return
            pool.wait_ge(*row_in.at(1))
            for b in range(B):
                xb = k.x[:, b * TB:(b + 1) * TB, :]
                nc.gpsimd.tensor_tensor(xb, xb, k.rows[:, 0:1, :].broadcast_to([P, TB, D]), ALU.add).then_inc(biased.sem, 1)

        @block.scalar
        def _(act):
            for r in range(n_rows):
                act.wait_ge(*row_made.at(r + 1))
                dst = k.rows[:, 0, :] if b_down is not None and r == 0 else gates[:, r - (b_down is not None), :]
                nc.scalar.activation(dst, k.ps[:, 7, 0:D], ACT.Copy).then_inc(row_in.sem, 1)
            for b in range(B):
                if b >= 2:
                    act.wait_ge(*down_product.at((b - 1) * TB))
                for m in range(FC):
                    u = b * FC + m
                    if norm and b >= 2 and m == 2:
                        norm.act_root(act, b - 2)
                    act.wait_ge(*product.at(u + 1))
                    if gate_up:
                        if u >= 2:
                            act.wait_ge(*hidden_ready.at(u - 1))
                        nc.scalar.activation(half[:, u % 2, :], k.ps[:, 2 * (u % 2), :], func).then_inc(halved.sem, 1)
                    else:
                        nc.scalar.activation(hidden[:, b % 2, m, :], k.ps[:, u % 4, :], func,
                                             bias=k.v(b_up, m)).then_inc(hidden_ready.sem, 1)
                if norm and b >= 2:
                    norm.act_modulate(act, b - 2)
            if norm:
                for b in (B - 2, B - 1):
                    norm.act_root(act, b)
                    norm.act_modulate(act, b)

        @block.vector
        def _(dve):
            def mix(b):
                for m in range(FC):
                    u = b * FC + m
                    dve.wait_ge(*halved.at(u + 1))
                    nc.vector.tensor_tensor(hidden[:, b % 2, m, :], k.ps[:, 2 * (u % 2) + 1, :], half[:, u % 2, :],
                                            ALU.mult).then_inc(hidden_ready.sem, 1)

            def add(b):
                for i in range(TB):
                    t = b * TB + i
                    if b_down is not None and i == 0:
                        dve.wait_ge(*biased.at(b + 1))
                    dve.wait_ge(*down_product.at(t + 1))
                    src = k.ps[:, 4 + t % 2, 0:D]
                    if gate is not None:
                        if t >= 2:
                            dve.wait_ge(*added.at(t - 1))
                        nc.vector.tensor_tensor(tmp[:, t % 2, :], src, gates[:, b, :], ALU.mult).then_inc(scaled.sem, 1)
                        dve.wait_ge(*scaled.at(t + 1))
                        src = tmp[:, t % 2, :]
                    nc.vector.tensor_tensor(k.x[:, t, :], src, k.x[:, t, :], ALU.add).then_inc(added.sem, 1)
                    if norm:
                        dve.wait_ge(*added.at(t + 1))
                        norm.dve_stats(t)
                if norm:
                    norm.dve_variances(dve, b)
                    norm.dve_rows(dve, b)

            if norm:
                norm.dve_coefficients(dve)
            if gate is not None:
                dve.wait_ge(*row_in.at(n_rows))
            for b in range(B):
                if gate_up:
                    mix(b)
                if b:
                    add(b - 1)
            add(B - 1)
    for s, n in ((product, B * FC), (halved, B * FC if gate_up else 0), (hidden_ready, B * FC), (row_made, n_rows), (row_in, n_rows),
                 (biased, B if b_down is not None else 0), (down_product, TILES), (scaled, TILES if gate is not None else 0),
                 (added, TILES), (final, 8 * TILES if last_stage else 0)):
        s.passed(n)
    if norm:
        norm.passed()
    k.end_stage()


def normalise_heads(k, next_weights, shift_at, scale_at, eps):
    nc = k.nc
    split = Split(k)
    row_made, row_in = k.semaphore("row_made"), k.semaphore("row_in")
    stats, var, root, rstd, normed = k.semaphore("stats"), k.semaphore("variances"), k.semaphore("roots"), k.semaphore("rstd"), k.semaphore("normed_rows")
    h_scaled, h_ready, v_copied = k.semaphore("h_scaled"), k.semaphore("h_ready"), k.semaphore("v_copied")
    h_sum, h_mean, h_centred, h_squared = k.semaphore("h_sum"), k.semaphore("h_mean"), k.semaphore("h_centred"), k.semaphore("h_squared")
    h_var, h_root, h_rstd, h_normed, turned = k.semaphore("h_var"), k.semaphore("h_root"), k.semaphore("h_rstd"), k.semaphore("h_normed"), k.semaphore("transposed")
    st = k.small[:, 0:96].rearrange("p (t s) -> p t s", s=6)
    mv = k.small[:, 96:128].rearrange("p (t s) -> p t s", s=2)
    sd, rs = k.small[:, 128:144], k.small[:, 144:160]
    hs, hm, hv, hsd, hr = (k.small[:, 160 + 64 * i:224 + 64 * i] for i in range(5))
    xn = k.big1[:, 6144:7168].rearrange("p (i d) -> p i d", i=TB)
    h1 = k.big1[:, 7168:8192].rearrange("p (i d) -> p i d", i=TB)
    h = k.big1[:, 8192:10240].rearrange("p (s i d) -> p s i d", s=2, i=TB)
    hc = k.big1[:, 10240:11264]
    sq = k.big1[:, 11264:12288]
    hn = k.big1[:, 12288:14336].rearrange("p (s j) -> p s j", s=2)
    rows = rows_at(k, 2 * B)
    v = v_narrow(k)
    units = [(b, c, kind) for b in range(B) for c in range(C) for kind in range(2)]
    split.plan([2] * len(units))

    def per_head(flat):
        return flat.unsqueeze(2).broadcast_to([P, TB * H, NARROW])

    with nc.Block() as block:
        @block.sync
        def _(sp):
            k.load_weights(sp, next_weights)
            for u, (b, c, kind) in enumerate(units):
                split.store(sp, u, (k.q_parts, k.k_parts)[kind], b * 4 + c * 2)
            split.all_stored(sp)

        @block.tensor
        def _(pe):
            for r in range(2 * B):
                b, at = r // 2, (scale_at, shift_at)[r % 2]
                if r >= 2:
                    pe.wait_ge(*row_in.at(r - 1))
                set_row(k, k.ps[:, 6 + r % 2, :], [k.mod[:, at + c, b:b + 1] for c in range(C)]).then_inc(row_made.sem, 1)
            for b in range(B):
                pe.wait_ge(*h_normed.at(b + 1))
                if b >= 2:
                    pe.wait_ge(*split.whole_ready.at(4 * (b - 1)))
                for c in range(C):
                    for i in range(TB):
                        src = hn[:, b % 2, i * D + c * P:i * D + (c + 1) * P]
                        last = nc.tensor.transpose(k.ps[:, 2 * (b % 2) + c, i * P:(i + 1) * P], src, k.ident[:, :])
                last.then_inc(turned.sem, 1)

        @block.gpsimd
        def _(pool):
            for b in range(B):
                pool.wait_ge(*h_ready.at(b + 1))
                nc.gpsimd.tensor_copy(v[:, b].rearrange("p g i d -> p i g d"),
                                      h[:, b % 2].rearrange("p i (g d) -> p i g d", g=4)).then_inc(v_copied.sem, 1)

        @block.scalar
        def _(act):
            for r in range(2 * B):
                act.wait_ge(*row_made.at(r + 1))
                nc.scalar.activation(rows[:, r, :], k.ps[:, 6 + r % 2, 0:D], ACT.Identity, bias=1.0 if r % 2 == 0 else 0.0).then_inc(row_in.sem, 1)
            act.wait_ge(*var.at(TILES))
            nc.scalar.activation(sd, mv[:, :, 1], ACT.Sqrt, bias=k.eps[:, eps:eps + 1]).then_inc(root.sem, 1)

            def parts(b):
                act.wait_ge(*turned.at(b + 1))
                for u in range(4 * b, 4 * b + 4):
                    _, c, kind = units[u]
                    w, bias = (("L3_qn_w", "L3_qn_b"), ("L3_kn_w", "L3_kn_b"))[kind]
                    split.act_whole(act, u, k.ps[:, 2 * (b % 2) + c, :], k.v(bias), N, scale=k.v(w))
                    split.act_first(act, u, N)

            for b in range(B):
                act.wait_ge(*h_centred.at(b + 1))
                nc.scalar.activation(sq, hc, ACT.Square).then_inc(h_squared.sem, 1)
                act.wait_ge(*h_var.at(b + 1))
                nc.scalar.activation(hsd, hv, ACT.Sqrt, bias=k.eps[:, eps:eps + 1], scale=1.0 / NARROW).then_inc(h_root.sem, 1)
                if b:
                    parts(b - 1)
            parts(B - 1)

        @block.vector
        def _(dve):
            for t in range(TILES):
                nc.vector.bn_stats(st[:, t, :], k.x[:, t, :]).then_inc(stats.sem, 1)
            for t in range(TILES):
                dve.wait_ge(*stats.at(t + 1))
                nc.vector.bn_aggr(mv[:, t, :], st[:, t, :]).then_inc(var.sem, 1)
            dve.wait_ge(*root.at(1))
            nc.vector.reciprocal(rs, sd).then_inc(rstd.sem, 1)
            dve.wait_ge(*rstd.at(1))
            dve.wait_ge(*row_in.at(2 * B))
            for b in range(B):
                if b:
                    dve.wait_ge(*h_scaled.at(b))
                for i in range(TB):
                    t = b * TB + i
                    nc.vector.tensor_scalar(xn[:, i, :], k.x[:, t, :], mv[:, t, 0:1], rs[:, t:t + 1],
                                            ALU.subtract, ALU.mult).then_inc(normed.sem, 1)
                dve.wait_ge(*normed.at((b + 1) * TB))
                if b:
                    dve.wait_ge(*h_ready.at(b))
                nc.vector.tensor_tensor(h1, xn, rows[:, 2 * b:2 * b + 1, :].broadcast_to([P, TB, D]), ALU.mult).then_inc(h_scaled.sem, 1)
                dve.wait_ge(*h_scaled.at(b + 1))
                if b >= 2:
                    dve.wait_ge(*v_copied.at(b - 1))
                nc.vector.tensor_tensor(h[:, b % 2], h1, rows[:, 2 * b + 1:2 * b + 2, :].broadcast_to([P, TB, D]), ALU.add).then_inc(h_ready.sem, 1)
                dve.wait_ge(*h_ready.at(b + 1))
                heads = h[:, b % 2].rearrange("p i (h d) -> p (i h) d", d=NARROW)
                if b:
                    dve.wait_ge(*h_mean.at(b))
                nc.vector.tensor_reduce(hs, heads, axis=AX.X, op=ALU.add).then_inc(h_sum.sem, 1)
                dve.wait_ge(*h_sum.at(b + 1))
                if b:
                    dve.wait_ge(*h_centred.at(b))
                nc.vector.tensor_scalar(hm, hs, 1.0 / NARROW, None, ALU.mult).then_inc(h_mean.sem, 1)
                dve.wait_ge(*h_mean.at(b + 1))
                if b:
                    dve.wait_ge(*h_normed.at(b))
                nc.vector.tensor_tensor(hc.rearrange("p (j d) -> p j d", d=NARROW), heads, per_head(hm),
                                        ALU.subtract).then_inc(h_centred.sem, 1)
                dve.wait_ge(*h_squared.at(b + 1))
                if b:
                    dve.wait_ge(*h_root.at(b))
                nc.vector.tensor_reduce(hv, sq.rearrange("p (j d) -> p j d", d=NARROW), axis=AX.X, op=ALU.add).then_inc(h_var.sem, 1)
                dve.wait_ge(*h_root.at(b + 1))
                nc.vector.reciprocal(hr, hsd).then_inc(h_rstd.sem, 1)
                dve.wait_ge(*h_rstd.at(b + 1))
                if b >= 2:
                    dve.wait_ge(*turned.at(b - 1))
                nc.vector.tensor_tensor(hn[:, b % 2].rearrange("p (j d h) -> p j h d", h=4, d=NARROW),
                                        hc.rearrange("p (j h d) -> p j h d", h=4, d=NARROW),
                                        hr.rearrange("p (j h) -> p j h", h=4).unsqueeze(3).broadcast_to([P, TB * 4, 4, NARROW]),
                                        ALU.mult).then_inc(h_normed.sem, 1)
                if b:
                    for u in range(4 * b - 4, 4 * b):
                        split.dve_rest(dve, u, N)
            for u in range(4 * B - 4, 4 * B):
                split.dve_rest(dve, u, N)
    for s, n in ((row_made, 2 * B), (row_in, 2 * B), (stats, TILES), (var, TILES), (root, 1), (rstd, 1), (normed, TILES),
                 (h_scaled, B), (h_ready, B), (v_copied, B), (h_sum, B), (h_mean, B), (h_centred, B), (h_squared, B), (h_var, B),
                 (h_root, B), (h_rstd, B), (h_normed, B), (turned, B)):
        s.passed(n)
    split.passed()
    k.end_stage()


def normalise_context(k, next_weights, w, b):
    nc = k.nc
    loaded, stats, var, root, rstd = k.semaphore("context_loaded"), k.semaphore("stats"), k.semaphore("variances"), k.semaphore("roots"), k.semaphore("rstd")
    rows, turned, out = k.semaphore("normed_rows"), k.semaphore("transposed"), k.semaphore("modulated")
    tok = k.big2[:, 0:2 * DC].rearrange("p (t d) -> p t d", t=2)
    xn = k.big2[:, 512:512 + 2 * DC].rearrange("p (t d) -> p t d", t=2)
    st, mv = k.small[:, 0:12].rearrange("p (t s) -> p t s", s=6), k.small[:, 12:16].rearrange("p (t s) -> p t s", s=2)
    sd, rs = k.small[:, 16:18], k.small[:, 18:20]
    depth = (P, DC - P)
    with nc.Block() as block:
        @block.sync
        def _(sp):
            sp.dma_start(tok, k.ins["ctx"].rearrange("(t p) d -> p t d", p=P)).then_inc(loaded.sem, 16)
            k.load_weights(sp, next_weights)

        @block.vector
        def _(dve):
            dve.wait_ge(*loaded.at(16))
            for t in range(2):
                nc.vector.bn_stats(st[:, t, :], tok[:, t, :]).then_inc(stats.sem, 1)
            dve.wait_ge(*stats.at(2))
            for t in range(2):
                nc.vector.bn_aggr(mv[:, t, :], st[:, t, :]).then_inc(var.sem, 1)
            dve.wait_ge(*root.at(1))
            nc.vector.reciprocal(rs, sd).then_inc(rstd.sem, 1)
            dve.wait_ge(*rstd.at(1))
            for t in range(2):
                nc.vector.tensor_scalar(xn[:, t, :], tok[:, t, :], mv[:, t, 0:1], rs[:, t:t + 1],
                                        ALU.subtract, ALU.mult).then_inc(rows.sem, 1)

        @block.scalar
        def _(act):
            act.wait_ge(*var.at(2))
            nc.scalar.activation(sd, mv[:, :, 1], ACT.Sqrt, bias=k.eps[:, 0:1]).then_inc(root.sem, 1)
            act.wait_ge(*turned.at(1))
            for c, r in enumerate(depth):
                nc.scalar.activation(k.ctx2T[0:r, c, :], k.ps[0:r, c, 0:B * M], ACT.Identity, bias=k.v(b, c)[0:r],
                                     scale=k.v(w, c)[0:r]).then_inc(out.sem, 1)

        @block.tensor
        def _(pe):
            pe.wait_ge(*rows.at(2))
            for c, r in enumerate(depth):
                for t in range(2):
                    last = nc.tensor.transpose(k.ps[0:r, c, t * P:(t + 1) * P], xn[:, t, c * P:c * P + r], k.ident[:, :])
            last.then_inc(turned.sem, 1)
    for s, n in ((loaded, 16), (stats, 2), (var, 2), (root, 1), (rstd, 1), (rows, 2), (turned, 1), (out, 2)):
        s.passed(n)
    k.end_stage()


def vx_pairs(k):
    return k.big2[:, 0:HEADS * WIDE].rearrange("p (n d) -> p n d", d=2 * WIDE)


def project_wide(k, next_weights, wq, wk, wv, context):
    nc = k.nc
    product, turned, joined = k.semaphore("product"), k.semaphore("rotated"), k.semaphore("joined")
    tables = k.semaphore("tables_in")
    stored = [k.semaphore(f"parts_stored_{i}") for i in range(2)]
    v_product, v_read, v_cleared = k.semaphore("v_product"), k.semaphore("v_read"), k.semaphore("v_cleared")
    reads = 2 if context else 1
    table = k.big1[:, 0:2 * N].rearrange("p (a t) -> p a t", a=2)
    terms = k.big1[:, 1024:1024 + 8 * N].rearrange("p (s a t) -> p s a t", s=2, a=4)
    both = k.big1[:, 5120:5120 + 4 * N].rearrange("p (s a t) -> p s a t", s=2, a=2)
    parts = k.big1[:, 7168:7168 + 4 * N].bitcast(BF16).rearrange("p (s a c t) -> p s a c t", s=2, a=2, c=2)
    first_ready, second_ready = k.semaphore("part_1_ready"), k.semaphore("part_2_ready")
    parts_out = [k.semaphore(f"wide_parts_stored_{i}") for i in range(2)]
    units = ([("k", p, 0) for p in range(4)] if context else [("k", p, b) for p in range(4) for b in range(B)]) \
        + [("q", p, b) for p in range(4) for b in range(B)]
    dmas = [8 if context and kind == "k" else 2 for kind, _, _ in units]
    before = [16 * sum(dmas[i] for i in range(u % 2, u, 2)) for u in range(len(units))]
    depth = (P, DC - P) if context else (P, P)
    if context:
        v = vx_pairs(k)
        v_units = [(b, half) for b in range(B) for half in range(2)]
    else:
        v = k.big2[:, :].rearrange("p (b h i d) -> p b h i d", b=B, h=H, i=TB)
        v_units = [(t, half) for t in range(TILES) for half in range(2)]

    def width(kind):
        return B * M if context and kind == "k" else N

    def angles(a, kind):
        return table[:, a, 0:M].unsqueeze(1).broadcast_to([P, B, M]) if width(kind) < N else table[:, a, :]

    def cut(ap, kind):
        return ap[:, 0:B * M].rearrange("p (b t) -> p b t", b=B) if width(kind) < N else ap

    with nc.Block() as block:
        @block.sync
        def _(sp):
            for a in range(2):
                sp.dma_start(table[:, a, :], k.ins["rotary"][a]).then_inc(tables.sem, 16)
            k.load_weights(sp, next_weights)
            for u, (kind, p, b) in enumerate(units):
                sp.wait_ge(*joined.at(2 * u + 2))
                for a in range(2):
                    rows = slice(a * WIDE // 2, (a + 1) * WIDE // 2)
                    if width(kind) == N:
                        h = b * H + 4 * p
                        dst = (k.q_wide if kind == "q" else k.k_wide)[h:h + 4, rows, :]
                        sp.dma_start(dst, both[:, u % 2, a, :]).then_inc(stored[u % 2].sem, 16)
                        if not context:
                            sp.wait_ge(*second_ready.at(2 * u + a + 1))
                            dst = (k.q_wide_parts if kind == "q" else k.k_wide_parts)[h:h + 4, rows, :, :]
                            sp.dma_start(dst.rearrange("h d c t -> h d (c t)"), parts[:, u % 2, a, :, :].rearrange("p c t -> p (c t)")).then_inc(parts_out[u % 2].sem, 16)
                        continue
                    for bb in range(B):
                        h = bb * H + 4 * p
                        sp.dma_start(k.kx_wide[h:h + 4, rows, :], both[:, u % 2, a, bb * M:(bb + 1) * M]).then_inc(stored[u % 2].sem, 16)
            for s in range(2):
                sp.wait_ge(*stored[s].at(16 * sum(dmas[s::2])))
                if not context:
                    sp.wait_ge(*parts_out[s].at(16 * len(units)))

        @block.tensor
        def _(pe):
            pe.wait_ge(*k.weights_due())
            for u, (kind, p, b) in enumerate(units):
                if u >= 3:
                    pe.wait_ge(*turned.at(4 * (u - 2)))
                wt = k.where[wq if kind == "q" else wk]
                for a in range(2):
                    for c in range(C):
                        cols = slice((2 * p + a) * P, (2 * p + a + 1) * P)
                        if context and kind == "k":
                            r = depth[c]
                            lhs, rhs = wt[0:r, c, cols], k.ctx2T[0:r, c, :]
                        else:
                            lhs, rhs = wt[:, c, cols], k.hT[:, c, b * N:(b + 1) * N]
                        last = nc.tensor.matmul(k.ps[:, 2 * (u % 3) + a, 0:width(kind)], lhs, rhs, start=c == 0, stop=c == C - 1)
                last.then_inc(product.sem, 1)
            for u, (t, half) in enumerate(v_units):
                if u >= 2:
                    pe.wait_ge(*v_read.at(reads * (u - 1)))
                for rows in ((slice(0, M), slice(M, P)) if context else (slice(0, P),)):
                    for c in range(C):
                        r = depth[c]
                        lhs = k.ctx2T[0:r, c, t * M:(t + 1) * M] if context else k.hT[:, c, t * P:(t + 1) * P]
                        last = nc.tensor.matmul(k.ps[rows, 6 + u % 2, :], lhs,
                                                k.where[wv][0:r, c, half * 512:(half + 1) * 512], start=c == 0, stop=c == C - 1)
                last.then_inc(v_product.sem, 1)

        @block.vector
        def _(dve):
            def second_parts(u):
                for a in range(2):
                    dve.wait_ge(*first_ready.at(2 * u + a + 1))
                    nc.vector.tensor_tensor(parts[:, u % 2, a, 1, :], both[:, u % 2, a, :], parts[:, u % 2, a, 0, :],
                                            ALU.subtract).then_inc(second_ready.sem, 1)

            dve.wait_ge(*tables.at(32))
            for u, (kind, p, b) in enumerate(units):
                dve.wait_ge(*product.at(u + 1))
                if u >= 2:
                    dve.wait_ge(*joined.at(2 * (u - 1)))
                for i, (a, f) in enumerate(((0, 0), (1, 1), (0, 1), (1, 0))):
                    nc.vector.tensor_tensor(cut(terms[:, u % 2, i, :], kind), cut(k.ps[:, 2 * (u % 3) + a, :], kind),
                                            angles(f, kind), ALU.mult).then_inc(turned.sem, 1)
                if not context and u:
                    second_parts(u - 1)
            if not context:
                second_parts(len(units) - 1)

        @block.gpsimd
        def _(pool):
            if context:
                nc.gpsimd.memset(v, 0.0).then_inc(v_cleared.sem, 1)
            for u, (kind, p, b) in enumerate(units):
                w = slice(0, width(kind))
                pool.wait_ge(*turned.at(4 * u + 4))
                if u >= 2:
                    pool.wait_ge(*stored[u % 2].at(before[u]))
                    if not context:
                        pool.wait_ge(*second_ready.at(2 * (u - 1)))
                nc.gpsimd.tensor_tensor(both[:, u % 2, 0, w], terms[:, u % 2, 0, w], terms[:, u % 2, 1, w],
                                        ALU.subtract).then_inc(joined.sem, 1)
                nc.gpsimd.tensor_tensor(both[:, u % 2, 1, w], terms[:, u % 2, 2, w], terms[:, u % 2, 3, w],
                                        ALU.add).then_inc(joined.sem, 1)

        @block.scalar
        def _(act):
            for u in range(0 if context else len(units)):
                for a in range(2):
                    act.wait_ge(*joined.at(2 * u + a + 1))
                    if u >= 2:
                        act.wait_ge(*parts_out[u % 2].at(32 * (u // 2)))
                    nc.scalar.activation(parts[:, u % 2, a, 0, :], both[:, u % 2, a, :], ACT.Copy).then_inc(first_ready.sem, 1)
            for u, (t, half) in enumerate(v_units):
                if context and u == 0:
                    act.wait_ge(*v_cleared.at(1))
                act.wait_ge(*v_product.at(u + 1))
                if context:
                    for a, rows in enumerate((slice(0, M), slice(M, P))):
                        src = k.ps[rows, 6 + u % 2, :].rearrange("p (n a d) -> p n a d", a=2, d=WIDE)[:, :, a, :]
                        nc.scalar.activation(v[rows, u * 4:u * 4 + 4, a * WIDE:(a + 1) * WIDE], src, ACT.Copy).then_inc(v_read.sem, 1)
                    continue
                src = k.ps[:, 6 + u % 2, :].rearrange("p (h d) -> p h d", d=WIDE)
                nc.scalar.activation(v[:, t // TB, half * 8:half * 8 + 8, t % TB, :], src, ACT.Copy).then_inc(v_read.sem, 1)
    for s in range(2):
        stored[s].passed(16 * sum(dmas[s::2]))
        parts_out[s].passed(0 if context else 16 * len(units))
    for s, n in ((first_ready, 0 if context else 2 * len(units)), (second_ready, 0 if context else 2 * len(units)), (product, len(units)), (turned, 4 * len(units)), (joined, 2 * len(units)), (tables, 32),
                 (v_product, len(v_units)), (v_read, reads * len(v_units)), (v_cleared, 1 if context else 0)):
        s.passed(n)
    k.end_stage()


def attend_wide(k, next_weights):
    nc = k.nc
    groups, turn, slots = HEADS // 4, 2, 4
    heads, turns, pairs = 4 * turn, groups // turn, HEADS // 2
    stack = WIDE + 2
    v = k.big2[:, :].rearrange("p (n i d) -> p n i d", n=HEADS, i=TB)
    q_st = k.big1[0:stack, 0:4096].rearrange("p (u h t) -> p u h t", u=turn, h=4)
    k_st = k.big1[0:stack, 4096:8192].rearrange("p (u h t) -> p u h t", u=turn, h=4)
    probs = k.big1[:, 8192:16384].rearrange("p (s i t) -> p s i t", s=slots, i=TB)
    assert len(next_weights) == 1
    free = [k.w[(k.w_turn + i) % 4][:, :].bitcast(BF16) for i in (1, 2, 3)]
    q_parts = free[0].rearrange("p (u h t) -> p u h t", u=turn, h=4)
    k_parts = [z.rearrange("p (h c t) -> p h c t", h=4, c=2) for z in free[1:]]
    spare = k.hT[:, :, :].rearrange("p c t -> p (c t)")
    v_st = spare[:, 0:1024].rearrange("p (s i d) -> p s i d", s=slots, i=TB)
    o_sb = spare[:, 1024:2048].rearrange("p (s t) -> p s t", s=2)
    sum_sb = spare[0:WIDE, 2048:2560]
    half_sum = spare[:, 2560:3072]
    block_sum = [k.rows[:, 0:2, :].rearrange("p a d -> p (a d)"), k.rows[:, 2:4, :].rearrange("p a d -> p (a d)"),
                 spare[:, 3072:3584], spare[:, 3584:4096]]
    neg_max = k.small[:, 0:8].rearrange("p (s a) -> p s a", s=2)
    max_parts = k.small[:, 8:16].bitcast(BF16).rearrange("p (s a c) -> p s a c", s=2, c=2)
    one = k.small[:, 32:64]

    q_in, k_in = [k.semaphore(f"q_in_{u}") for u in range(turn)], [k.semaphore(f"k_in_{u}") for u in range(turn)]
    parts_in = [k.semaphore(f"wide_parts_in_{u}") for u in range(turn)]
    out_stored, sums_stored = [k.semaphore(f"out_stored_{u}") for u in range(2)], k.semaphore("sums_stored")
    ones, v_in = k.semaphore("ones_made"), k.semaphore("v_staged")
    scores, maxed, max_split = k.semaphore("scores"), k.semaphore("maxed"), k.semaphore("max_split")
    max_turned, max_rows = k.semaphore("max_turned"), k.semaphore("max_rows")
    scores_t, exped, weighted, o_out = k.semaphore("scores_t"), k.semaphore("exped"), k.semaphore("weighted"), k.semaphore("o_out")
    half_added, blocks_added, summed, sums_out = k.semaphore("half_added"), k.semaphore("blocks_added"), k.semaphore("summed"), k.semaphore("sums_out")

    with nc.Block() as block:
        @block.sync
        def _(sp):
            def load(it, u):
                g = turn * it + u
                if due(g - turn + 1):
                    sp.wait_ge(*scores_t.at((g - turn + 1) * 8))
                of_group = bass.ds(g * 4, 4)
                for c in range(2):
                    half = slice(c * WIDE, (c + 1) * WIDE)
                    sp.dma_start(q_parts[half, u, :, :], k.q_wide_parts[of_group, :, c, :].rearrange("h d t -> d h t")).then_inc(parts_in[u].sem, 16)
                    sp.dma_start(k_parts[u][half].rearrange("p h c t -> p h (c t)"),
                                 k.k_wide_parts[of_group].rearrange("h d c t -> d h (c t)")).then_inc(parts_in[u].sem, 16)
                sp.dma_start(q_st[0:WIDE, u, :, :], k.q_wide[of_group].rearrange("h d t -> d h t")).then_inc(q_in[u].sem, 16)
                sp.dma_start(k_st[0:WIDE, u, :, :], k.k_wide[of_group].rearrange("h d t -> d h t")).then_inc(k_in[u].sem, 16)

            def store(m, s):
                sp.wait_ge(*o_out.at(m + 1))
                sp.dma_start(k.o_wide[bass.ds(2 * m, 2), 0:WIDE, :], o_sb[:, s, :]).then_inc(out_stored[s].sem, 16)
                sp.wait_ge(*sums_out.at(m + 1))
                for a in range(2):
                    sp.dma_start(k.o_wide[bass.ds(2 * m + a, 1), WIDE, :], sum_sb[32 * a:32 * a + 1, :]).then_inc(sums_stored.sem, 16)

            def groups_of(it):
                for u in range(turn):
                    load(it, u)
                    for i in range(2):
                        if due(4 * it + 2 * u + i - 3):
                            store(4 * it + 2 * u + i - 4, i)

            load(0, 0)
            load(0, 1)
            k.load_weights(sp, next_weights)
            groups_of(1)
            with sp.Fori(2, turns) as it:
                groups_of(it)
            for m in range(pairs - 4, pairs):
                store(m, m % 2)
            for s in range(2):
                sp.wait_ge(*out_stored[s].at(16 * pairs // 2))
            sp.wait_ge(*sums_stored.at(32 * pairs))

        @block.gpsimd
        def _(pool):
            nc.gpsimd.memset(k_st[WIDE:stack, :, :, :], 1.0).then_inc(ones.sem, 1)
            pool.wait_ge(*ones.at(1))
            nc.gpsimd.memset(one, 1.0).then_inc(ones.sem, 1)
            pool.wait_ge(*ones.at(2))

            def stage(it, j):
                n = heads * it + j
                if due(n - slots + 1):
                    pool.wait_ge(*weighted.at(4 * it + (j - slots) // 2 + 1))
                nc.gpsimd.tensor_copy(v_st[:, j % slots], v[:, bass.ds(n, 1), :, :].rearrange("p n i d -> p (n i) d")).then_inc(v_in.sem, 1)

            def add_blocks(it, j):
                n, s = heads * it + j - 2, (j - 2) % slots
                pool.wait_ge(*exped.at(2 * n + 1))
                if due(n):
                    pool.wait_ge(*blocks_added.at(2 * n))
                nc.gpsimd.tensor_tensor(half_sum, probs[:, s, 0, :], probs[:, s, 1, :], ALU.add).then_inc(half_added.sem, 1)
                pool.wait_ge(*exped.at(2 * n + 2))
                if due(n - slots + 1):
                    pool.wait_ge(*summed.at(4 * it + (j - 2 - slots) // 2 + 1))
                nc.gpsimd.tensor_tensor(block_sum[s], probs[:, s, 2, :], probs[:, s, 3, :], ALU.add).then_inc(blocks_added.sem, 1)
                pool.wait_ge(*half_added.at(n + 1))
                pool.wait_ge(*blocks_added.at(2 * n + 1))
                nc.gpsimd.tensor_tensor(block_sum[s], block_sum[s], half_sum, ALU.add).then_inc(blocks_added.sem, 1)

            def step(it, j):
                stage(it, j)
                if due(heads * it + j - 1):
                    add_blocks(it, j)

            for j in range(heads):
                step(0, j)
            with pool.Fori(1, turns) as it:
                for j in range(heads):
                    step(it, j)
            for j in range(2):
                add_blocks(turns, j)

        @block.tensor
        def _(pe):
            def score(it, j, i):
                u, h = j // 4, j % 4
                if h == 0 and i == 0:
                    pe.wait_ge(*parts_in[u].at(64 * it + 64))
                m = (heads * it + j) * TB + i
                if due(m - 1):
                    pe.wait_ge(*maxed.at(m - 1))
                for c in range(2):
                    last = nc.tensor.matmul(k.ps[:, i % 2, :], q_parts[:, u, h, i * P:(i + 1) * P], k_parts[u][:, h, c, :],
                                            start=c == 0, stop=c == 1)
                last.then_inc(scores.sem, 1)

            def turn_max(it, j):
                n = heads * it + j - 1
                pe.wait_ge(*max_split.at(2 * n + 2))
                if due(n):
                    pe.wait_ge(*max_rows.at(n))
                for a in range(TB):
                    last = nc.tensor.matmul(k.ps[WIDE:stack, 7, a * P:(a + 1) * P], max_parts[:, (j - 1) % 2, a, :],
                                            k.identb[:, :], start=True, stop=True)
                last.then_inc(max_turned.sem, 1)

            def score_t(it, j, e):
                n = heads * it + j - 2
                u, h = (j - 2) // 4 % turn, (j - 2) % 4
                if e == 0:
                    if h == 0:
                        pe.wait_ge(*q_in[u].at(16 * (it + (j - 2) // heads) + 16))
                        pe.wait_ge(*k_in[u].at(16 * (it + (j - 2) // heads) + 16))
                    pe.wait_ge(*max_rows.at(n + 1))
                m = n * 2 + e
                if due(m - 1):
                    pe.wait_ge(*exped.at(m - 1))
                for i in (2 * e, 2 * e + 1):
                    last = nc.tensor.matmul(k.ps[:, 2 + i, :], k_st[:, u, h, i * P:(i + 1) * P], q_st[:, u, h, :],
                                            start=True, stop=True)
                last.then_inc(scores_t.sem, 1)

            def weigh(it, j, i):
                m = 4 * it + (j - 4) // 2
                if i == 0:
                    pe.wait_ge(*exped.at(4 * m + 4))
                    pe.wait_ge(*v_in.at(2 * m + 2))
                    if due(m):
                        pe.wait_ge(*o_out.at(m))
                for a in range(2):
                    s = ((j - 4) // 2 * 2 + a) % slots
                    last = nc.tensor.matmul(k.ps[a * WIDE:(a + 1) * WIDE, 6, :], v_st[:, s, i, :], probs[:, s, i, :],
                                            start=i == 0, stop=i == TB - 1)
                if i == TB - 1:
                    last.then_inc(weighted.sem, 1)

            def sum_up(it, j):
                m = 4 * it + (j - 5) // 2
                pe.wait_ge(*blocks_added.at(4 * m + 4))
                if due(m):
                    pe.wait_ge(*sums_out.at(m))
                for a in range(2):
                    last = nc.tensor.matmul(k.ps[32 * a:32 * a + 32, 7, :], one, block_sum[(j - 5 + a) % slots], start=True, stop=True)
                last.then_inc(summed.sem, 1)

            def step(it, j, scoring=True):
                n = heads * it + j
                turning, scoring_t = (due(n), due(n - 1)) if scoring else (j < 1, j < 2)
                weighing = due(n - 3)
                if scoring:
                    score(it, j, 0)
                if scoring_t:
                    score_t(it, j, 0)
                if scoring:
                    score(it, j, 1)
                if weighing:
                    weigh(it, j, 2 * (j % 2))
                if turning:
                    turn_max(it, j)
                if scoring:
                    score(it, j, 2)
                if scoring_t:
                    score_t(it, j, 1)
                if scoring:
                    score(it, j, 3)
                if weighing:
                    weigh(it, j, 2 * (j % 2) + 1)
                    if j % 2:
                        sum_up(it, j)

            pe.wait_ge(*ones.at(2))
            for j in range(heads):
                step(0, j)
            with pe.Fori(1, turns) as it:
                for j in range(heads):
                    step(it, j)
            for j in range(4):
                step(turns, j, scoring=False)

        @block.vector
        def _(dve):
            def out(it, j):
                m, s = 4 * it + (j - 6) // 2, (j - 6) // 2 % 2
                dve.wait_ge(*weighted.at(m + 1))
                if due(m - 1):
                    dve.wait_ge(*out_stored[s].at(8 * (m - s)))
                nc.vector.tensor_copy(o_sb[:, s, :], k.ps[:, 6, :]).then_inc(o_out.sem, 1)

            def maxima(it, j):
                n, s = heads * it + j, j % 2
                if due(n - 1):
                    dve.wait_ge(*max_split.at(2 * n - 2))
                    dve.wait_ge(*max_turned.at(n - 1))
                for i in range(TB):
                    dve.wait_ge(*scores.at(n * TB + i + 1))
                    nc.vector.tensor_reduce(neg_max[:, s, i:i + 1], k.ps[:, i % 2, :], axis=AX.X, op=ALU.max,
                                            negate=True).then_inc(maxed.sem, 1)
                dve.wait_ge(*maxed.at((n + 1) * TB))
                nc.vector.tensor_copy(max_parts[:, s, :, 0], neg_max[:, s, :]).then_inc(max_split.sem, 1)
                dve.wait_ge(*max_split.at(2 * n + 1))
                nc.vector.tensor_tensor(max_parts[:, s, :, 1], neg_max[:, s, :], max_parts[:, s, :, 0],
                                        ALU.subtract).then_inc(max_split.sem, 1)

            def step(it, j):
                if j % 2 == 0 and due(heads * it + j - 5):
                    out(it, j)
                maxima(it, j)

            for it in range(2):
                for j in range(heads):
                    step(it, j)
            with dve.Fori(2, turns) as it:
                for j in range(heads):
                    step(it, j)
            for j in (0, 2, 4):
                out(turns, j)

        @block.scalar
        def _(act):
            def max_row(it, j):
                n = heads * it + j - 1
                u, h = (j - 1) // 4 % turn, (j - 1) % 4
                act.wait_ge(*max_turned.at(n + 1))
                nc.scalar.activation(q_st[WIDE:stack, u, h, :], k.ps[WIDE:stack, 7, :], ACT.Copy).then_inc(max_rows.sem, 1)

            def exps(it, j, e):
                n, s = heads * it + j - 2, (j - 2) % slots
                if e == 0 and due(n - slots + 1):
                    act.wait_ge(*summed.at(4 * it + (j - 2 - slots) // 2 + 1))
                act.wait_ge(*scores_t.at(n * 2 + e + 1))
                nc.scalar.activation(probs[:, s, 2 * e:2 * e + 2, :], k.ps[:, 2 + 2 * e:4 + 2 * e, :], ACT.Exp,
                                     scale=WIDE ** -0.5).then_inc(exped.sem, 1)

            def sums(it, j):
                m = 4 * it + (j - 6) // 2
                act.wait_ge(*summed.at(m + 1))
                if due(m):
                    act.wait_ge(*sums_stored.at(32 * m))
                nc.scalar.activation(sum_sb, k.ps[0:WIDE, 7, :], ACT.Copy).then_inc(sums_out.sem, 1)

            def step(it, j):
                n = heads * it + j
                if j % 2 == 0 and due(n - 5):
                    sums(it, j)
                if due(n - 1):
                    exps(it, j, 0)
                if due(n):
                    max_row(it, j)
                if due(n - 1):
                    exps(it, j, 1)

            for j in range(heads):
                step(0, j)
            with act.Fori(1, turns) as it:
                for j in range(heads):
                    step(it, j)
            for j in range(2):
                if j == 0:
                    sums(turns, j)
                    max_row(turns, j)
                exps(turns, j, 0)
                exps(turns, j, 1)
            sums(turns, 2)
            sums(turns, 4)
    for s in q_in + k_in:
        s.passed(16 * turns)
    for s in parts_in:
        s.passed(64 * turns)
    for s in out_stored:
        s.passed(8 * pairs)
    for s, n in ((ones, 2), (v_in, HEADS), (scores, HEADS * TB), (maxed, HEADS * TB), (max_split, 2 * HEADS), (max_turned, HEADS),
                 (max_rows, HEADS), (scores_t, HEADS * 2), (exped, HEADS * 2), (weighted, pairs), (o_out, pairs),
                 (half_added, HEADS), (blocks_added, 2 * HEADS), (summed, pairs), (sums_out, pairs), (sums_stored, 32 * pairs)):
        s.passed(n)
    k.end_stage()


def attend_wide_context(k, next_weights):
    nc = k.nc
    pairs, groups, turn = HEADS // 2, HEADS // 4, 4
    per, turns, slots = 2 * turn, groups // turn, 8
    v = vx_pairs(k)
    q_st = k.big1[:, 0:turn * 2 * N].rearrange("p (u i t) -> p u i t", u=turn, i=2)
    k_st = k.big1[:, 4096:4096 + turn * 2 * P].rearrange("p (u i t) -> p u i t", u=turn, i=2)
    probs = k.big1[:, 5120:5120 + slots * N].rearrange("p (s t) -> p s t", s=slots)
    spare = k.hT[:, :, :].rearrange("p c t -> p (c t)")
    v_st = spare[:, 0:4 * P].rearrange("p (s d) -> p s d", s=4)
    o_sb = spare[:, 1024:2048].rearrange("p (s t) -> p s t", s=2)
    sum_sb = spare[:, 2048:2560]
    max_row = spare[0:4, 2560:3072].bitcast(BF16).rearrange("p (s t) -> p s t", s=2)
    of_head = spare[0:4, 3072:3136].bitcast(BF16)
    by_head = spare[:, 3136:3168]
    neg_max = k.small[:, 0:16].rearrange("p (s a h) -> p s a h", s=2, a=TB)
    max_parts = k.small[:, 16:32].bitcast(BF16).rearrange("p (s a c h) -> p s a c h", s=2, a=TB, c=2)

    q_in, k_in = [k.semaphore(f"q_in_{u}") for u in range(turn)], [k.semaphore(f"k_in_{u}") for u in range(turn)]
    out_stored, sums_stored = [k.semaphore(f"out_stored_{u}") for u in range(2)], k.semaphore("sums_stored")
    cleared, ones, v_in = k.semaphore("cleared"), k.semaphore("ones_made"), k.semaphore("v_staged")
    scores, maxed, max_split = k.semaphore("scores"), k.semaphore("maxed"), k.semaphore("max_split")
    max_turned, max_rows = k.semaphore("max_turned"), k.semaphore("max_rows")
    scores_t, exped, weighted, o_out = k.semaphore("scores_t"), k.semaphore("exped"), k.semaphore("weighted"), k.semaphore("o_out")
    summed, sums_out = k.semaphore("summed"), k.semaphore("sums_out")

    def by_parity(dram):
        return dram.rearrange("(n a) d t -> a d n t", a=2)

    with nc.Block() as block:
        @block.sync
        def _(sp):
            def load(it, u):
                g = turn * it + u
                if due(g - turn + 1):
                    sp.wait_ge(*scores_t.at((g - turn + 1) * 2))
                for a in range(2):
                    half = slice(a * WIDE, (a + 1) * WIDE)
                    sp.dma_start(q_st[half, u, :, :], by_parity(k.q_wide)[a, :, bass.ds(g * 2, 2), :]).then_inc(q_in[u].sem, 16)
                    sp.dma_start(k_st[half, u, :, a * M:(a + 1) * M],
                                 by_parity(k.kx_wide)[a, :, bass.ds(g * 2, 2), :]).then_inc(k_in[u].sem, 16)

            def store(n, s):
                sp.wait_ge(*o_out.at(n + 1))
                sp.dma_start(k.o_wide[bass.ds(2 * n, 2), 0:WIDE, :], o_sb[:, s, :]).then_inc(out_stored[s].sem, 16)

            def store_sums(r):
                sp.wait_ge(*sums_out.at(r + 1))
                for i in range(4):
                    sp.dma_start(k.o_wide[bass.ds(8 * r + 2 * i, 2), WIDE, :], sum_sb[32 * i:32 * i + 2, :]).then_inc(sums_stored.sem, 16)

            def groups_of(it):
                for u in range(turn):
                    load(it, u)
                    for i in range(2):
                        store(per * (it - 1) + 2 * u + i, i)
                    if u % 2:
                        store_sums(2 * (it - 1) + u // 2)

            sp.wait_ge(*cleared.at(2))
            for u in range(turn):
                load(0, u)
            k.load_weights(sp, next_weights)
            groups_of(1)
            with sp.Fori(2, turns) as it:
                groups_of(it)
            for n in range(per):
                store(pairs - per + n, n % 2)
                if n % 4 == 3:
                    store_sums(2 * (turns - 1) + n // 4)
            for s in range(2):
                sp.wait_ge(*out_stored[s].at(16 * pairs // 2))
            sp.wait_ge(*sums_stored.at(16 * pairs))

        @block.gpsimd
        def _(pool):
            nc.gpsimd.memset(k_st, 0.0).then_inc(cleared.sem, 1)
            nc.gpsimd.memset(by_head, 0.0).then_inc(cleared.sem, 1)
            pool.wait_ge(*cleared.at(2))
            for a in range(2):
                nc.gpsimd.memset(by_head[a * M:(a + 1) * M, a:a + 1], 1.0).then_inc(ones.sem, 1)
            pool.wait_ge(*ones.at(3))

            def stage(it, j):
                n = per * it + j
                if due(n - 3):
                    pool.wait_ge(*weighted.at(n - 3))
                nc.gpsimd.tensor_copy(v_st[:, j % 4, :], v[:, bass.ds(n, 1), :].rearrange("p n d -> p (n d)")).then_inc(v_in.sem, 1)

            for j in range(per):
                stage(0, j)
            with pool.Fori(1, turns) as it:
                for j in range(per):
                    stage(it, j)

        @block.tensor
        def _(pe):
            def score(it, j):
                n, u, i = per * it + j, j // 2, j % 2
                if i == 0:
                    pe.wait_ge(*q_in[u].at(32 * it + 32))
                    pe.wait_ge(*k_in[u].at(32 * it + 32))
                if due(n - 1):
                    pe.wait_ge(*maxed.at(n - 1))
                for a in range(TB):
                    last = nc.tensor.matmul(k.ps[:, j % 2, a * P:(a + 1) * P], q_st[:, u, i, a * P:(a + 1) * P], k_st[:, u, i, :],
                                            start=True, stop=True)
                last.then_inc(scores.sem, 1)

            def turn_max(it, j):
                n = per * it + j - 1
                pe.wait_ge(*max_split.at(2 * n + 2))
                if due(n):
                    pe.wait_ge(*max_rows.at(n))
                for a in range(TB):
                    parts = max_parts[:, (j - 1) % 2, a, :, :].rearrange("p c h -> p (c h)")
                    last = nc.tensor.matmul(k.ps[0:4, 7, a * P:(a + 1) * P], parts, k.identb[:, :], start=True, stop=True)
                last.then_inc(max_turned.sem, 1)

            def score_t(it, j):
                n = per * it + j - 2
                u, i = (j - 2) // 2 % turn, (j - 2) % 2
                pe.wait_ge(*max_rows.at(n + 1))
                if due(n - 1):
                    pe.wait_ge(*exped.at(n - 1))
                nc.tensor.matmul(k.ps[:, 2 + j % 2, :], k_st[:, u, i, :], q_st[:, u, i, :], start=True, stop=False)
                nc.tensor.matmul(k.ps[:, 2 + j % 2, :], of_head, max_row[:, j % 2, :], start=False, stop=True).then_inc(scores_t.sem, 1)

            def weigh(it, j):
                n = per * it + j - 3
                pe.wait_ge(*exped.at(n + 1))
                pe.wait_ge(*v_in.at(n + 1))
                if due(n - 1):
                    pe.wait_ge(*o_out.at(n - 1))
                nc.tensor.matmul(k.ps[:, 4 + (j - 3) % 2, :], v_st[:, (j - 3) % 4, :], probs[:, (j - 3) % slots, :],
                                 start=True, stop=True).then_inc(weighted.sem, 1)

            def sum_up(it, j):
                r = 2 * it + (j - 6) // 4
                if due(r):
                    pe.wait_ge(*sums_out.at(r))
                for i in range(4):
                    last = nc.tensor.matmul(k.ps[32 * i:32 * i + 32, 6, :], by_head, probs[:, (j - 6 + i) % slots, :], start=True, stop=True)
                last.then_inc(summed.sem, 1)

            def step(it, j, scoring=True):
                n = per * it + j
                if scoring:
                    score(it, j)
                if due(n) and (scoring or j < 1):
                    turn_max(it, j)
                if due(n - 1) and (scoring or j < 2):
                    score_t(it, j)
                if due(n - 2):
                    weigh(it, j)
                if j % 4 == 2 and due(n - 5):
                    sum_up(it, j)

            pe.wait_ge(*ones.at(3))
            for j in range(per):
                step(0, j)
            with pe.Fori(1, turns) as it:
                for j in range(per):
                    step(it, j)
            for j in range(3):
                step(turns, j, scoring=False)

        @block.vector
        def _(dve):
            nc.vector.tensor_tensor(of_head.rearrange("p (h m) -> p h m", h=2), k.identb[0:4, 0:2].unsqueeze(2).broadcast_to([4, 2, M]),
                                    k.identb[0:4, 2:4].unsqueeze(2).broadcast_to([4, 2, M]), ALU.add).then_inc(ones.sem, 1)

            def out(it, j):
                n, s = per * it + j - 4, j % 2
                dve.wait_ge(*weighted.at(n + 1))
                if due(n - 1):
                    dve.wait_ge(*out_stored[s].at(8 * (n - s)))
                nc.vector.tensor_copy(o_sb[:, s, :], k.ps[:, 4 + s, :]).then_inc(o_out.sem, 1)

            def maxima(it, j):
                n, s = per * it + j, j % 2
                if due(n - 1):
                    dve.wait_ge(*max_split.at(2 * n - 2))
                    dve.wait_ge(*max_turned.at(n - 1))
                dve.wait_ge(*scores.at(n + 1))
                nc.vector.tensor_reduce(neg_max[:, s, :, :].rearrange("p a h -> p (a h)"),
                                        k.ps[:, s, :].rearrange("p (x m) -> p x m", m=M), axis=AX.X, op=ALU.max,
                                        negate=True).then_inc(maxed.sem, 1)
                dve.wait_ge(*maxed.at(n + 1))
                nc.vector.tensor_copy(max_parts[:, s, :, 0, :], neg_max[:, s, :, :]).then_inc(max_split.sem, 1)
                dve.wait_ge(*max_split.at(2 * n + 1))
                nc.vector.tensor_tensor(max_parts[:, s, :, 1, :], neg_max[:, s, :, :], max_parts[:, s, :, 0, :],
                                        ALU.subtract).then_inc(max_split.sem, 1)

            def step(it, j):
                if due(per * it + j - 3):
                    out(it, j)
                maxima(it, j)

            for j in range(per):
                step(0, j)
            with dve.Fori(1, turns) as it:
                for j in range(per):
                    step(it, j)
            for j in range(4):
                out(turns, j)

        @block.scalar
        def _(act):
            def copy_rows(it, j):
                n, s = per * it + j - 1, (j - 1) % 2
                act.wait_ge(*max_turned.at(n + 1))
                if due(n - 1):
                    act.wait_ge(*scores_t.at(n - 1))
                nc.scalar.activation(max_row[:, s, :], k.ps[0:4, 7, :], ACT.Copy).then_inc(max_rows.sem, 1)

            def exps(it, j):
                n = per * it + j - 2
                if due(n - slots + 1):
                    act.wait_ge(*weighted.at(n - slots + 1))
                    act.wait_ge(*summed.at(2 * it + (j - 2 - slots) // 4 + 1))
                act.wait_ge(*scores_t.at(n + 1))
                nc.scalar.activation(probs[:, (j - 2) % slots, :], k.ps[:, 2 + j % 2, :], ACT.Exp, scale=WIDE ** -0.5).then_inc(exped.sem, 1)

            def sums(it, j):
                r = 2 * it + (j - 7) // 4
                act.wait_ge(*summed.at(r + 1))
                if due(r):
                    act.wait_ge(*sums_stored.at(64 * r))
                nc.scalar.activation(sum_sb, k.ps[:, 6, :], ACT.Copy).then_inc(sums_out.sem, 1)

            def step(it, j):
                n = per * it + j
                if due(n):
                    copy_rows(it, j)
                if due(n - 1):
                    exps(it, j)
                if j % 4 == 3 and due(n - 6):
                    sums(it, j)

            for it in range(2):
                for j in range(per):
                    step(it, j)
            with act.Fori(2, turns) as it:
                for j in range(per):
                    step(it, j)
            copy_rows(turns, 0)
            exps(turns, 0)
            exps(turns, 1)
            sums(turns, 3)
    for s in q_in + k_in:
        s.passed(32 * turns)
    for s in out_stored:
        s.passed(8 * pairs)
    for s, n in ((sums_stored, 16 * pairs), (cleared, 2), (ones, 3), (v_in, pairs), (scores, pairs), (maxed, pairs), (max_split, 2 * pairs),
                 (max_turned, pairs), (max_rows, pairs), (scores_t, pairs), (exped, pairs), (weighted, pairs), (o_out, pairs),
                 (summed, pairs // 4), (sums_out, pairs // 4)):
        s.passed(n)
    k.end_stage()


def stages():
    out = []

    def add(f, weights, *args):
        out.append((f, weights, args))

    def add_norm(*spec, alone=False):
        if out and not alone and out[-1][0] in (project_out, feed_forward):
            f, weights, args = out[-1]
            out[-1] = (f, weights, args[:-1] + (spec,))
        else:
            add(normalise, [], spec)

    def chunk(block, n):
        return MOD_AT[block] + 2 * n

    if "0" in BLOCKS:
        def norm0(i):
            add_norm(chunk("L0", 2 * i - 2), chunk("L0", 2 * i - 1), f"L0_ln{i}_w", f"L0_ln{i}_b", 0)

        norm0(1)
        add(project_qkv, ["L0_Wqkv"], "L0_Wqkv", "L0_bqkv")
        add(attend, [])
        add(project_out, ["L0_Wos"], "L0_Wos", "L0_bos", None, False, None)
        norm0(2)
        add(project_cross, ["L0_Wq", "L0_Wk", "L0_Wv"], None, "L0_Wq", "L0_Wk", "L0_Wv", ("L0_bq", 0), ("L0_bk", 0), ("L0_bv", 0))
        add(attend_context, [])
        add(project_out, ["L0_Woc"], "L0_Woc", "L0_boc", None, False, None)
        norm0(3)
        add(feed_forward, ["L0_W1", "L0_W2"], "L0_W1", None, "L0_W2", "L0_b1", "L0_b2", ACT.Gelu, None, None)
    if "1" in BLOCKS:
        def norm1(i, alone=False):
            add_norm(chunk("L1", 2 * i - 1), chunk("L1", 2 * i - 2), f"L1_ln{i}_w", f"L1_ln{i}_b", 0, alone=alone)

        norm1(1, alone=True)
        add(project_wide, ["L1_sa_wq", "L1_sa_wk", "L1_sa_wv"], "L1_sa_wq", "L1_sa_wk", "L1_sa_wv", False)
        add(attend_wide, [])
        add(project_out, ["L1_sa_wo"], "L1_sa_wo", "L1_sa_bo", None, True, None)
        norm1(1)
        add(normalise_context, [], "L1_ca_lnc_w", "L1_ca_lnc_b")
        add(project_wide, ["L1_ca_wq", "L1_ca_wk", "L1_ca_wv"], "L1_ca_wq", "L1_ca_wk", "L1_ca_wv", True)
        add(attend_wide_context, [])
        add(project_out, ["L1_ca_wo"], "L1_ca_wo", "L1_ca_bo", None, True, None)
        norm1(2)
        add(feed_forward, ["L1_ff_w1", "L1_ff_w2"], "L1_ff_w1", None, "L1_ff_w2", "L1_ff_b1", "L1_ff_b2", ACT.Gelu, None, None)
    if "2" in BLOCKS:
        def norm2(i):
            add_norm(chunk("L2", 2 * i - 2), chunk("L2", 2 * i - 1), None, None, 1)

        norm2(1)
        add(project_qkv, ["L2_W_qkv"], "L2_W_qkv", "L2_b_qkv")
        add(attend, [])
        add(project_out, ["L2_W_proj"], "L2_W_proj", "L2_b_proj", None, False, None)
        norm2(2)
        add(project_cross, ["L2_W_ctx", "L2_W_q", "L2_W_k", "L2_W_v"], ("L2_W_ctx", "L2_b_ctx"), "L2_W_q", "L2_W_k", "L2_W_v",
            None, None, None)
        add(attend_context, [])
        add(project_out, ["L2_W_out"], "L2_W_out", "L2_b_out", None, False, None)
        norm2(3)
        add(feed_forward, ["L2_W_fc1", "L2_W_fc2"], "L2_W_fc1", None, "L2_W_fc2", "L2_b_fc1", "L2_b_fc2", ACT.Gelu_apprx_tanh, None, None)
    if "3" in BLOCKS:
        add(normalise_heads, [], chunk("L3", 0), chunk("L3", 1), 1)
        add(attend, [])
        add(project_out, [], None, None, chunk("L3", 2), False, None)
        add_norm(chunk("L3", 3), chunk("L3", 4), None, None, 1)
        add(project_cross, ["L3_cond_w", "L3_ca_q", "L3_ca_k", "L3_ca_v"], ("L3_cond_w", "L3_cond_b"), "L3_ca_q", "L3_ca_k", "L3_ca_v",
            ("L3_ca_in_b", 0), ("L3_ca_in_b", 2), ("L3_ca_in_b", 4))
        add(attend_context, [])
        add(project_out, ["L3_ca_out_w"], "L3_ca_out_w", "L3_ca_out_b", chunk("L3", 5), False, None)
        add_norm(chunk("L3", 6), chunk("L3", 7), None, None, 1)
        add(feed_forward, ["L3_w1", "L3_w3", "L3_w2"], "L3_w1", "L3_w3", "L3_w2", None, None, ACT.Silu, chunk("L3", 8), None)
    return out


def program(nc, ins, out):
    with ExitStack() as ctx:
        k = Chip(nc, ctx, ins, out)
        todo = stages()
        setup(k, todo[0][1])
        for i, (f, _, args) in enumerate(todo):
            f(k, todo[i + 1][1] if i + 1 < len(todo) else None, *args)


BLOCKS = "0123"


def kernel(**inputs):
    import concourse.bacc as _bacc
    from concourse.bass_utils import run_bass_kernel_spmd as _run

    a = {n.replace("_xcond", ""): np.asarray(v) for n, v in inputs.items()}
    a["L3_adaln_w"] = a["L3_adaln_w"].T
    order = np.arange(MID).reshape(4, 4, WIDE // 2, 2).transpose(0, 3, 1, 2).reshape(MID)
    mixed = np.arange(D).reshape(4, 4, NARROW).transpose(0, 2, 1).reshape(D)
    for n in ("L0_Wqkv", "L0_bqkv", "L2_W_qkv", "L2_b_qkv"):
        a[n] = a[n][..., np.concatenate([mixed, D + mixed, 2 * D + np.arange(D)])]
    for n in ("L0_Wq", "L0_bq", "L0_Wk", "L0_bk", "L2_W_q", "L2_W_k"):
        a[n] = a[n][..., mixed]
    wk, wv = a["L1_sa_wkv"][:, :MID], a["L1_sa_wkv"][:, MID:]
    a["L1_sa_wq"], a["L1_sa_wk"], a["L1_sa_wv"] = a["L1_sa_wq"][:, order], wk[:, order], wv
    wk, wv = a["L1_ca_wkv"][:, :MID], a["L1_ca_wkv"][:, MID:]
    a["L1_ca_wq"], a["L1_ca_wk"], a["L1_ca_wv"] = a["L1_ca_wq"][:, order], wk[:, order], wv
    a["L3_ca_q"], a["L3_ca_k"], a["L3_ca_v"] = (a["L3_ca_in_w"][i * D:(i + 1) * D].T for i in range(3))
    a["L3_ca_q"], a["L3_ca_k"] = a["L3_ca_q"][:, mixed], a["L3_ca_k"][:, mixed]
    a["L3_ca_in_b"] = a["L3_ca_in_b"][np.concatenate([mixed, D + mixed, 2 * D + np.arange(D)])]
    for n in ("L3_cond_w", "L3_ca_out_w", "L3_w1", "L3_w3", "L3_w2"):
        a[n] = a[n].T
    for n in ("L1_ca_lnc_w", "L1_ca_lnc_b"):
        a[n] = np.concatenate([a[n], np.zeros(2 * P - DC, np.float32)])
    for n in ("L3_qn_w", "L3_qn_b", "L3_kn_w", "L3_kn_b"):
        a[n] = np.tile(np.repeat(a[n], 4), 2)
    arrays = {n: a[n] for n in WEIGHTS}
    arrays["vectors"] = np.concatenate([a[n].reshape(c, P) for n, c in VECTORS]).T
    arrays["mods"] = np.concatenate([a[n] for n, _ in MODS], axis=1)
    arrays["x"] = a["x"].reshape(T, D)
    arrays["ctx"] = a["ctx_768"].reshape(B * M, DC)
    arrays["condT"] = a["cond_1024"].T
    inv = (1.0 / 10000.0 ** (np.arange(0, WIDE, 2, dtype=np.float32) / np.float32(WIDE))).astype(np.float32)
    angle = np.arange(N, dtype=np.float32)[None, :] * inv[:, None]
    arrays["rotary"] = np.concatenate([np.stack([np.cos(angle), np.sin(angle)])] * 4, axis=1).astype(np.float32)

    nc = _bacc.Bacc("TRN2", target_bir_lowering=False, num_devices=1)
    ins = {}
    for n in arrays:
        arrays[n] = np.ascontiguousarray(arrays[n])
        ins[n] = nc.dram_tensor(f"in_{n}", arrays[n].shape, mybir.dt.from_np(arrays[n].dtype), kind="ExternalInput").ap()
    out = nc.dram_tensor("out_0", (B, N, D), F32, kind="ExternalOutput").ap()
    program(nc, ins, out)
    r = _run(nc, [{f"in_{n}": v for n, v in arrays.items()}], core_ids=[0])
    return r.results[0]["out_0"]
```
